# Optimizing a Trainium2 kernel written in Bass

```python
import numpy as np
import jax
import jax.numpy as jnp

def _softmax(x, axis=-1):
    return jax.nn.softmax(x, axis=axis)

def _gelu(x):
    return jax.nn.gelu(x, approximate=True)

def _silu(x):
    return jax.nn.silu(x)

def _sigmoid(x):
    return jax.nn.sigmoid(x)

def _layernorm(x, axis=-1, eps=1e-05):
    m = jnp.mean(x, axis=axis, keepdims=True)
    v = jnp.var(x, axis=axis, keepdims=True)
    return (x - m) / jnp.sqrt(v + eps)

def _scatter_add(tgt, idx, src, axis=0):
    return tgt.at[idx].add(src)

def _segment_sum(src, seg, n):
    return jax.ops.segment_sum(src, seg, n)
kernel_name = 'mk_decoder_preln_d1_seqx_r4_a88e6a'

def setup_inputs(seed: int=0):
    np.random.seed(seed)
    _w = jnp.asarray

    def _rec_inputs():
        import jax
        import jax.numpy as jnp
        _rk = jax.random.key(seed)
        x = -0.0002928 + 1 * jax.random.normal(jax.random.fold_in(_rk, 1), (4, 512, 256), jnp.float32)
        _lenS = 512 - jax.random.randint(jax.random.fold_in(_rk, 7), (4,), 0, max(1, 512 // 4) + 1, jnp.int32)
        _lenS2 = 1024 - jax.random.randint(jax.random.fold_in(_rk, 8), (4,), 0, max(1, 1024 // 4) + 1, jnp.int32)
        _ctx_768P = jax.random.normal(jax.random.fold_in(_rk, 11), (4, 16, 192), jnp.float32)
        _ctx_768c = jax.random.dirichlet(jax.random.fold_in(_rk, 511), 0.3 * jnp.ones((16,), jnp.float32), (4, 1024))
        _ctx_768t = jnp.einsum('bsk,bkd->bsd', _ctx_768c, _ctx_768P)
        _ctx_768t = _ctx_768t * jax.lax.rsqrt(jnp.mean(jnp.square(_ctx_768t)) + 1e-12) * 0.953939
        ctx_768 = 2.09791e-05 + 1.00001 * (_ctx_768t + 0.3 * jax.random.normal(jax.random.fold_in(_rk, 611), (4, 1024, 192), jnp.float32))
        return (x, ctx_768)
    x, ctx_768 = _rec_inputs()

    def _L0_attn_setup():
        import jax, jax.numpy as jnp
        import numpy as np
        EMBED_DIM = 256
        NUM_HEADS = 16
        HEAD_DIM = EMBED_DIM // NUM_HEADS
        B, N = (2, 512)
        BIAS_S = 32

        def _interp_matrix(n, s):
            pos = jnp.arange(n, dtype=jnp.float32) * ((s - 1) / (n - 1))
            i0 = jnp.floor(pos).astype(jnp.int32)
            i1 = jnp.minimum(i0 + 1, s - 1)
            frac = pos - i0.astype(jnp.float32)
            rows = jnp.arange(n)
            M = jnp.zeros((n, s), dtype=jnp.float32)
            M = M.at[rows, i0].add(1.0 - frac).at[rows, i1].add(frac)
            return M
        key = jax.random.key(seed)
        ks = jax.random.split(key, 12)
        std = 0.02
        d = {'x': jax.random.normal(ks[0], (B, N, EMBED_DIM), dtype=jnp.float32), 'Wq': jax.random.normal(ks[1], (EMBED_DIM, EMBED_DIM), dtype=jnp.float32) * std, 'bq': jnp.zeros((EMBED_DIM,), dtype=jnp.float32), 'Wk': jax.random.normal(ks[2], (EMBED_DIM, EMBED_DIM), dtype=jnp.float32) * std, 'bk': jnp.zeros((EMBED_DIM,), dtype=jnp.float32), 'Wv': jax.random.normal(ks[3], (EMBED_DIM, EMBED_DIM), dtype=jnp.float32) * std, 'bv': jnp.zeros((EMBED_DIM,), dtype=jnp.float32), 'Wo': jax.random.normal(ks[4], (EMBED_DIM, EMBED_DIM), dtype=jnp.float32) * std, 'bo': jnp.zeros((EMBED_DIM,), dtype=jnp.float32), 'gamma': jnp.ones((EMBED_DIM,), dtype=jnp.float32), 'beta': jnp.zeros((EMBED_DIM,), dtype=jnp.float32), 'rel_bias': jax.random.normal(ks[5], (NUM_HEADS, BIAS_S, BIAS_S), dtype=jnp.float32) * std}
        return d
    _L0_attn_all = _L0_attn_setup()
    _L0_attn_in = {k: v for k, v in _L0_attn_all.items() if k in ('Wq', 'bq', 'Wk', 'bk', 'Wv', 'bv', 'Wo', 'bo', 'gamma', 'beta', 'rel_bias')}
    del _L0_attn_all

    def _L0_xattn_setup():
        import jax, jax.numpy as jnp
        import numpy as np
        HEADS = 8
        DIM_HEAD = 128
        ATTN_MATRIX_SCALE = 1.5
        SCALE = DIM_HEAD ** (-0.5)

        def _split_heads(t):
            b, n, _ = t.shape
            t = t.reshape(b, n, HEADS, DIM_HEAD)
            return t.transpose(2, 0, 1, 3).reshape(HEADS, b * n, DIM_HEAD)
        key = jax.random.key(seed)
        ks = jax.random.split(key, 7)
        b, n, m = (2, 512, 512)
        qd, cd, inner = (256, 192, HEADS * DIM_HEAD)
        x = jax.random.normal(ks[0], (b, n, qd), dtype=jnp.float32)
        context = jax.random.normal(ks[1], (b, m, cd), dtype=jnp.float32)
        Wq = jax.random.normal(ks[2], (qd, inner), dtype=jnp.float32) * qd ** (-0.5)
        Wk = jax.random.normal(ks[3], (cd, inner), dtype=jnp.float32) * cd ** (-0.5)
        Wv = jax.random.normal(ks[4], (cd, inner), dtype=jnp.float32) * cd ** (-0.5)
        Wout = jax.random.normal(ks[5], (inner, qd), dtype=jnp.float32) * inner ** (-0.5)
        bout = jnp.zeros((qd,), dtype=jnp.float32)
        return {'x': x, 'context': context, 'Wq': Wq, 'Wk': Wk, 'Wv': Wv, 'Wout': Wout, 'bout': bout}
    _L0_xattn_all = _L0_xattn_setup()
    _L0_xattn_in = {k: v for k, v in _L0_xattn_all.items() if k in ('Wq', 'Wk', 'Wv', 'Wout', 'bout')}
    del _L0_xattn_all

    def _L0_ffn_setup():
        import jax, jax.numpy as jnp
        import numpy as np
        DIM = 256

        def _reference_tuple_inner(x, W_r, W_k, W_v, mu_r, mu_k):
            B, T, C = x.shape
            x_prev = jnp.concatenate([jnp.zeros((B, 1, C), x.dtype), x[:, :-1, :]], axis=1)
            xr = mu_r * x + (1.0 - mu_r) * x_prev
            xk = mu_k * x + (1.0 - mu_k) * x_prev
            r = jax.nn.sigmoid(jnp.einsum('btc,dc->btd', xr, W_r))
            k = jnp.einsum('btc,dc->btd', xk, W_k)
            k_act = jnp.square(jax.nn.relu(k))
            out = r * jnp.einsum('btc,dc->btd', k_act, W_v)
            new_state = x[:, -1, :]
            return (out, new_state)
        key = jax.random.key(seed)
        ks = jax.random.split(key, 6)
        B, T, C = (8, 512, DIM)
        x = jax.random.normal(ks[0], (B, T, C), dtype=jnp.float32)
        s = 1.0 / np.sqrt(C)
        W_r = jax.random.uniform(ks[1], (C, C), jnp.float32, -s, s)
        W_k = jax.random.uniform(ks[2], (C, C), jnp.float32, -s, s)
        W_v = jax.random.uniform(ks[3], (C, C), jnp.float32, -s, s)
        mu_r = jax.random.uniform(ks[4], (C,), jnp.float32)
        mu_k = jax.random.uniform(ks[5], (C,), jnp.float32)
        return {'x': x, 'W_r': W_r, 'W_k': W_k, 'W_v': W_v, 'mu_r': mu_r, 'mu_k': mu_k}
    _L0_ffn_all = _L0_ffn_setup()
    _L0_ffn_in = {k: v for k, v in _L0_ffn_all.items() if k in ('W_r', 'W_k', 'W_v', 'mu_r', 'mu_k')}
    del _L0_ffn_all
    return {'x': x, 'ctx_768': ctx_768, 'L0_attn_Wq': _L0_attn_in['Wq'], 'L0_attn_bq': _L0_attn_in['bq'], 'L0_attn_Wk': _L0_attn_in['Wk'], 'L0_attn_bk': _L0_attn_in['bk'], 'L0_attn_Wv': _L0_attn_in['Wv'], 'L0_attn_bv': _L0_attn_in['bv'], 'L0_attn_Wo': _L0_attn_in['Wo'], 'L0_attn_bo': _L0_attn_in['bo'], 'L0_attn_gamma': _L0_attn_in['gamma'], 'L0_attn_beta': _L0_attn_in['beta'], 'L0_attn_rel_bias': _L0_attn_in['rel_bias'], 'L0_xattn_Wq': _L0_xattn_in['Wq'], 'L0_xattn_Wk': _L0_xattn_in['Wk'], 'L0_xattn_Wv': _L0_xattn_in['Wv'], 'L0_xattn_Wout': _L0_xattn_in['Wout'], 'L0_xattn_bout': _L0_xattn_in['bout'], 'L0_ffn_W_r': _L0_ffn_in['W_r'], 'L0_ffn_W_k': _L0_ffn_in['W_k'], 'L0_ffn_W_v': _L0_ffn_in['W_v'], 'L0_ffn_mu_r': _L0_ffn_in['mu_r'], 'L0_ffn_mu_k': _L0_ffn_in['mu_k']}

def reference(x, ctx_768, L0_attn_Wq, L0_attn_bq, L0_attn_Wk, L0_attn_bk, L0_attn_Wv, L0_attn_bv, L0_attn_Wo, L0_attn_bo, L0_attn_gamma, L0_attn_beta, L0_attn_rel_bias, L0_xattn_Wq, L0_xattn_Wk, L0_xattn_Wv, L0_xattn_Wout, L0_xattn_bout, L0_ffn_W_r, L0_ffn_W_k, L0_ffn_W_v, L0_ffn_mu_r, L0_ffn_mu_k):
    import jax
    import jax.numpy as jnp

    def _L0_attn_ref(x, Wq, bq, Wk, bk, Wv, bv, Wo, bo, gamma, beta, rel_bias):
        import jax, jax.numpy as jnp
        import numpy as np
        EMBED_DIM = 256
        NUM_HEADS = 16
        HEAD_DIM = EMBED_DIM // NUM_HEADS
        B, N = (2, 512)
        BIAS_S = 32

        def _interp_matrix(n, s):
            pos = jnp.arange(n, dtype=jnp.float32) * ((s - 1) / (n - 1))
            i0 = jnp.floor(pos).astype(jnp.int32)
            i1 = jnp.minimum(i0 + 1, s - 1)
            frac = pos - i0.astype(jnp.float32)
            rows = jnp.arange(n)
            M = jnp.zeros((n, s), dtype=jnp.float32)
            M = M.at[rows, i0].add(1.0 - frac).at[rows, i1].add(frac)
            return M
        Bx, Nx, C = x.shape
        H, D = (NUM_HEADS, HEAD_DIM)
        scale = 1.0 / jnp.sqrt(jnp.float32(D))
        mu = jnp.mean(x, axis=-1, keepdims=True)
        var = jnp.mean(jnp.square(x - mu), axis=-1, keepdims=True)
        xn = (x - mu) * jax.lax.rsqrt(var + 1e-05) * gamma + beta
        q = (xn @ Wq.T + bq).reshape(Bx, Nx, H, D).transpose(0, 2, 1, 3)
        k = (xn @ Wk.T + bk).reshape(Bx, Nx, H, D).transpose(0, 2, 1, 3)
        v = (xn @ Wv.T + bv).reshape(Bx, Nx, H, D).transpose(0, 2, 1, 3)
        attn = jnp.einsum('bhnd,bhmd->bhnm', q, k) * scale
        M = _interp_matrix(Nx, BIAS_S)
        rel = jnp.einsum('ni,hij,mj->hnm', M, rel_bias, M)
        rel = rel.at[:, -1, :].set(0.0).at[:, :, -1].set(0.0)
        attn = attn + rel[None]
        mask = jnp.triu(jnp.ones((Nx, Nx), dtype=bool), k=1)
        attn = jnp.where(mask, -jnp.inf, attn)
        attn = jax.nn.softmax(attn, axis=-1)
        out = jnp.einsum('bhnm,bhmd->bhnd', attn, v)
        out = out.transpose(0, 2, 1, 3).reshape(Bx, Nx, C)
        out = out @ Wo.T + bo
        return out

    def _L0_xattn_ref(x, context, Wq, Wk, Wv, Wout, bout):
        import jax, jax.numpy as jnp
        import numpy as np
        HEADS = 8
        DIM_HEAD = 128
        ATTN_MATRIX_SCALE = 1.5
        SCALE = DIM_HEAD ** (-0.5)

        def _split_heads(t):
            b, n, _ = t.shape
            t = t.reshape(b, n, HEADS, DIM_HEAD)
            return t.transpose(2, 0, 1, 3).reshape(HEADS, b * n, DIM_HEAD)
        b, n, _ = x.shape
        qh = _split_heads(jnp.einsum('bnq,qi->bni', x, Wq))
        kh = _split_heads(jnp.einsum('bmc,ci->bmi', context, Wk))
        vh = _split_heads(jnp.einsum('bmc,ci->bmi', context, Wv))
        sim = jnp.einsum('hid,hjd->hij', qh, kh) * SCALE
        mean = jnp.mean(sim, axis=-1, keepdims=True)
        sim = (sim - mean) * ATTN_MATRIX_SCALE + mean
        attn = jax.nn.softmax(sim, axis=-1)
        out = jnp.einsum('hij,hjd->hid', attn, vh)
        out = out.reshape(HEADS, b, n, DIM_HEAD).transpose(1, 2, 0, 3)
        out = out.reshape(b, n, HEADS * DIM_HEAD)
        return jnp.einsum('bni,iq->bnq', out, Wout) + bout

    def _L0_ffn_ref(x, W_r, W_k, W_v, mu_r, mu_k):
        import jax, jax.numpy as jnp
        import numpy as np
        DIM = 256

        def _reference_tuple_inner(x, W_r, W_k, W_v, mu_r, mu_k):
            B, T, C = x.shape
            x_prev = jnp.concatenate([jnp.zeros((B, 1, C), x.dtype), x[:, :-1, :]], axis=1)
            xr = mu_r * x + (1.0 - mu_r) * x_prev
            xk = mu_k * x + (1.0 - mu_k) * x_prev
            r = jax.nn.sigmoid(jnp.einsum('btc,dc->btd', xr, W_r))
            k = jnp.einsum('btc,dc->btd', xk, W_k)
            k_act = jnp.square(jax.nn.relu(k))
            out = r * jnp.einsum('btc,dc->btd', k_act, W_v)
            new_state = x[:, -1, :]
            return (out, new_state)
        return _reference_tuple_inner(x, W_r, W_k, W_v, mu_r, mu_k)[0]
    x = x + _L0_attn_ref(_layernorm(x, axis=-1), L0_attn_Wq, L0_attn_bq, L0_attn_Wk, L0_attn_bk, L0_attn_Wv, L0_attn_bv, L0_attn_Wo, L0_attn_bo, L0_attn_gamma, L0_attn_beta, L0_attn_rel_bias)
    x = x + _L0_xattn_ref(_layernorm(x, axis=-1), ctx_768, L0_xattn_Wq, L0_xattn_Wk, L0_xattn_Wv, L0_xattn_Wout, L0_xattn_bout)
    x = x + _L0_ffn_ref(_layernorm(x, axis=-1), L0_ffn_W_r, L0_ffn_W_k, L0_ffn_W_v, L0_ffn_mu_r, L0_ffn_mu_k)
    return x

_drawn_inputs = setup_inputs


def setup_inputs(seed=0):
    import zlib

    import numpy as np

    out = dict(_drawn_inputs(seed))
    spreads = {'L0_attn_bq': (0.0, 0.8),
     'L0_attn_bk': (0.0, 2.0),
     'L0_attn_bv': (0.0, 0.301),
     'L0_attn_bo': (0.0, 0.1),
     'L0_attn_gamma': (1.0, 0.6),
     'L0_attn_beta': (0.0, 0.8),
     'L0_xattn_bout': (0.0, 0.1)}
    factors = {'L0_attn_Wq': 8.0,
     'L0_attn_Wk': 8.0,
     'L0_attn_Wv': 3.588,
     'L0_attn_rel_bias': 44.559,
     'L0_ffn_W_r': 3.356,
     'L0_ffn_mu_r': 7.049}
    for name, (base, spread) in spreads.items():
        noise = np.random.default_rng([zlib.crc32(name.encode()), seed]).standard_normal(out[name].shape)
        drawn = base * np.exp(spread * noise) if base else spread * noise
        out[name] = jnp.asarray(drawn.astype(out[name].dtype))
    for name, factor in factors.items():
        out[name] = (out[name] * factor).astype(out[name].dtype)
    return out
```

```python
from contextlib import ExitStack

import numpy as np

import concourse.bass as bass
from concourse import mybir

ALU = mybir.AluOpType
ACT = mybir.ActivationFunctionType
AX = mybir.AxisListType
F32 = mybir.dt.float32
F32R = mybir.dt.float32r

P = 128
B, N, C = 4, 512, 256
T = B * N
NT = T // P
CH = C // P
EPS = 1e-5

SH, SD = 16, 16
BIAS_S = 32
QI = N // P
STACK = 3 * SD
REL_STACK = 3 * BIAS_S
MASKED = -1e30

XH, XD = 8, 128
CD, M = 192, 1024
KEYS = B * M
TAIL = CD - P
LOGIT = 1.5 * XD ** -0.5
G = 8
GQ = T // G
BLK = 512
NB = KEYS // BLK
CHUNK = 1024


def flat(ap):
    return ap.rearrange("p a b -> p (a b)")


def decoder_layer(nc, a, out, stages=3):
    with ExitStack() as ctx:
        x = ctx.enter_context(nc.sbuf_tensor("x", [P, NT, C], F32))
        ident = ctx.enter_context(nc.sbuf_tensor("ident", [P, P], F32))
        q_stacks = nc.dram_tensor("q_stacks", (SH, 3, SD, T), F32).ap()
        k_stacks = nc.dram_tensor("k_stacks", (SH, 3, SD, T), F32).ap()
        x2_split = nc.dram_tensor("x2_split", (G, P, 2, CH, GQ), F32).ap()
        ctx_split = nc.dram_tensor("ctx_split", (NB, P, 3, BLK), F32).ap()
        with ExitStack() as keep:
            v_self = keep.enter_context(nc.sbuf_tensor("v_self", [P, NT, C], F32))
            attn_out = keep.enter_context(nc.sbuf_tensor("attn_out", [P, NT, C], F32))
            self_projections(nc, a, x, ident, v_self, q_stacks, k_stacks)
            self_attention(nc, a, ident, v_self, attn_out, q_stacks, k_stacks)
            self_output(nc, a, x, ident, attn_out)
        if stages >= 2:
            k_shift = ctx.enter_context(nc.sbuf_tensor("k_shift", [P, XH], F32))
            cross_prepare(nc, a, x, ident, x2_split, ctx_split, k_shift)
            cross_attention(nc, a, x, ident, x2_split, ctx_split, k_shift)
        if stages >= 3:
            channel_mix(nc, a, x, ident)
        store_output(nc, x, out)


def store_output(nc, x, out):
    with ExitStack() as ctx:
        stored = ctx.enter_context(nc.semaphore("stored"))
        block = ctx.enter_context(nc.Block())

        @block.sync
        def _(sp):
            sp.dma_start(out.rearrange("(t p) c -> p t c", p=P), x[:]).then_inc(stored, 16)
            sp.wait_ge(stored, 16)


class Chain:

    def __init__(self, eng, sem):
        self.eng, self.sem, self.n = eng, sem, 0

    def __call__(self, ins):
        self.n += 1
        ins.then_inc(self.sem, 1)

    def wait(self):
        self.eng.wait_ge(self.sem, self.n)


def row_moments(dve, chain, src, parts, mv):
    for t in range(NT):
        chain(dve.bn_stats(parts[:, t, :], src[:, t, :]))
    chain.wait()
    for t in range(NT):
        chain(dve.bn_aggr(mv[:, t, :], parts[:, t, :]))
    chain.wait()


def inverse_root_seed(dve, chain, mv, var_eps, var_ready):
    dve.tensor_scalar(var_eps[:], mv[:, :, 1], EPS, None, ALU.add).then_inc(var_ready, 1)


def inverse_root(dve, chain, var_eps, root, rstd, tmp):
    chain(dve.reciprocal(rstd[:], root[:]))
    chain.wait()
    chain(dve.tensor_tensor(tmp[:], rstd[:], rstd[:], ALU.mult))
    chain.wait()
    chain(dve.tensor_tensor(tmp[:], tmp[:], var_eps[:], ALU.mult))
    chain.wait()
    chain(dve.tensor_scalar(tmp[:], tmp[:], -0.5, 1.5, ALU.mult, ALU.add))
    chain.wait()
    chain(dve.tensor_tensor(rstd[:], rstd[:], tmp[:], ALU.mult))
    chain.wait()


def self_projections(nc, a, x, ident, v_self, q_stacks, k_stacks):
    with ExitStack() as ctx:
        def sb(name, shape, dt=F32):
            return ctx.enter_context(nc.sbuf_tensor(name, shape, dt))

        def sem(name):
            return ctx.enter_context(nc.semaphore(name))

        y = sb("y", [P, NT, C])
        z_full = sb("z_full", [P, 2, 512])
        z_hi = sb("z_hi", [P, CH, T], F32R)
        z_lo = sb("z_lo", [P, CH, T], F32R)
        w_raw = sb("w_raw", [P, 3, CH, C])
        w_hi = sb("w_hi", [P, 3, CH, C], F32R)
        w_lo = sb("w_lo", [P, 3, CH, C], F32R)
        stage_hi = sb("stage_hi", [P, 2, T], F32R)
        stage_lo = sb("stage_lo", [P, 2, T], F32R)
        gamma, beta = sb("gamma", [P, CH]), sb("beta", [P, CH])
        bqk = sb("bqk", [P, 2, CH])
        bqk_scaled = sb("bqk_scaled", [P, 2, CH])
        bv = sb("bv", [P, C])
        parts, mv = sb("parts", [P, NT, 6]), sb("mv", [P, NT, 2])
        mv2 = sb("mv2", [P, NT, 2])
        var_eps, root = sb("var_eps", [P, NT]), sb("root", [P, NT])
        rstd, tmp = sb("rstd", [P, NT]), sb("tmp", [P, NT])
        banks = ctx.enter_context(nc.psum_tensor("banks", [P, 8, 512], F32))

        x_loaded, w_loaded, small_loaded = sem("x_loaded"), sem("w_loaded"), sem("small_loaded")
        var_ready, root_ready, z_ready = sem("var_ready"), sem("root_ready"), sem("z_ready")
        dve_self = sem("dve_self")
        w_hi_ready, w_lo_ready = sem("w_hi_ready"), sem("w_lo_ready")
        turned, z_hi_ready, z_lo_ready = sem("turned"), sem("z_hi_ready"), sem("z_lo_ready")
        projected, stage_hi_ready, stage_lo_ready = sem("projected"), sem("stage_hi_ready"), sem("stage_lo_ready")
        stack_stored = [sem("q_stack_stored"), sem("k_stack_stored")]
        v_done, v_ready = sem("v_done"), sem("v_ready")
        block = ctx.enter_context(nc.Block())

        TB = T // 512
        QK_UNITS = [(w, oh, tb) for oh in range(CH) for w in range(2) for tb in range(TB)]
        SMALL = 8

        @block.sync
        def _(sp):
            xs = a["x"].rearrange("(t p) c -> p t c", p=P)
            for t in range(0, NT, 4):
                sp.dma_start(x[:, t:t + 4, :], xs[:, t:t + 4, :]).then_inc(x_loaded, 16)
            for n, name in enumerate(("WqT", "WkT", "WvT")):
                sp.dma_start(w_raw[:, n, :, :], a[name].rearrange("(h p) o -> p h o", p=P)).then_inc(w_loaded, 16)
            with nc.allow_non_contiguous_dma(reason="a few per-channel vectors"):
                sp.dma_start(gamma[:], a["gamma"].rearrange("(h p) -> p h", p=P)).then_inc(small_loaded, 16)
                sp.dma_start(beta[:], a["beta"].rearrange("(h p) -> p h", p=P)).then_inc(small_loaded, 16)
                sp.dma_start(bqk[:, 0, :], a["bq"].rearrange("(h p) -> p h", p=P)).then_inc(small_loaded, 16)
                sp.dma_start(bqk[:, 1, :], a["bk"].rearrange("(h p) -> p h", p=P)).then_inc(small_loaded, 16)
            sp.dma_start(bv[:], a["bv"].rearrange("(a c) -> a c", a=1).to_broadcast([P, C])).then_inc(small_loaded, 16)
            sp.dma_start(ident[:], a["identity"]).then_inc(small_loaded, 16)
            half = SH // CH
            n = 0
            for oh in range(CH):
                for w, stacks, rows in ((0, q_stacks, ("hi", "hi", "lo")), (1, k_stacks, ("hi", "lo", "hi"))):
                    n += TB
                    sp.wait_ge(stage_hi_ready, n)
                    sp.wait_ge(stage_lo_ready, n)
                    for j, kind in enumerate(rows):
                        src = (stage_hi if kind == "hi" else stage_lo)[:, w, :].bitcast(F32)
                        for h in range(half):
                            sp.dma_start(stacks[oh * half + h, j], src[SD * h:SD * (h + 1), :]).then_inc(stack_stored[w], 16)
            for w in range(2):
                sp.wait_ge(stack_stored[w], 16 * 3 * SH)

        @block.vector
        def _(dve):
            chain = Chain(dve, dve_self)
            dve.wait_ge(x_loaded, 16 * 4)
            row_moments(dve, chain, x, parts, mv)
            inverse_root_seed(dve, chain, mv, var_eps, var_ready)
            dve.wait_ge(root_ready, 1)
            inverse_root(dve, chain, var_eps, root, rstd, tmp)
            for t in range(NT):
                chain(dve.tensor_scalar(y[:, t, :], x[:, t, :], mv[:, t, 0:1], rstd[:, t:t + 1],
                                        ALU.subtract, ALU.mult))
            chain.wait()
            row_moments(dve, chain, y, parts, mv2)
            inverse_root_seed(dve, chain, mv2, var_eps, var_ready)
            for n in range(3):
                dve.wait_ge(w_hi_ready, n + 1)
                dve.scalar_tensor_tensor(out=flat(w_lo[:, n]), in0=flat(w_raw[:, n]), scalar=SD ** -0.5 if n == 0 else 1.0,
                                         in1=flat(w_hi[:, n]).bitcast(F32), op0=ALU.mult,
                                         op1=ALU.subtract).then_inc(w_lo_ready, 1)
            dve.wait_ge(small_loaded, 16 * 6)
            dve.tensor_scalar(bqk_scaled[:, 0, :], bqk[:, 0, :], SD ** -0.5, None, ALU.mult)
            chain(dve.tensor_copy(bqk_scaled[:, 1, :], bqk[:, 1, :]))
            dve.wait_ge(root_ready, 2)
            inverse_root(dve, chain, var_eps, root, rstd, tmp)
            for t in range(NT):
                dve.tensor_scalar(y[:, t, :], y[:, t, :], mv2[:, t, 0:1], rstd[:, t:t + 1],
                                  ALU.subtract, ALU.mult).then_inc(z_ready, 1)
            for n in range(TB * CH):
                tb, h = n // CH, n % CH
                dve.wait_ge(turned, n + 1)
                dve.wait_ge(z_hi_ready, n + 1)
                if n >= 2:
                    dve.wait_ge(z_lo_ready, n - 1)
                chain(dve.tensor_scalar(z_full[:, n % 2, :], banks[:, n % 4, :], gamma[:, h:h + 1], beta[:, h:h + 1],
                                        ALU.mult, ALU.add))
                chain.wait()
                dve.tensor_tensor(z_lo[:, h, 512 * tb:512 * (tb + 1)], z_full[:, n % 2, :],
                                  z_hi[:, h, 512 * tb:512 * (tb + 1)].bitcast(F32), ALU.subtract).then_inc(z_lo_ready, 1)
            for n, (w, oh, tb) in enumerate(QK_UNITS):
                dve.wait_ge(stage_hi_ready, n + 1)
                if n >= 2 * TB and tb == 0:
                    dve.wait_ge(stack_stored[w], 16 * 3 * (SH // CH))
                dve.scalar_tensor_tensor(out=stage_lo[:, w, 512 * tb:512 * (tb + 1)], in0=banks[:, 4 + n % 4, :],
                                         scalar=bqk_scaled[:, w, oh:oh + 1],
                                         in1=stage_hi[:, w, 512 * tb:512 * (tb + 1)].bitcast(F32),
                                         op0=ALU.add, op1=ALU.subtract).then_inc(stage_lo_ready, 1)
            for t in range(NT):
                dve.wait_ge(v_done, t + 1)
                dve.tensor_tensor(v_self[:, t, :], banks[:, t % 4, 0:C], bv[:], ALU.add).then_inc(v_ready, 1)

        @block.scalar
        def _(act):
            act.wait_ge(var_ready, 1)
            act.activation(root[:], var_eps[:], ACT.Sqrt).then_inc(root_ready, 1)
            act.wait_ge(w_loaded, 16 * 3)
            for n in range(3):
                act.activation(flat(w_hi[:, n]), flat(w_raw[:, n]), ACT.Copy,
                               scale=SD ** -0.5 if n == 0 else 1.0).then_inc(w_hi_ready, 1)
            act.wait_ge(var_ready, 2)
            act.activation(root[:], var_eps[:], ACT.Sqrt).then_inc(root_ready, 1)
            act.wait_ge(small_loaded, 16 * 6)
            for n in range(TB * CH):
                tb, h = n // CH, n % CH
                act.wait_ge(turned, n + 1)
                act.activation(z_hi[:, h, 512 * tb:512 * (tb + 1)], banks[:, n % 4, :], ACT.Identity,
                               bias=beta[:, h:h + 1], scale=gamma[:, h:h + 1]).then_inc(z_hi_ready, 1)
            act.wait_ge(z_ready, 1)
            for n, (w, oh, tb) in enumerate(QK_UNITS):
                act.wait_ge(projected, n + 1)
                if n >= 2 * TB and tb == 0:
                    act.wait_ge(stack_stored[w], 16 * 3 * (SH // CH))
                act.activation(stage_hi[:, w, 512 * tb:512 * (tb + 1)], banks[:, 4 + n % 4, :], ACT.Identity,
                               bias=bqk_scaled[:, w, oh:oh + 1]).then_inc(stage_hi_ready, 1)

        @block.tensor
        def _(pe):
            pe.wait_ge(small_loaded, 16 * 6)
            for n in range(TB * CH):
                tb, h = n // CH, n % CH
                pe.wait_ge(z_ready, 4 * tb + 4)
                if n >= 4:
                    pe.wait_ge(z_lo_ready, n - 3)
                for t in range(4):
                    last = pe.transpose(banks[:, n % 4, P * t:P * (t + 1)], y[:, 4 * tb + t, P * h:P * (h + 1)], ident[:])
                last.then_inc(turned, 1)
            pe.wait_ge(z_lo_ready, TB * CH)
            pe.wait_ge(w_lo_ready, 3)
            for n, (w, oh, tb) in enumerate(QK_UNITS):
                if n >= 4:
                    pe.wait_ge(stage_lo_ready, n - 3)
                passes = [(ws, zs, h) for h in range(CH) for ws, zs in ((w_hi, z_hi), (w_hi, z_lo), (w_lo, z_hi))]
                for i, (ws, zs, h) in enumerate(passes):
                    last = pe.matmul(banks[:, 4 + n % 4, :], ws[:, w, h, P * oh:P * (oh + 1)],
                                     zs[:, h, 512 * tb:512 * (tb + 1)], start=i == 0, stop=i == len(passes) - 1)
                last.then_inc(projected, 1)
            for t in range(NT):
                if t >= 4:
                    pe.wait_ge(v_ready, t - 3)
                passes = [(ws, zs, h) for h in range(CH) for ws, zs in ((w_hi, z_hi), (w_lo, z_hi), (w_hi, z_lo))]
                for i, (ws, zs, h) in enumerate(passes):
                    last = pe.matmul(banks[:, t % 4, 0:C], zs[:, h, P * t:P * (t + 1)], ws[:, 2, h, :],
                                     start=i == 0, stop=i == len(passes) - 1)
                last.then_inc(v_done, 1)


UNITS = [[(3, 0)], [(0, 0), (2, P)], [(1, 0)]]


def self_attention(nc, a, ident, v_self, attn_out, q_stacks, k_stacks):
    with ExitStack() as ctx:
        def sb(name, shape, dt=F32):
            return ctx.enter_context(nc.sbuf_tensor(name, shape, dt))

        def sem(name):
            return ctx.enter_context(nc.semaphore(name))

        def psum(name, shape):
            return ctx.enter_context(nc.psum_tensor(name, shape, F32))

        q_st = [sb(f"q_st{h}", [STACK, T], F32R) for h in range(2)]
        k_st = [sb(f"k_st{h}", [STACK, T], F32R) for h in range(2)]
        rel_st = [sb(f"rel_st{h}", [BIAS_S, 3, BIAS_S]) for h in range(2)]
        interp = sb("interp", [BIAS_S, N])
        interp3 = sb("interp3", [REL_STACK, N])
        key_st = sb("key_st", [REL_STACK, N], F32R)
        key_hi = sb("key_hi", [REL_STACK, N], F32R)
        rows_hi = sb("rows_hi", [REL_STACK, N], F32R)
        rows_st = [sb(f"rows_st{h}", [REL_STACK, N], F32R) for h in range(2)]
        mask_raw, mask = sb("mask_raw", [P, P]), sb("mask", [P, P], F32R)
        ident_r = sb("ident_r", [P, P], F32R)
        probs = sb("probs", [P, 3, 512])
        probs_t = sb("probs_t", [P, 3, 512])
        neg_max = sb("neg_max", [P, 3, QI])
        sums, inv = sb("sums", [P, 2, QI]), sb("inv", [P, 2, QI])
        s_ps = psum("s_ps", [P, 3, 512])
        t_ps = psum("t_ps", [P, 2, 512])
        o_ps = psum("o_ps", [P, 2, 512])
        r_ps = psum("r_ps", [P, 512])

        const_loaded, const_hi, const_ready = sem("const_loaded"), sem("const_hi"), sem("const_ready")
        head_loaded = [sem(f"head_loaded{h}") for h in range(2)]
        rel_done, rows_hi_ready, rows_ready = sem("rel_done"), sem("rows_hi_ready"), sem("rows_ready")
        scored, maxed, exped = sem("scored"), sem("maxed"), sem("exped")
        turned, copied_act, copied_dve = sem("turned"), sem("copied_act"), sem("copied_dve")
        weighed, item_done, inv_ready, item_out = sem("weighed"), sem("item_done"), sem("inv_ready"), sem("item_out")
        block = ctx.enter_context(nc.Block())

        PER = 2 * B * len(UNITS)
        HALF = PER // 2
        LOADS = 16 * 5
        units = [(n // HALF, (n % HALF) // len(UNITS), UNITS[n % len(UNITS)]) for n in range(PER)]
        dve_copies = [n % len(UNITS) == 0 for n in range(PER)]
        seen = {True: [0], False: [0]}
        for n in range(PER):
            for who in (True, False):
                seen[who].append(seen[who][-1] + (dve_copies[n] == who))

        def wait_weighed(eng, it, n):
            if n % len(UNITS) == 2:
                eng.wait_ge(item_done, it * 2 * B + n // len(UNITS) + 1)
            else:
                eng.wait_ge(weighed, it * 4 * B + 2 * (n // len(UNITS)) + n % len(UNITS) + 1)

        @block.sync
        def _(sp):
            sp.dma_start(interp[:], a["interp"]).then_inc(const_loaded, 16)
            for j in range(3):
                sp.dma_start(interp3[BIAS_S * j:BIAS_S * (j + 1), :], a["interp"]).then_inc(const_loaded, 16)
            sp.dma_start(mask_raw[:], a["causal"]).then_inc(const_loaded, 16)

            def load(slot, head):
                sp.dma_start(q_st[slot][:].bitcast(F32), q_stacks.rearrange("h j r t -> h (j r) t")[bass.ds(head, 1)].rearrange("o r t -> (o r) t")).then_inc(head_loaded[slot], 16)
                sp.dma_start(k_st[slot][:].bitcast(F32), k_stacks.rearrange("h j r t -> h (j r) t")[bass.ds(head, 1)].rearrange("o r t -> (o r) t")).then_inc(head_loaded[slot], 16)
                for j in range(3):
                    sp.dma_start(rel_st[slot][:, j, :], a["rel_bias"][bass.ds(head, 1)].rearrange("o i j -> (o i) j")).then_inc(head_loaded[slot], 16)

            load(0, 0)
            load(1, 1)
            with sp.Fori(0, SH // 2 - 1) as it:
                for slot in range(2):
                    sp.wait_ge(scored, it * PER + HALF * (slot + 1))
                    load(slot, it * 2 + 2 + slot)

        @block.tensor
        def _(pe):
            pe.wait_ge(const_ready, 1)
            with pe.Fori(0, SH // 2) as it:
                def relative_rows(slot):
                    pe.wait_ge(head_loaded[slot], it * LOADS + LOADS)
                    if slot:
                        pe.wait_ge(rows_ready, it * 2 + 1)
                    pe.matmul(r_ps[0:REL_STACK, :], rel_st[slot][:].rearrange("i j c -> i (j c)"), interp[:],
                              start=True, stop=True).then_inc(rel_done, 1)

                def scores(n):
                    slot, b, tiles = units[n]
                    if n % HALF == 0:
                        pe.wait_ge(rows_ready, it * 2 + slot + 1)
                    if n >= 3:
                        pe.wait_ge(exped, it * PER + n - 2)
                    for i, c0 in tiles:
                        w = P * (i + 1)
                        q0 = N * b + P * i
                        pe.matmul(s_ps[:, n % 3, c0:c0 + w], rows_st[slot][:, P * i:P * (i + 1)], key_st[:, 0:w],
                                  start=True, stop=False)
                        pe.matmul(s_ps[:, n % 3, c0:c0 + w], q_st[slot][:, q0:q0 + P], k_st[slot][:, N * b:N * b + w],
                                  start=False, stop=False)
                        last = pe.matmul(s_ps[:, n % 3, c0 + w - P:c0 + w], ident_r[:], mask[:], start=False, stop=True)
                    last.then_inc(scored, 1)

                def turn(n):
                    slot, b, tiles = units[n]
                    pe.wait_ge(exped, it * PER + n + 1)
                    if n >= 2:
                        who = dve_copies[n - 2]
                        pe.wait_ge(copied_dve if who else copied_act, it * seen[who][PER] + seen[who][n - 1])
                    for i, c0 in tiles:
                        for j in range(i + 1):
                            cols = slice(c0 + P * j, c0 + P * (j + 1))
                            last = pe.transpose(t_ps[:, n % 2, cols], probs[:, n % 3, cols], ident[:])
                    last.then_inc(turned, 1)

                def weigh(n):
                    slot, b, tiles = units[n]
                    item = n // len(UNITS)
                    who = dve_copies[n]
                    pe.wait_ge(copied_dve if who else copied_act, it * seen[who][PER] + seen[who][n + 1])
                    if n % len(UNITS) == 0 and item >= 2:
                        pe.wait_ge(item_out, it * 2 * B + item - 1)
                    for i, c0 in tiles:
                        for j in range(i + 1):
                            last = pe.matmul(o_ps[:, item % 2, SD * i:SD * (i + 1)],
                                             probs_t[:, n % 3, c0 + P * j:c0 + P * (j + 1)],
                                             v_self[:, QI * b + j, bass.ds(it * 2 * SD + SD * slot, SD)],
                                             start=j == 0, stop=j == i)
                    last.then_inc(item_done if n % len(UNITS) == 2 else weighed, 1)

                relative_rows(0)
                for n in range(PER + 3):
                    if n == 2:
                        relative_rows(1)
                    if n < PER:
                        scores(n)
                    if 2 <= n < PER + 2:
                        turn(n - 2)
                    if n >= 3:
                        weigh(n - 3)

        @block.scalar
        def _(act):
            act.wait_ge(const_loaded, 16 * 5)
            act.copy(key_hi[:], interp3[:])
            act.copy(key_st[0:BIAS_S, :], interp3[0:BIAS_S, :])
            act.copy(key_st[2 * BIAS_S:, :], interp3[2 * BIAS_S:, :])
            act.copy(mask[:], mask_raw[:])
            act.copy(ident_r[:], ident[:]).then_inc(const_hi, 1)
            with act.Fori(0, SH // 2) as it:
                def relative_rows(slot):
                    act.wait_ge(rel_done, it * 2 + slot + 1)
                    act.copy(rows_st[slot][0:2 * BIAS_S, :], r_ps[0:2 * BIAS_S, :])
                    act.copy(rows_hi[2 * BIAS_S:, :], r_ps[2 * BIAS_S:REL_STACK, :]).then_inc(rows_hi_ready, 1)

                def exponents(n):
                    slot, b, tiles = units[n]
                    item = n // len(UNITS)
                    act.wait_ge(maxed, it * PER + n + 1)
                    if n >= 3:
                        act.wait_ge(turned, it * PER + n - 2)
                    if n % len(UNITS) == 0 and item >= 2:
                        act.wait_ge(item_out, it * 2 * B + item - 1)
                    for i, c0 in tiles:
                        w = P * (i + 1)
                        last = act.activation(probs[:, n % 3, c0:c0 + w], s_ps[:, n % 3, c0:c0 + w], ACT.Exp,
                                              bias=neg_max[:, n % 3, i:i + 1], accum_out=sums[:, item % 2, i:i + 1])
                    last.then_inc(exped, 1)

                def copy_turned(n):
                    slot, b, tiles = units[n]
                    w = sum(P * (i + 1) for i, _ in tiles)
                    act.wait_ge(turned, it * PER + n + 1)
                    if n >= 3:
                        wait_weighed(act, it, n - 3)
                    act.copy(probs_t[:, n % 3, 0:w], t_ps[:, n % 2, 0:w]).then_inc(copied_act, 1)

                relative_rows(0)
                for n in range(PER + 2):
                    if n == 2:
                        relative_rows(1)
                    if n < PER:
                        exponents(n)
                    if n >= 2 and not dve_copies[n - 2]:
                        copy_turned(n - 2)

        @block.vector
        def _(dve):
            dve.wait_ge(const_hi, 1)
            dve.tensor_tensor(key_st[BIAS_S:2 * BIAS_S, :], interp3[BIAS_S:2 * BIAS_S, :],
                              key_hi[BIAS_S:2 * BIAS_S, :].bitcast(F32), ALU.subtract).then_inc(const_ready, 1)
            with dve.Fori(0, SH // 2) as it:
                def relative_rows(slot):
                    dve.wait_ge(rows_hi_ready, it * 2 + slot + 1)
                    dve.tensor_tensor(rows_st[slot][2 * BIAS_S:, :], r_ps[2 * BIAS_S:REL_STACK, :],
                                      rows_hi[2 * BIAS_S:, :].bitcast(F32), ALU.subtract).then_inc(rows_ready, 1)

                def maxima(n):
                    slot, b, tiles = units[n]
                    dve.wait_ge(scored, it * PER + n + 1)
                    for i, c0 in tiles:
                        last = dve.tensor_reduce(neg_max[:, n % 3, i:i + 1], s_ps[:, n % 3, c0:c0 + P * (i + 1)],
                                                 AX.X, ALU.max, negate=True)
                    last.then_inc(maxed, 1)

                def copy_turned(n):
                    dve.wait_ge(turned, it * PER + n + 1)
                    if n >= 3:
                        wait_weighed(dve, it, n - 3)
                    dve.tensor_copy(probs_t[:, n % 3, :], t_ps[:, n % 2, :]).then_inc(copied_dve, 1)

                def normalise(item):
                    slot, b = item // B, item % B
                    dve.wait_ge(item_done, it * 2 * B + item + 1)
                    dve.reciprocal(inv[:, item % 2, :], sums[:, item % 2, :]).then_inc(inv_ready, 1)
                    dve.wait_ge(inv_ready, it * 2 * B + item + 1)
                    dve.tensor_tensor(
                        attn_out[:, QI * b:QI * (b + 1), bass.ds(it * 2 * SD + SD * slot, SD)],
                        o_ps[:, item % 2, 0:QI * SD].rearrange("p (i d) -> p i d", d=SD),
                        inv[:, item % 2, :].rearrange("p (i o) -> p i o", o=1).to_broadcast([P, QI, SD]),
                        ALU.mult).then_inc(item_out, 1)

                relative_rows(0)
                for n in range(PER + 4):
                    if n == 2:
                        relative_rows(1)
                    if n < PER:
                        maxima(n)
                    if 2 <= n < PER + 2 and dve_copies[n - 2]:
                        copy_turned(n - 2)
                    if n >= 4 and (n - 4) % len(UNITS) == 2:
                        normalise((n - 4) // len(UNITS))


def self_output(nc, a, x, ident, attn_out):
    with ExitStack() as ctx:
        def sb(name, shape, dt=F32):
            return ctx.enter_context(nc.sbuf_tensor(name, shape, dt))

        def sem(name):
            return ctx.enter_context(nc.semaphore(name))

        w_raw = sb("wo_raw", [P, CH, C])
        w_hi, w_lo = sb("wo_hi", [P, CH, C], F32R), sb("wo_lo", [P, CH, C], F32R)
        bo = sb("bo", [P, C])
        o_hi, o_lo = sb("so_hi", [P, 2, CH, P], F32R), sb("so_lo", [P, 2, CH, P], F32R)
        t_ps = ctx.enter_context(nc.psum_tensor("so_t", [P, 2, 512], F32))
        y_ps = ctx.enter_context(nc.psum_tensor("so_y", [P, 2, 512], F32))
        loaded, w_hi_ready, w_ready = sem("so_loaded"), sem("so_w_hi"), sem("so_w")
        turned, hi_ready, lo_ready = sem("so_turned"), sem("so_hi_ready"), sem("so_lo_ready")
        projected, biased, added = sem("so_projected"), sem("so_biased"), sem("so_added")
        block = ctx.enter_context(nc.Block())

        @block.sync
        def _(sp):
            sp.dma_start(w_raw[:], a["WoT"].rearrange("(h p) o -> p h o", p=P)).then_inc(loaded, 16)
            sp.dma_start(bo[:], a["bo"].rearrange("(a c) -> a c", a=1).to_broadcast([P, C])).then_inc(loaded, 16)

        @block.scalar
        def _(act):
            act.wait_ge(loaded, 32)
            act.copy(flat(w_hi[:]), flat(w_raw[:])).then_inc(w_hi_ready, 1)
            for t in range(NT):
                act.wait_ge(turned, t + 1)
                if t >= 2:
                    act.wait_ge(projected, t - 1)
                act.copy(flat(o_hi[:, t % 2]), t_ps[:, t % 2, 0:C]).then_inc(hi_ready, 1)

        @block.vector
        def _(dve):
            dve.wait_ge(w_hi_ready, 1)
            dve.tensor_tensor(flat(w_lo[:]), flat(w_raw[:]), flat(w_hi[:]).bitcast(F32), ALU.subtract).then_inc(w_ready, 1)
            for t in range(NT):
                dve.tensor_tensor(x[:, t, :], x[:, t, :], bo[:], ALU.add).then_inc(biased, 1)
            for t in range(NT + 1):
                if t < NT:
                    dve.wait_ge(hi_ready, t + 1)
                    if t >= 2:
                        dve.wait_ge(projected, t - 1)
                    dve.tensor_tensor(flat(o_lo[:, t % 2]), t_ps[:, t % 2, 0:C], flat(o_hi[:, t % 2]).bitcast(F32),
                                      ALU.subtract).then_inc(lo_ready, 1)
                if t >= 1:
                    dve.wait_ge(projected, t)
                    dve.wait_ge(biased, t)
                    dve.tensor_tensor(x[:, t - 1, :], x[:, t - 1, :], y_ps[:, (t - 1) % 2, 0:C], ALU.add).then_inc(added, 1)

        @block.tensor
        def _(pe):
            def turn(t):
                if t >= 2:
                    pe.wait_ge(lo_ready, t - 1)
                for h in range(CH):
                    last = pe.transpose(t_ps[:, t % 2, P * h:P * (h + 1)], attn_out[:, t, P * h:P * (h + 1)], ident[:])
                last.then_inc(turned, 1)

            turn(0)
            pe.wait_ge(w_ready, 1)
            for t in range(NT):
                if t + 1 < NT:
                    turn(t + 1)
                pe.wait_ge(lo_ready, t + 1)
                if t >= 2:
                    pe.wait_ge(added, t - 1)
                passes = [(os, ws, h) for h in range(CH) for os, ws in ((o_hi, w_hi), (o_hi, w_lo), (o_lo, w_hi))]
                for i, (os, ws, h) in enumerate(passes):
                    last = pe.matmul(y_ps[:, t % 2, 0:C], os[:, t % 2, h, :], ws[:, h, :], start=i == 0,
                                     stop=i == len(passes) - 1)
                last.then_inc(projected, 1)

def cross_prepare(nc, a, x, ident, x2_split, ctx_split, k_shift):
    with ExitStack() as ctx:
        def sb(name, shape, dt=F32):
            return ctx.enter_context(nc.sbuf_tensor(name, shape, dt))

        def sem(name):
            return ctx.enter_context(nc.semaphore(name))

        y = sb("y2", [P, NT, C])
        parts, mv = sb("parts2", [P, NT, 6]), sb("mv2b", [P, NT, 2])
        var_eps, root = sb("var_eps2", [P, NT]), sb("root2", [P, NT])
        rstd, tmp = sb("rstd2", [P, NT]), sb("tmp2", [P, NT])
        bout = sb("bout", [P, C])
        ctx_main, ctx_tail = sb("ctx_main", [P, KEYS]), sb("ctx_tail", [P, KEYS])
        ctx_sum = sb("ctx_sum", [P, 2])
        wk_main, wk_tail = sb("wk_main", [P, XH * XD]), sb("wk_tail", [TAIL, XH * XD])
        tail_hi = sb("tail_hi", [P, 2, BLK], F32R)
        ctx_out = sb("ctx_out", [P, 2, 3, BLK], F32R)
        xq_out = sb("xq_out", [P, 2, 2, CH, GQ], F32R)
        banks = ctx.enter_context(nc.psum_tensor("banks2", [P, 4, 512], F32))
        mean_ps = ctx.enter_context(nc.psum_tensor("mean_ps", [P, 512], F32))

        ctx_loaded = [sem(f"ctx_loaded{b}") for b in range(2)]
        small_loaded = sem("small_loaded2")
        var_ready, root_ready, y_ready = sem("var_ready2"), sem("root_ready2"), sem("y_ready")
        dve_self = sem("dve_self2")
        ctx_hi, ctx_lo = sem("ctx_hi"), sem("ctx_lo")
        ctx_stored = [sem(f"ctx_stored{s}") for s in range(2)]
        xq_stored = [sem(f"xq_stored{s}") for s in range(2)]
        sums_ready, means_done = sem("sums_ready"), sem("means_done")
        turned, xq_hi, xq_lo = sem("turned2"), sem("xq_hi"), sem("xq_lo")
        block = ctx.enter_context(nc.Block())

        @block.sync
        def _(sp):
            half = KEYS // 2
            for b in range(2):
                cols = slice(half * b, half * (b + 1))
                sp.dma_start(ctx_main[:, cols], a["ctxT"][0:P, cols]).then_inc(ctx_loaded[b], 16)
                for d in range(2):
                    sp.dma_start(ctx_tail[TAIL * d:TAIL * (d + 1), cols], a["ctxT"][P:CD, cols]).then_inc(ctx_loaded[b], 16)
            sp.dma_start(wk_main[:], a["XWk"][0:P, :]).then_inc(small_loaded, 16)
            sp.dma_start(wk_tail[:], a["XWk"][P:CD, :]).then_inc(small_loaded, 16)
            sp.dma_start(bout[:], a["Xbout"].rearrange("(a c) -> a c", a=1).to_broadcast([P, C])).then_inc(small_loaded, 16)
            for b in range(NB):
                sp.wait_ge(ctx_hi, b + 1)
                sp.wait_ge(ctx_lo, b + 1)
                sp.dma_start(ctx_split[b], ctx_out[:, b % 2].bitcast(F32)).then_inc(ctx_stored[b % 2], 16)
            for g in range(G):
                sp.wait_ge(xq_hi, g + 1)
                sp.wait_ge(xq_lo, g + 1)
                sp.dma_start(x2_split[g], xq_out[:, g % 2].bitcast(F32)).then_inc(xq_stored[g % 2], 16)
            for s in range(2):
                sp.wait_ge(ctx_stored[s], 16 * NB // 2)
                sp.wait_ge(xq_stored[s], 16 * G // 2)

        @block.vector
        def _(dve):
            chain = Chain(dve, dve_self)
            row_moments(dve, chain, x, parts, mv)
            inverse_root_seed(dve, chain, mv, var_eps, var_ready)
            for b in range(NB):
                cols = slice(BLK * b, BLK * (b + 1))
                dve.wait_ge(ctx_hi, b + 1)
                if b >= 2:
                    dve.wait_ge(ctx_stored[b % 2], 16 * (b // 2))
                dve.tensor_tensor(ctx_out[:, b % 2, 1, :], ctx_main[:, cols], ctx_out[:, b % 2, 0, :].bitcast(F32),
                                  ALU.subtract)
                dve.tensor_tensor(ctx_out[TAIL:, b % 2, 2, :], ctx_tail[TAIL:, cols], tail_hi[TAIL:, b % 2, :].bitcast(F32),
                                  ALU.subtract).then_inc(ctx_lo, 1)
            dve.tensor_reduce(ctx_sum[:, 0:1], ctx_main[:], AX.X, ALU.add)
            dve.tensor_reduce(ctx_sum[0:TAIL, 1:2], ctx_tail[0:TAIL, :], AX.X, ALU.add).then_inc(sums_ready, 1)
            dve.wait_ge(root_ready, 1)
            inverse_root(dve, chain, var_eps, root, rstd, tmp)
            for t in range(NT):
                dve.tensor_scalar(y[:, t, :], x[:, t, :], mv[:, t, 0:1], rstd[:, t:t + 1],
                                  ALU.subtract, ALU.mult).then_inc(y_ready, 1)
            for g in range(G):
                dve.wait_ge(xq_hi, g + 1)
                if g >= 2:
                    dve.wait_ge(xq_stored[g % 2], 16 * (g // 2))
                dve.tensor_tensor(flat(xq_out[:, g % 2, 1]), banks[:, g % 4, :], flat(xq_out[:, g % 2, 0]).bitcast(F32),
                                  ALU.subtract).then_inc(xq_lo, 1)
            dve.wait_ge(means_done, 1)
            dve.tensor_scalar(k_shift[:], mean_ps[:, 0:XH], -1.0 / (3.0 * KEYS), None, ALU.mult)
            dve.wait_ge(small_loaded, 48)
            dve.wait_ge(y_ready, NT)
            for t in range(NT):
                dve.tensor_tensor(x[:, t, :], x[:, t, :], bout[:], ALU.add)

        @block.scalar
        def _(act):
            act.wait_ge(var_ready, 1)
            act.activation(root[:], var_eps[:], ACT.Sqrt).then_inc(root_ready, 1)
            for b in range(NB):
                cols = slice(BLK * b, BLK * (b + 1))
                act.wait_ge(ctx_loaded[b // (NB // 2)], 48)
                if b >= 2:
                    act.wait_ge(ctx_stored[b % 2], 16 * (b // 2))
                    act.wait_ge(ctx_lo, b - 1)
                act.copy(ctx_out[:, b % 2, 0, :], ctx_main[:, cols])
                act.copy(ctx_out[0:TAIL, b % 2, 2, :], ctx_tail[0:TAIL, cols])
                act.copy(tail_hi[TAIL:, b % 2, :], ctx_tail[TAIL:, cols]).then_inc(ctx_hi, 1)
            for g in range(G):
                act.wait_ge(turned, g + 1)
                if g >= 2:
                    act.wait_ge(xq_stored[g % 2], 16 * (g // 2))
                act.copy(flat(xq_out[:, g % 2, 0]), banks[:, g % 4, :]).then_inc(xq_hi, 1)

        @block.tensor
        def _(pe):
            pe.wait_ge(sums_ready, 1)
            pe.wait_ge(small_loaded, 48)
            for h in range(XH):
                pe.matmul(mean_ps[:, h:h + 1], wk_main[:, XD * h:XD * (h + 1)], ctx_sum[:, 0:1], start=True, stop=False)
                last = pe.matmul(mean_ps[:, h:h + 1], wk_tail[:, XD * h:XD * (h + 1)], ctx_sum[0:TAIL, 1:2],
                                 start=False, stop=True)
            last.then_inc(means_done, 1)
            for g in range(G):
                pe.wait_ge(y_ready, 2 * g + 2)
                if g >= 4:
                    pe.wait_ge(xq_lo, g - 3)
                for h in range(CH):
                    for t in range(2):
                        last = pe.transpose(banks[:, g % 4, GQ * h + P * t:GQ * h + P * (t + 1)],
                                            y[:, 2 * g + t, P * h:P * (h + 1)], ident[:])
                last.then_inc(turned, 1)


FIRST = 8
PER_HEAD = 8 * G + G + 8
TAIL_AT = 8 * G + G - 2
T_CHUNKS = KEYS // (2 * P)
KV_ORDER = [("K", 0), ("K", 1), ("V", 0), ("V", 1), ("K", 2), ("V", 2), ("K", 3), ("V", 3)]
TAIL_CHUNK = {("K", 0): 0, ("K", 1): 1, ("out", 6): 2, ("V", 0): 3, ("V", 1): 4, ("out", 7): 5,
              ("K", 2): 6, ("V", 2): 7, ("K", 3): 8, ("V", 3): 9}


def cross_attention(nc, a, x, ident, x2_split, ctx_split, k_shift):
    with ExitStack() as ctx:
        def sb(name, shape, dt=F32):
            return ctx.enter_context(nc.sbuf_tensor(name, shape, dt))

        def sem(name):
            return ctx.enter_context(nc.semaphore(name))

        k_hi, k_lo = sb("k_hi", [P, KEYS], F32R), sb("k_lo", [P, KEYS], F32R)
        v_hi, v_lo = sb("v_hi", [P, KEYS], F32R), sb("v_lo", [P, KEYS], F32R)
        probs = sb("xprobs", [P, 2, 2, KEYS])
        blocks = sb("blocks", [P, 4, 3, BLK], F32R)
        pt_hi, pt_lo = sb("pt_hi", [P, 3, 2 * GQ], F32R), sb("pt_lo", [P, 3, 2 * GQ], F32R)
        xq = sb("xq", [P, 2, CH, GQ], F32R)
        q_hi, q_lo = sb("q_hi", [P, 2, GQ], F32R), sb("q_lo", [P, 2, GQ], F32R)
        o_hi, o_lo = sb("o_hi", [P, GQ], F32R), sb("o_lo", [P, GQ], F32R)
        wq_raw, wq_hi, wq_lo = sb("wq_raw", [P, CH * XD]), sb("wq_hi", [P, CH * XD], F32R), sb("wq_lo", [P, CH * XD], F32R)
        kv_raw, kv_hi, kv_lo = sb("kv_raw", [P, 4 * XD]), sb("kv_hi", [P, 4 * XD], F32R), sb("kv_lo", [P, 4 * XD], F32R)
        wo_raw, wo_hi, wo_lo = sb("wo_raw2", [P, C]), sb("wo_hi2", [P, C], F32R), sb("wo_lo2", [P, C], F32R)
        shift = sb("shift", [P, 1])
        chunk_max, neg_max = sb("chunk_max", [P, 2, 4]), sb("xneg_max", [P, 2, 2])
        chunk_sum, denom, inv = sb("chunk_sum", [P, 2, 2, 4]), sb("denom", [P, 2]), sb("xinv", [P, 2, 2])
        s_ps = ctx.enter_context(nc.psum_tensor("xs_ps", [P, 2, CHUNK], F32))
        t_ps = ctx.enter_context(nc.psum_tensor("xt_ps", [P, 3, 512], F32))
        o_ps = ctx.enter_context(nc.psum_tensor("xo_ps", [P, 512], F32))

        kv_loaded, wq_loaded, wo_loaded = sem("kv_loaded"), sem("wq_loaded"), sem("wo_loaded")
        kv_w_hi, wq_w_hi, wo_w_hi = sem("kv_w_hi"), sem("wq_w_hi"), sem("wo_w_hi")
        kv_w, wq_w, wo_w = sem("kv_w"), sem("wq_w"), sem("wo_w")
        blocks_loaded = [sem(f"blocks_loaded{s}") for s in range(2)]
        xq_loaded = sem("xq_loaded")
        filled, freed = sem("filled"), sem("freed")
        kv_rounded = sem("kv_rounded")
        q_done, q_rounded, q_ready = sem("q_done"), sem("q_rounded"), sem("q_ready")
        maxed, exped, inv_ready = sem("xmaxed"), sem("xexped"), sem("xinv_ready")
        summed = sem("summed")
        turned, t_rounded, t_ready = sem("xturned"), sem("t_rounded"), sem("t_ready")
        weighed = sem("xweighed")
        o_done, o_rounded, o_ready = sem("o_done"), sem("o_rounded"), sem("o_ready")
        shifted = sem("shifted")
        block = ctx.enter_context(nc.Block())

        def heads(eng, head):
            with eng.Fori(0, XH - 1) as h:
                head(h, False)
            head(XH - 1, True)

        def at(h, chunk):
            return h * PER_HEAD + (FIRST + chunk)

        @block.sync
        def _(sp):
            def load_weights(which, col):
                if which == "kv":
                    for n, name in enumerate(("XWk", "XWv")):
                        w = a[name][:, bass.ds(col, XD)]
                        sp.dma_start(kv_raw[:, 2 * XD * n:2 * XD * n + XD], w[0:P, :]).then_inc(kv_loaded, 16)
                        for d in range(2):
                            sp.dma_start(kv_raw[TAIL * d:TAIL * (d + 1), 2 * XD * n + XD:2 * XD * (n + 1)],
                                         w[P:CD, :]).then_inc(kv_loaded, 16)
                elif which == "q":
                    for k in range(CH):
                        sp.dma_start(wq_raw[:, XD * k:XD * (k + 1)],
                                     a["XWq"][P * k:P * (k + 1), bass.ds(col, XD)]).then_inc(wq_loaded, 16)
                else:
                    sp.dma_start(wo_raw[:], a["XWout"][bass.ds(col, XD), :]).then_inc(wo_loaded, 16)

            def load_blocks(pair):
                for b in (2 * pair, 2 * pair + 1):
                    sp.dma_start(blocks[:, b % 4].bitcast(F32), ctx_split[b]).then_inc(blocks_loaded[pair % 2], 16)

            def load_queries(group):
                sp.dma_start(xq[:].bitcast(F32), x2_split[bass.ds(group, 1)].rearrange("o p s k q -> (o p) s k q")).then_inc(xq_loaded, 16)

            load_weights("kv", 0)
            load_blocks(0)
            load_weights("q", 0)
            load_queries(0)
            load_blocks(1)
            sp.wait_ge(filled, 3)
            load_blocks(2)
            sp.wait_ge(filled, 4)
            load_blocks(3)

            def head(h, last):
                def value(v):
                    return v if last else sp.snap(v)

                used = value(at(h, 0))
                wo_cols = value(h * XD)
                q_base = value(h * G)
                if not last:
                    next_cols = sp.snap(h * XD + XD)
                sp.wait_ge(filled, used)
                if not last:
                    load_weights("kv", next_cols)
                    load_weights("q", next_cols)
                load_weights("out", wo_cols)
                if not last:
                    load_blocks(0)
                    load_blocks(1)
                with sp.Fori(0, G - 1) as g:
                    projected, group = sp.snap(q_base + g + 1), sp.snap(g + 1)
                    sp.wait_ge(q_done, projected)
                    load_queries(group)
                if not last:
                    projected = sp.snap(q_base + G)
                    used = [sp.snap(at(h, TAIL_AT + TAIL_CHUNK["V", i] + 1)) for i in range(2)]
                    sp.wait_ge(q_done, projected)
                    load_queries(0)
                    sp.wait_ge(filled, used[0])
                    load_blocks(2)
                    sp.wait_ge(filled, used[1])
                    load_blocks(3)

            heads(sp, head)

        @block.tensor
        def _(pe):
            def fill(chunk, first=False):
                if not first:
                    pe.wait_ge(freed, chunk - 1)

            def project_kv(kind, i, h, chunk, buf, first=False):
                fill(chunk, first)
                if kind == "K" or i < 2:
                    pe.wait_ge(blocks_loaded[i % 2], h * 64 + 32 * (i // 2) + 32)
                n0 = 0 if kind == "K" else 2 * XD
                main, tail = slice(n0, n0 + XD), slice(n0 + XD, n0 + 2 * XD)
                for b in (2 * i, 2 * i + 1):
                    s = b % 4
                    passes = [(kv_hi[:, main], 0, P), (kv_lo[:, main], 0, P), (kv_hi[:, main], 1, P),
                              (kv_hi[:, tail], 2, P), (kv_lo[0:TAIL, tail], 2, TAIL)]
                    o0 = BLK * (b % 2)
                    if kind == "K":
                        for n, (w, part, rows) in enumerate(passes):
                            last = pe.matmul(s_ps[:, buf, o0:o0 + BLK], w, blocks[0:rows, s, part, :],
                                             start=n == 0, stop=n == len(passes) - 1)
                    else:
                        for t in range(BLK // P):
                            for n, (w, part, rows) in enumerate(passes):
                                last = pe.matmul(s_ps[:, buf, o0 + P * t:o0 + P * (t + 1)],
                                                 blocks[0:rows, s, part, P * t:P * (t + 1)], w,
                                                 start=n == 0, stop=n == len(passes) - 1)
                last.then_inc(filled, 1)

            def project_q(step, par):
                pe.wait_ge(xq_loaded, step * 16 + 16)
                passes = [(w, part, k) for k in range(CH) for w, part in ((wq_hi, 0), (wq_hi, 1), (wq_lo, 0))]
                for n, (w, part, k) in enumerate(passes):
                    last = pe.matmul(o_ps[:, 0:GQ], w[:, XD * k:XD * (k + 1)], xq[:, part, k, :],
                                     start=n == 0, stop=n == len(passes) - 1)
                last.then_inc(q_done, 1)

            def scores(step, par, chunk):
                pe.wait_ge(q_ready, step + 1)
                for n in range(8):
                    t, i = n // 4, n % 4
                    buf = (n + chunk_parity[0]) % 2
                    fill(chunk + n)
                    qs = slice(P * t, P * (t + 1))
                    for m, (q, k) in enumerate(((q_hi, k_hi), (q_hi, k_lo), (q_lo, k_hi))):
                        for b in range(2):
                            k0 = CHUNK * i + BLK * b
                            last = pe.matmul(s_ps[:, buf, BLK * b:BLK * (b + 1)], q[:, par, qs], k[:, k0:k0 + BLK],
                                             start=m == 0, stop=m == 2)
                    last.then_inc(filled, 1)

            chunk_parity = [0]

            def turn(c, par, step):
                if c >= 3:
                    pe.wait_ge(t_ready, step * T_CHUNKS + (c - 2))
                for j in range(2):
                    for t in range(2):
                        last = pe.transpose(t_ps[:, c % 3, GQ * j + P * t:GQ * j + P * (t + 1)],
                                            probs[:, par, t, P * (2 * c + j):P * (2 * c + j + 1)], ident[:])
                last.then_inc(turned, 1)

            def weigh(c, step):
                pe.wait_ge(t_ready, step * T_CHUNKS + (c + 1))
                for j in range(2):
                    vs = slice(P * (2 * c + j), P * (2 * c + j + 1))
                    for m, (v, pt) in enumerate(((v_hi, pt_hi), (v_hi, pt_lo), (v_lo, pt_hi))):
                        last = pe.matmul(o_ps[:, 0:GQ], v[:, vs], pt[:, c % 3, GQ * j:GQ * (j + 1)],
                                         start=c == 0 and j == 0 and m == 0, stop=c == T_CHUNKS - 1 and j == 1 and m == 2)
                last.then_inc(o_done if c == T_CHUNKS - 1 else weighed, 1)

            def attend(step, par, q_behind):
                pe.wait_ge(exped, step * 2 + 2)
                for c in range(T_CHUNKS + 2):
                    if c < T_CHUNKS:
                        turn(c, par, step)
                    if c == 2 and q_behind is not None:
                        pe.wait_ge(q_ready, q_behind + 1)
                    if c >= 2:
                        weigh(c - 2, step)

            def project_out(h, step, chunk, buf):
                pe.wait_ge(wo_w, h + 1)
                pe.wait_ge(o_ready, step + 1)
                fill(chunk)
                for t in range(2):
                    qs = slice(P * t, P * (t + 1))
                    for m, (o, w) in enumerate(((o_hi, wo_hi), (o_hi, wo_lo), (o_lo, wo_hi))):
                        last = pe.matmul(s_ps[:, buf, C * t:C * (t + 1)], o[:, qs], w[:], start=m == 0, stop=m == 2)
                last.then_inc(filled, 1)

            def tail(h, last):
                def chunk(key):
                    if last:
                        return at(h, TAIL_AT + {6: 0, 7: 1}[key[1]])
                    return at(h, TAIL_AT + TAIL_CHUNK[key])

                def buf(key):
                    return (TAIL_AT + ({6: 0, 7: 1}[key[1]] if last else TAIL_CHUNK[key])) % 2

                def kv(kind, i):
                    project_kv(kind, i, h + 1, chunk((kind, i)), buf((kind, i)))

                if not last:
                    pe.wait_ge(kv_w, h + 2)
                    kv("K", 0)
                    kv("K", 1)
                    pe.wait_ge(wq_w, h + 2)
                    pe.wait_ge(o_ready, h * G + (G - 1))
                    project_q(h * G + G, 0)
                project_out(h, h * G + (G - 2), chunk(("out", 6)), buf(("out", 6)))
                attend(h * G + (G - 1), 1, None if last else h * G + G)
                if not last:
                    kv("V", 0)
                    kv("V", 1)
                project_out(h, h * G + (G - 1), chunk(("out", 7)), buf(("out", 7)))
                if not last:
                    for kind, i in KV_ORDER[4:]:
                        kv(kind, i)

            pe.wait_ge(kv_w, 1)
            for n, (kind, i) in enumerate(KV_ORDER):
                project_kv(kind, i, 0, n, n % 2, first=n < 2)
                if n == 1:
                    pe.wait_ge(wq_w, 1)
                    project_q(0, 0)

            def head(h, last):
                scores(h * G, 0, at(h, 0))
                project_q(h * G + 1, 1)
                scores(h * G + 1, 1, at(h, 8))
                project_q(h * G + 2, 0)
                attend(h * G, 0, h * G + 2)

                def step(u, s, chunk, g):
                    chunk_parity[0] = u
                    scores(s, u, chunk)
                    if u == 0:
                        pe.wait_ge(o_ready, s - 1)
                        project_q(s + 1, 1)
                    project_out(h, s - 2, chunk + 8, u)
                    attend(s - 1, 1 - u, s + 1 if u == 0 else None)

                def middle_step(u, s, chunk, g):
                    chunk_parity[0] = u
                    scores(s, u, chunk)
                    pe.wait_ge(o_ready, s - 1)
                    project_q(s + 1, 1 - u)
                    project_out(h, s - 2, chunk + 8, u)
                    attend(s - 1, 1 - u, s + 1)

                with pe.Fori(0, G // 2 - 2) as p:
                    for u in range(2):
                        middle_step(u, h * G + p * 2 + (2 + u), h * PER_HEAD + p * 18 + (FIRST + 16 + 9 * u), None)
                for u in range(2):
                    step(u, h * G + (G - 2 + u), at(h, 16 + 9 * (G - 4 + u)), None)
                chunk_parity[0] = 0
                tail(h, last)

            heads(pe, head)

        @block.scalar
        def _(act):
            def round_weights(raw, hi, loaded, count, done):
                act.wait_ge(loaded, count)
                act.copy(hi[:], raw[:]).then_inc(done, 1)

            def round_kv(kind, i, chunk, buf):
                act.wait_ge(filled, chunk + 1)
                cols = slice(CHUNK * i, CHUNK * (i + 1))
                if kind == "K":
                    act.activation(k_hi[:, cols], s_ps[:, buf, :], ACT.Identity, bias=shift[:, 0:1]).then_inc(kv_rounded, 1)
                else:
                    act.copy(v_hi[:, cols], s_ps[:, buf, :]).then_inc(kv_rounded, 1)

            def round_q(step, par):
                act.wait_ge(q_done, step + 1)
                act.copy(q_hi[:, par, :], o_ps[:, 0:GQ]).then_inc(q_rounded, 1)

            def round_o(step):
                act.wait_ge(o_done, step + 1)
                act.copy(o_hi[:], o_ps[:, 0:GQ]).then_inc(o_rounded, 1)

            def exponent(t, i, par, step):
                if i == 0:
                    act.wait_ge(maxed, step * 2 + (t + 1))
                cols = slice(CHUNK * i, CHUNK * (i + 1))
                ins = act.activation(probs[:, par, t, cols], probs[:, par, t, cols], ACT.Exp,
                                     bias=neg_max[:, par, t:t + 1], accum_out=chunk_sum[:, par, t, i:i + 1])
                if i == 3:
                    ins.then_inc(exped, 1)

            def round_turned(step, exp_step=None, exp_par=None):
                for c in range(T_CHUNKS):
                    act.wait_ge(turned, step * T_CHUNKS + (c + 1))
                    if c >= 3:
                        act.wait_ge(weighed, step * (T_CHUNKS - 1) + (c - 2))
                    act.copy(pt_hi[:, c % 3, :], t_ps[:, c % 3, :]).then_inc(t_rounded, 1)
                    if exp_step is not None and c % 3 == 2 and c < 12:
                        exponent(1, c // 3, exp_par, exp_step)

            round_weights(kv_raw, kv_hi, kv_loaded, 96, kv_w_hi)
            round_weights(wq_raw, wq_hi, wq_loaded, 32, wq_w_hi)
            act.wait_ge(shifted, 1)
            for n, (kind, i) in enumerate(KV_ORDER):
                round_kv(kind, i, n, n % 2)
                if n == 1:
                    round_q(0, 0)

            def head(h, last):
                for i in range(4):
                    exponent(0, i, 0, h * G)
                round_q(h * G + 1, 1)
                for i in range(4):
                    exponent(1, i, 0, h * G)
                for i in range(4):
                    exponent(0, i, 1, h * G + 1)
                round_q(h * G + 2, 0)
                round_weights(wo_raw, wo_hi, wo_loaded, h * 16 + 16, wo_w_hi)
                if not last:
                    round_weights(kv_raw, kv_hi, kv_loaded, h * 96 + 192, kv_w_hi)
                round_turned(h * G, h * G + 1, 1)

                def step(u, s, q):
                    round_o(s - 2)
                    for i in range(4):
                        exponent(0, i, u, s)
                    if q:
                        round_q(s + 1, 1 - u)
                    round_turned(s - 1, s, u)

                with act.Fori(0, G // 2 - 2) as p:
                    for u in range(2):
                        step(u, h * G + p * 2 + (2 + u), True)
                for u in range(2):
                    step(u, h * G + (G - 2 + u), u == 0)

                round_o(h * G + (G - 2))
                if not last:
                    round_weights(wq_raw, wq_hi, wq_loaded, h * 32 + 64, wq_w_hi)
                    act.wait_ge(shifted, h + 2)
                    for kind, i in KV_ORDER[:2]:
                        c = TAIL_AT + TAIL_CHUNK[kind, i]
                        round_kv(kind, i, at(h, c), c % 2)
                    round_q(h * G + G, 0)
                round_turned(h * G + (G - 1))
                round_o(h * G + (G - 1))
                if not last:
                    for kind, i in KV_ORDER[2:]:
                        c = TAIL_AT + TAIL_CHUNK[kind, i]
                        round_kv(kind, i, at(h, c), c % 2)

            heads(act, head)

        @block.vector
        def _(dve):
            def split_weights(raw, hi, lo, rounded, count, done):
                dve.wait_ge(rounded, count)
                dve.tensor_tensor(lo[:], raw[:], hi[:].bitcast(F32), ALU.subtract).then_inc(done, 1)

            def split_kv(kind, i, count, buf):
                dve.wait_ge(kv_rounded, count)
                cols = slice(CHUNK * i, CHUNK * (i + 1))
                if kind == "K":
                    dve.scalar_tensor_tensor(out=k_lo[:, cols], in0=s_ps[:, buf, :], scalar=shift[:, 0:1],
                                             in1=k_hi[:, cols].bitcast(F32), op0=ALU.add,
                                             op1=ALU.subtract).then_inc(freed, 1)
                else:
                    dve.tensor_tensor(v_lo[:, cols], s_ps[:, buf, :], v_hi[:, cols].bitcast(F32),
                                      ALU.subtract).then_inc(freed, 1)

            def split_q(step, par):
                dve.wait_ge(q_rounded, step + 1)
                dve.tensor_tensor(q_lo[:, par, :], o_ps[:, 0:GQ], q_hi[:, par, :].bitcast(F32),
                                  ALU.subtract).then_inc(q_ready, 1)

            def split_o(step):
                dve.wait_ge(o_rounded, step + 1)
                dve.tensor_tensor(o_lo[:], o_ps[:, 0:GQ], o_hi[:].bitcast(F32), ALU.subtract).then_inc(o_ready, 1)

            def move_scores(n, par, chunk, buf):
                t, i = n // 4, n % 4
                dve.wait_ge(filled, chunk + n + 1)
                dve.tensor_scalar(probs[:, par, t, CHUNK * i:CHUNK * (i + 1)], s_ps[:, buf, :], LOGIT, None,
                                  ALU.mult, ALU.max, accum_out=chunk_max[:, t, i:i + 1]).then_inc(freed, 1)
                if i == 3:
                    dve.wait_ge(freed, chunk + n + 1)
                    dve.tensor_reduce(neg_max[:, par, t:t + 1], chunk_max[:, t, :], AX.X, ALU.max,
                                      negate=True).then_inc(maxed, 1)

            def invert_sums(step, par):
                dve.wait_ge(exped, step * 2 + 2)
                dve.tensor_reduce(denom[:], chunk_sum[:, par, :, :], AX.X, ALU.add).then_inc(summed, 1)
                dve.wait_ge(summed, step + 1)
                dve.reciprocal(inv[:, par, :], denom[:]).then_inc(inv_ready, 1)

            def add_out(step, par, g, chunk, buf):
                dve.wait_ge(filled, chunk + 1)
                dve.wait_ge(inv_ready, step + 1)
                for t in range(2):
                    tile = x[:, bass.ds(g * 2 + t, 1), :].rearrange("p o c -> p (o c)")
                    last = dve.scalar_tensor_tensor(out=tile, in0=s_ps[:, buf, C * t:C * (t + 1)],
                                                    scalar=inv[:, par, t:t + 1], in1=tile, op0=ALU.mult, op1=ALU.add)
                last.then_inc(freed, 1)

            def split_turned(step):
                for c in range(T_CHUNKS):
                    dve.wait_ge(t_rounded, step * T_CHUNKS + (c + 1))
                    dve.tensor_tensor(pt_lo[:, c % 3, :], t_ps[:, c % 3, :], pt_hi[:, c % 3, :].bitcast(F32),
                                      ALU.subtract).then_inc(t_ready, 1)

            dve.tensor_copy(shift[:], k_shift[:, 0:1]).then_inc(shifted, 1)
            split_weights(kv_raw, kv_hi, kv_lo, kv_w_hi, 1, kv_w)
            split_weights(wq_raw, wq_hi, wq_lo, wq_w_hi, 1, wq_w)
            for n, (kind, i) in enumerate(KV_ORDER):
                split_kv(kind, i, n + 1, n % 2)
                if n == 1:
                    split_q(0, 0)

            def head(h, last):
                for n in range(8):
                    move_scores(n, 0, at(h, 0), n % 2)
                split_q(h * G + 1, 1)
                for n in range(8):
                    move_scores(n, 1, at(h, 8), n % 2)
                    if n == 1:
                        invert_sums(h * G, 0)
                split_q(h * G + 2, 0)
                split_weights(wo_raw, wo_hi, wo_lo, wo_w_hi, h + 1, wo_w)
                if not last:
                    split_weights(kv_raw, kv_hi, kv_lo, kv_w_hi, h + 2, kv_w)
                split_turned(h * G)

                def step(u, s, chunk, g, q):
                    for n in range(8):
                        move_scores(n, u, chunk, (n + u) % 2)
                        if n == 0:
                            split_o(s - 2)
                        if n == 1:
                            invert_sums(s - 1, 1 - u)
                    if q:
                        split_q(s + 1, 1 - u)
                    add_out(s - 2, u, g, chunk + 8, u)
                    split_turned(s - 1)

                with dve.Fori(0, G // 2 - 2) as p:
                    for u in range(2):
                        step(u, h * G + p * 2 + (2 + u), h * PER_HEAD + p * 18 + (FIRST + 16 + 9 * u), p * 2 + u, True)
                for u in range(2):
                    step(u, h * G + (G - 2 + u), at(h, 16 + 9 * (G - 4 + u)), G - 4 + u, u == 0)

                split_o(h * G + (G - 2))
                invert_sums(h * G + (G - 1), 1)
                if not last:
                    dve.tensor_copy(shift[:], k_shift[:, bass.ds(h + 1, 1)]).then_inc(shifted, 1)
                    split_weights(wq_raw, wq_hi, wq_lo, wq_w_hi, h + 2, wq_w)
                    dve.wait_ge(shifted, h + 2)
                    for n, (kind, i) in enumerate(KV_ORDER[:2]):
                        split_kv(kind, i, h * 8 + (9 + n), (TAIL_AT + TAIL_CHUNK[kind, i]) % 2)
                    split_q(h * G + G, 0)
                c = TAIL_AT + (0 if last else TAIL_CHUNK["out", 6])
                add_out(h * G + (G - 2), 0, G - 2, at(h, c), c % 2)
                split_turned(h * G + (G - 1))
                split_o(h * G + (G - 1))
                if not last:
                    for n, (kind, i) in enumerate(KV_ORDER[2:4]):
                        split_kv(kind, i, h * 8 + (11 + n), (TAIL_AT + TAIL_CHUNK[kind, i]) % 2)
                c = TAIL_AT + (1 if last else TAIL_CHUNK["out", 7])
                add_out(h * G + (G - 1), 1, G - 1, at(h, c), c % 2)
                if not last:
                    for n, (kind, i) in enumerate(KV_ORDER[4:]):
                        split_kv(kind, i, h * 8 + (13 + n), (TAIL_AT + TAIL_CHUNK[kind, i]) % 2)

            heads(dve, head)
            dve.wait_ge(freed, FIRST + (XH - 1) * PER_HEAD + TAIL_AT + 2)


def channel_mix(nc, a, x, ident):
    with ExitStack() as ctx:
        def sb(name, shape, dt=F32):
            return ctx.enter_context(nc.sbuf_tensor(name, shape, dt))

        def sem(name):
            return ctx.enter_context(nc.semaphore(name))

        y = sb("y3", [P, NT, C])
        parts, mv = sb("parts3", [P, NT, 6]), sb("mv3", [P, NT, 2])
        var_eps, root = sb("var_eps3", [P, NT]), sb("root3", [P, NT])
        rstd, tmp = sb("rstd3", [P, NT]), sb("tmp3", [P, NT])
        w_raw = sb("fw_raw", [P, 3, CH, C])
        w_hi, w_lo = sb("fw_hi", [P, 3, CH, C], F32R), sb("fw_lo", [P, 3, CH, C], F32R)
        mu, nu = sb("mu", [P, 2, CH]), sb("nu", [P, 2, CH])
        yt = sb("yt", [P, CH, B, N + 1])
        part = sb("mix_part", [P, 2, N])
        full = sb("mix_full", [P, 4, N])
        mix_hi, mix_lo = sb("mix_hi", [P, 2, CH, T], F32R), sb("mix_lo", [P, 2, CH, T], F32R)
        relu, square = sb("relu", [P, 2, N]), sb("square", [P, 2, N])
        act_hi, act_lo = sb("act_hi", [P, CH, T], F32R), sb("act_lo", [P, CH, T], F32R)
        gate, gated = sb("gate", [P, 2, C]), sb("gated", [P, 2, C])
        banks = ctx.enter_context(nc.psum_tensor("banks3", [P, 8, 512], F32))

        loaded = sem("loaded3")
        var_ready, root_ready, y_ready = sem("var_ready3"), sem("root_ready3"), sem("y_ready3")
        dve_self, padded, nu_ready = sem("dve_self3"), sem("padded"), sem("nu_ready")
        w_hi_ready, w_ready = sem("fw_hi_ready"), sem("fw_ready")
        turned, yt_ready = sem("turned3"), sem("yt_ready")
        mixed, mix_rounded, mix_ready = sem("mixed"), sem("mix_rounded"), sem("mix_ready")
        k_done, relu_done, squared, act_rounded, act_ready = (sem("k_done"), sem("relu_done"), sem("squared"),
                                                              sem("act_rounded"), sem("act_ready"))
        rv_done, gate_ready, gated_ready, added = sem("rv_done"), sem("gate_ready"), sem("gated_ready"), sem("added3")
        block = ctx.enter_context(nc.Block())
        PIECES = [(b, h) for b in range(B) for h in range(CH)]

        @block.sync
        def _(sp):
            for n, name in enumerate(("W_rT", "W_kT", "W_vT")):
                sp.dma_start(w_raw[:, n, :, :], a[name].rearrange("(h p) o -> p h o", p=P)).then_inc(loaded, 16)
            with nc.allow_non_contiguous_dma(reason="a few per-channel vectors"):
                for n, name in enumerate(("mu_r", "mu_k")):
                    sp.dma_start(mu[:, n, :], a[name].rearrange("(h p) -> p h", p=P)).then_inc(loaded, 16)

        @block.gpsimd
        def _(pool):
            pool.memset(yt[:, :, :, 0:1], 0.0).then_inc(padded, 1)

        @block.vector
        def _(dve):
            chain = Chain(dve, dve_self)
            row_moments(dve, chain, x, parts, mv)
            inverse_root_seed(dve, chain, mv, var_eps, var_ready)
            dve.wait_ge(loaded, 80)
            dve.tensor_scalar(nu[:], mu[:], -1.0, 1.0, ALU.mult, ALU.add).then_inc(nu_ready, 1)
            for n in range(3):
                dve.wait_ge(w_hi_ready, n + 1)
                dve.tensor_tensor(flat(w_lo[:, n]), flat(w_raw[:, n]), flat(w_hi[:, n]).bitcast(F32),
                                  ALU.subtract).then_inc(w_ready, 1)
            dve.wait_ge(root_ready, 1)
            inverse_root(dve, chain, var_eps, root, rstd, tmp)
            for t in range(NT):
                dve.tensor_scalar(y[:, t, :], x[:, t, :], mv[:, t, 0:1], rstd[:, t:t + 1],
                                  ALU.subtract, ALU.mult).then_inc(y_ready, 1)
            dve.wait_ge(nu_ready, 1)
            dve.wait_ge(padded, 1)

            def mix_lo_of(n):
                b, h, m = n // 4, n // 2 % 2, n % 2
                dve.wait_ge(mix_rounded, n + 1)
                cols = slice(N * b, N * (b + 1))
                dve.tensor_tensor(mix_lo[:, m, h, cols], full[:, n % 4, :], mix_hi[:, m, h, cols].bitcast(F32),
                                  ALU.subtract).then_inc(mix_ready, 1)

            pieces = 2 * len(PIECES)
            for n in range(pieces + 2):
                if n < pieces:
                    (b, h), m = PIECES[n // 2], n % 2
                    dve.wait_ge(yt_ready, n // 2 + 1)
                    chain(dve.tensor_scalar(part[:, m, :], yt[:, h, b, 1:N + 1], mu[:, m, h:h + 1], None, ALU.mult))
                    chain.wait()
                    if n >= 4:
                        dve.wait_ge(mix_ready, n - 3)
                    dve.scalar_tensor_tensor(out=full[:, n % 4, :], in0=yt[:, h, b, 0:N], scalar=nu[:, m, h:h + 1],
                                             in1=part[:, m, :], op0=ALU.mult, op1=ALU.add).then_inc(mixed, 1)
                if n >= 2:
                    mix_lo_of(n - 2)
            for n in range(len(PIECES)):
                b, h = PIECES[n]
                cols = slice(N * b, N * (b + 1))
                dve.wait_ge(relu_done, n + 1)
                dve.tensor_tensor(square[:, n % 2, :], relu[:, n % 2, :], relu[:, n % 2, :], ALU.mult).then_inc(squared, 1)
                dve.wait_ge(act_rounded, n + 1)
                dve.tensor_tensor(act_lo[:, h, cols], square[:, n % 2, :], act_hi[:, h, cols].bitcast(F32),
                                  ALU.subtract).then_inc(act_ready, 1)
            for t in range(NT):
                dve.wait_ge(gate_ready, t + 1)
                if t >= 2:
                    dve.wait_ge(added, t - 1)
                dve.tensor_tensor(gated[:, t % 2, :], gate[:, t % 2, :], banks[:, t % 4, C:2 * C],
                                  ALU.mult).then_inc(gated_ready, 1)
                dve.wait_ge(gated_ready, t + 1)
                dve.tensor_tensor(x[:, t, :], x[:, t, :], gated[:, t % 2, :], ALU.add).then_inc(added, 1)

        @block.scalar
        def _(act):
            act.wait_ge(var_ready, 1)
            act.activation(root[:], var_eps[:], ACT.Sqrt).then_inc(root_ready, 1)
            act.wait_ge(loaded, 80)
            for n in range(3):
                act.copy(flat(w_hi[:, n]), flat(w_raw[:, n])).then_inc(w_hi_ready, 1)
            for n in range(len(PIECES) + 1):
                if n < len(PIECES):
                    b, h = PIECES[n]
                    act.wait_ge(turned, n + 1)
                    act.copy(yt[:, h, b, 1:N + 1], banks[:, n % 4, :]).then_inc(yt_ready, 1)
                if n >= 1:
                    b, h = PIECES[n - 1]
                    for m in range(2):
                        act.wait_ge(mixed, 2 * n - 1 + m)
                        act.copy(mix_hi[:, m, h, N * b:N * (b + 1)], full[:, (2 * n - 2 + m) % 4, :]).then_inc(mix_rounded, 1)
            for n in range(len(PIECES)):
                b, h = PIECES[n]
                act.wait_ge(k_done, n + 1)
                if n >= 2:
                    act.wait_ge(squared, n - 1)
                act.activation(relu[:, n % 2, :], banks[:, 4 + n % 4, :], ACT.Relu).then_inc(relu_done, 1)
                act.wait_ge(squared, n + 1)
                act.copy(act_hi[:, h, N * b:N * (b + 1)], square[:, n % 2, :]).then_inc(act_rounded, 1)
            for t in range(NT):
                act.wait_ge(rv_done, t + 1)
                if t >= 2:
                    act.wait_ge(gated_ready, t - 1)
                act.activation(gate[:, t % 2, :], banks[:, t % 4, 0:C], ACT.Sigmoid).then_inc(gate_ready, 1)

        @block.tensor
        def _(pe):
            for n, (b, h) in enumerate(PIECES):
                pe.wait_ge(y_ready, QI * (b + 1))
                if n >= 4:
                    pe.wait_ge(yt_ready, n - 3)
                for t in range(QI):
                    last = pe.transpose(banks[:, n % 4, P * t:P * (t + 1)], y[:, QI * b + t, P * h:P * (h + 1)], ident[:])
                last.then_inc(turned, 1)
            pe.wait_ge(w_ready, 3)
            for n, (b, oh) in enumerate(PIECES):
                pe.wait_ge(mix_ready, 4 * (b + 1))
                if n >= 4:
                    pe.wait_ge(relu_done, n - 3)
                passes = [(ws, zs, h) for h in range(CH) for ws, zs in ((w_hi, mix_hi), (w_hi, mix_lo), (w_lo, mix_hi))]
                for i, (ws, zs, h) in enumerate(passes):
                    last = pe.matmul(banks[:, 4 + n % 4, :], ws[:, 1, h, P * oh:P * (oh + 1)],
                                     zs[:, 1, h, N * b:N * (b + 1)], start=i == 0, stop=i == len(passes) - 1)
                last.then_inc(k_done, 1)
            for t in range(NT):
                pe.wait_ge(act_ready, CH * (t // QI + 1))
                if t >= 4:
                    pe.wait_ge(added, t - 3)
                rows = slice(P * t, P * (t + 1))
                for c0, w, hi, lo in ((0, 0, mix_hi[:, 0], mix_lo[:, 0]), (C, 2, act_hi, act_lo)):
                    passes = [(zs, ws, h) for h in range(CH) for zs, ws in ((hi, w_hi), (hi, w_lo), (lo, w_hi))]
                    for i, (zs, ws, h) in enumerate(passes):
                        last = pe.matmul(banks[:, t % 4, c0:c0 + C], zs[:, h, rows], ws[:, w, h, :],
                                         start=i == 0, stop=i == len(passes) - 1)
                last.then_inc(rv_done, 1)




def interpolation():
    pos = np.arange(N, dtype=np.float32) * np.float32((BIAS_S - 1) / (N - 1))
    i0 = np.floor(pos).astype(np.int32)
    i1 = np.minimum(i0 + 1, BIAS_S - 1)
    frac = pos - i0.astype(np.float32)
    m = np.zeros((N, BIAS_S), np.float32)
    np.add.at(m, (np.arange(N), i0), np.float32(1.0) - frac)
    np.add.at(m, (np.arange(N), i1), frac)
    m[-1] = 0.0
    return np.ascontiguousarray(m.T)


def kernel(**inputs):
    import concourse.bacc as bacc
    from concourse.bass_utils import run_bass_kernel_spmd

    def arr(name):
        return np.asarray(inputs[name])

    arrays = {
        "x": arr("x").reshape(T, C),
        "ctxT": arr("ctx_768").reshape(KEYS, CD).T,
        "WqT": arr("L0_attn_Wq").T, "WkT": arr("L0_attn_Wk").T, "WvT": arr("L0_attn_Wv").T, "WoT": arr("L0_attn_Wo").T,
        "bq": arr("L0_attn_bq"), "bk": arr("L0_attn_bk"), "bv": arr("L0_attn_bv"), "bo": arr("L0_attn_bo"),
        "gamma": arr("L0_attn_gamma"), "beta": arr("L0_attn_beta"), "rel_bias": arr("L0_attn_rel_bias"),
        "XWq": arr("L0_xattn_Wq"), "XWk": arr("L0_xattn_Wk"), "XWv": arr("L0_xattn_Wv"),
        "XWout": arr("L0_xattn_Wout"), "Xbout": arr("L0_xattn_bout"),
        "W_rT": arr("L0_ffn_W_r").T, "W_kT": arr("L0_ffn_W_k").T, "W_vT": arr("L0_ffn_W_v").T,
        "mu_r": arr("L0_ffn_mu_r"), "mu_k": arr("L0_ffn_mu_k"),
        "identity": np.eye(P, dtype=np.float32),
        "causal": np.triu(np.full((P, P), MASKED, np.float32), 1),
        "interp": interpolation(),
    }
    nc = bacc.Bacc("TRN2", target_bir_lowering=False, num_devices=1)
    feed, aps = {}, {}
    for name, value in arrays.items():
        value = np.ascontiguousarray(value)
        feed[f"in_{name}"] = value
        aps[name] = nc.dram_tensor(f"in_{name}", value.shape, mybir.dt.from_np(value.dtype), kind="ExternalInput").ap()
    out = nc.dram_tensor("out_x", (T, C), F32, kind="ExternalOutput").ap()
    decoder_layer(nc, aps, out)
    result = run_bass_kernel_spmd(nc, [feed], core_ids=[0])
    return result.results[0]["out_x"].reshape(B, N, C)
```

```python
from contextlib import ExitStack

import numpy as np

import concourse.bass as bass
from concourse import mybir

ALU = mybir.AluOpType
ACT = mybir.ActivationFunctionType
AX = mybir.AxisListType
F32 = mybir.dt.float32
F32R = mybir.dt.float32r

P = 128
B, N, C = 4, 512, 256
T = B * N
NT = T // P
CH = C // P
EPS = 1e-5

SH, SD = 16, 16
BIAS_S = 32
QI = N // P
STACK = 3 * SD
REL_STACK = 3 * BIAS_S
SLOT_ROWS = 2 * SD
MASKED = -1e30

XH, XD = 8, 128
CD, M = 192, 1024
KEYS = B * M
TAIL = CD - P
LOGIT = 1.5 * XD ** -0.5
G = 8
GQ = T // G
BLK = 512
NB = KEYS // BLK
CHUNK = 1024


def flat(ap):
    return ap.rearrange("p a b -> p (a b)")


def decoder_layer(nc, a, out):
    with ExitStack() as ctx:
        x = ctx.enter_context(nc.sbuf_tensor("x", [P, NT, C], F32))
        ident = ctx.enter_context(nc.sbuf_tensor("ident", [P, P], F32))
        ctx_sum = ctx.enter_context(nc.sbuf_tensor("ctx_sum", [P, 2], F32))
        q_split = nc.dram_tensor("q_split", (2, C, T), F32).ap()
        k_split = nc.dram_tensor("k_split", (2, C, T), F32).ap()
        x2_split = nc.dram_tensor("x2_split", (G, P, 2, CH, GQ), F32).ap()
        ctx_split = nc.dram_tensor("ctx_split", (NB, P, 3, BLK), F32).ap()
        with ExitStack() as keep:
            v_split = keep.enter_context(nc.sbuf_tensor("v_split", [P, NT, SH * SLOT_ROWS], F32R))
            self_projections(nc, a, x, ident, v_split, q_split, k_split)
            attn_t = keep.enter_context(nc.sbuf_tensor("attn_t", [2 * SLOT_ROWS, SH // 2 * T], F32))
            exp_sums = keep.enter_context(nc.sbuf_tensor("exp_sums", [P, SH * NT], F32))
            self_attention(nc, a, ident, v_split, attn_t, exp_sums, q_split, k_split, ctx_split, ctx_sum)
            self_output(nc, a, x, ident, attn_t, exp_sums)
        k_shift = ctx.enter_context(nc.sbuf_tensor("k_shift", [P, XH], F32))
        cross_prepare(nc, a, x, ident, x2_split, ctx_sum, k_shift)
        cross_attention(nc, a, x, ident, x2_split, ctx_split, k_shift)
        channel_mix(nc, a, x, ident)
        store_output(nc, x, out)


def store_output(nc, x, out):
    with ExitStack() as ctx:
        stored = ctx.enter_context(nc.semaphore("stored"))
        block = ctx.enter_context(nc.Block())

        @block.sync
        def _(sp):
            sp.dma_start(out.rearrange("(t p) c -> p t c", p=P), x[:]).then_inc(stored, 16)
            sp.wait_ge(stored, 16)


class Chain:

    def __init__(self, eng, sem):
        self.eng, self.sem, self.n = eng, sem, 0

    def __call__(self, ins):
        self.n += 1
        ins.then_inc(self.sem, 1)

    def wait(self):
        self.eng.wait_ge(self.sem, self.n)


def row_moments(dve, chain, src, parts, mv):
    for t in range(NT):
        chain(dve.bn_stats(parts[:, t, :], src[:, t, :]))
    chain.wait()
    for t in range(NT):
        chain(dve.bn_aggr(mv[:, t, :], parts[:, t, :]))
    chain.wait()


def inverse_root_seed(dve, chain, mv, var_eps, var_ready):
    dve.tensor_scalar(var_eps[:], mv[:, :, 1], EPS, None, ALU.add).then_inc(var_ready, 1)


def inverse_root(dve, chain, var_eps, root, rstd, tmp):
    chain(dve.reciprocal(rstd[:], root[:]))
    chain.wait()
    chain(dve.tensor_tensor(tmp[:], rstd[:], rstd[:], ALU.mult))
    chain.wait()
    chain(dve.tensor_tensor(tmp[:], tmp[:], var_eps[:], ALU.mult))
    chain.wait()
    chain(dve.tensor_scalar(tmp[:], tmp[:], -0.5, 1.5, ALU.mult, ALU.add))
    chain.wait()
    chain(dve.tensor_tensor(rstd[:], rstd[:], tmp[:], ALU.mult))
    chain.wait()


def self_projections(nc, a, x, ident, v_split, q_split, k_split):
    with ExitStack() as ctx:
        def sb(name, shape, dt=F32):
            return ctx.enter_context(nc.sbuf_tensor(name, shape, dt))

        def sem(name):
            return ctx.enter_context(nc.semaphore(name))

        y = sb("y", [P, NT, C])
        z_full = sb("z_full", [P, 2, 512])
        z_hi = sb("z_hi", [P, CH, T], F32R)
        z_lo = sb("z_lo", [P, CH, T], F32R)
        w_raw = sb("w_raw", [P, 3, CH, C])
        w_hi = sb("w_hi", [P, 3, CH, C], F32R)
        w_lo = sb("w_lo", [P, 3, CH, C], F32R)
        v_full = sb("v_full", [P, 2, C])
        stage_hi = sb("stage_hi", [P, 2, T], F32R)
        stage_lo = sb("stage_lo", [P, 2, T], F32R)
        gamma, beta = sb("gamma", [P, CH]), sb("beta", [P, CH])
        bqk = sb("bqk", [P, 2, CH])
        bqk_scaled = sb("bqk_scaled", [P, 2, CH])
        bv = sb("bv", [P, C])
        parts, mv = sb("parts", [P, NT, 6]), sb("mv", [P, NT, 2])
        mv2 = sb("mv2", [P, NT, 2])
        var_eps, root = sb("var_eps", [P, NT]), sb("root", [P, NT])
        rstd, tmp = sb("rstd", [P, NT]), sb("tmp", [P, NT])
        banks = ctx.enter_context(nc.psum_tensor("banks", [P, 8, 512], F32))

        x_loaded, w_loaded, small_loaded = sem("x_loaded"), sem("w_loaded"), sem("small_loaded")
        var_ready, root_ready, z_ready = sem("var_ready"), sem("root_ready"), sem("z_ready")
        dve_self = sem("dve_self")
        w_hi_ready, w_lo_ready = sem("w_hi_ready"), sem("w_lo_ready")
        turned, z_hi_ready, z_lo_ready = sem("turned"), sem("z_hi_ready"), sem("z_lo_ready")
        projected, stage_hi_ready, stage_lo_ready = sem("projected"), sem("stage_hi_ready"), sem("stage_lo_ready")
        stack_stored = [sem("q_stack_stored"), sem("k_stack_stored")]
        v_done, v_ready, v_hi_ready, v_lo_ready = sem("v_done"), sem("v_ready"), sem("v_hi_ready"), sem("v_lo_ready")
        block = ctx.enter_context(nc.Block())

        TB = T // 512
        QK_UNITS = [(w, oh, tb) for oh in range(CH) for w in range(2) for tb in range(TB)]

        def v_parts(t):
            heads = v_split[:, t, :].rearrange("p (h r) -> p h r", r=SLOT_ROWS)
            return heads[:, :, 0:SD], heads[:, :, SD:]

        @block.sync
        def _(sp):
            xs = a["x"].rearrange("(t p) c -> p t c", p=P)
            for t in range(0, NT, 4):
                sp.dma_start(x[:, t:t + 4, :], xs[:, t:t + 4, :]).then_inc(x_loaded, 16)
            for n, name in enumerate(("WqT", "WkT", "WvT")):
                sp.dma_start(w_raw[:, n, :, :], a[name].rearrange("(h p) o -> p h o", p=P)).then_inc(w_loaded, 16)
            with nc.allow_non_contiguous_dma(reason="a few per-channel vectors"):
                sp.dma_start(gamma[:], a["gamma"].rearrange("(h p) -> p h", p=P)).then_inc(small_loaded, 16)
                sp.dma_start(beta[:], a["beta"].rearrange("(h p) -> p h", p=P)).then_inc(small_loaded, 16)
                sp.dma_start(bqk[:, 0, :], a["bq"].rearrange("(h p) -> p h", p=P)).then_inc(small_loaded, 16)
                sp.dma_start(bqk[:, 1, :], a["bk"].rearrange("(h p) -> p h", p=P)).then_inc(small_loaded, 16)
            sp.dma_start(bv[:], a["bv"].rearrange("(a c) -> a c", a=1).to_broadcast([P, C])).then_inc(small_loaded, 16)
            sp.dma_start(ident[:], a["identity"]).then_inc(small_loaded, 16)
            n = 0
            for oh in range(CH):
                rows = slice(P * oh, P * (oh + 1))
                for w, dest in enumerate((q_split, k_split)):
                    n += TB
                    sp.wait_ge(stage_hi_ready, n)
                    sp.dma_start(dest[0, rows], stage_hi[:, w, :].bitcast(F32)).then_inc(stack_stored[w], 16)
                    sp.wait_ge(stage_lo_ready, n)
                    sp.dma_start(dest[1, rows], stage_lo[:, w, :].bitcast(F32)).then_inc(stack_stored[w], 16)
            for w in range(2):
                sp.wait_ge(stack_stored[w], 16 * 2 * CH)

        @block.vector
        def _(dve):
            chain = Chain(dve, dve_self)
            dve.wait_ge(x_loaded, 16 * 4)
            row_moments(dve, chain, x, parts, mv)
            inverse_root_seed(dve, chain, mv, var_eps, var_ready)
            dve.wait_ge(root_ready, 1)
            inverse_root(dve, chain, var_eps, root, rstd, tmp)
            for t in range(NT):
                chain(dve.tensor_scalar(y[:, t, :], x[:, t, :], mv[:, t, 0:1], rstd[:, t:t + 1],
                                        ALU.subtract, ALU.mult))
            chain.wait()
            row_moments(dve, chain, y, parts, mv2)
            inverse_root_seed(dve, chain, mv2, var_eps, var_ready)
            for n in range(3):
                dve.wait_ge(w_hi_ready, n + 1)
                dve.scalar_tensor_tensor(out=flat(w_lo[:, n]), in0=flat(w_raw[:, n]), scalar=SD ** -0.5 if n == 0 else 1.0,
                                         in1=flat(w_hi[:, n]).bitcast(F32), op0=ALU.mult,
                                         op1=ALU.subtract).then_inc(w_lo_ready, 1)
            dve.wait_ge(small_loaded, 16 * 6)
            dve.tensor_scalar(bqk_scaled[:, 0, :], bqk[:, 0, :], SD ** -0.5, None, ALU.mult)
            chain(dve.tensor_copy(bqk_scaled[:, 1, :], bqk[:, 1, :]))
            dve.wait_ge(root_ready, 2)
            inverse_root(dve, chain, var_eps, root, rstd, tmp)
            for t in range(NT):
                dve.tensor_scalar(y[:, t, :], y[:, t, :], mv2[:, t, 0:1], rstd[:, t:t + 1],
                                  ALU.subtract, ALU.mult).then_inc(z_ready, 1)
            for n in range(TB * CH):
                tb, h = n // CH, n % CH
                dve.wait_ge(turned, n + 1)
                dve.wait_ge(z_hi_ready, n + 1)
                if n >= 2:
                    dve.wait_ge(z_lo_ready, n - 1)
                chain(dve.tensor_scalar(z_full[:, n % 2, :], banks[:, n % 4, :], gamma[:, h:h + 1], beta[:, h:h + 1],
                                        ALU.mult, ALU.add))
                chain.wait()
                dve.tensor_tensor(z_lo[:, h, 512 * tb:512 * (tb + 1)], z_full[:, n % 2, :],
                                  z_hi[:, h, 512 * tb:512 * (tb + 1)].bitcast(F32), ALU.subtract).then_inc(z_lo_ready, 1)
            for n, (w, oh, tb) in enumerate(QK_UNITS):
                dve.wait_ge(stage_hi_ready, n + 1)
                if n >= 2 * TB and tb == 0:
                    dve.wait_ge(stack_stored[w], 16 * 2)
                dve.scalar_tensor_tensor(out=stage_lo[:, w, 512 * tb:512 * (tb + 1)], in0=banks[:, 4 + n % 4, :],
                                         scalar=bqk_scaled[:, w, oh:oh + 1],
                                         in1=stage_hi[:, w, 512 * tb:512 * (tb + 1)].bitcast(F32),
                                         op0=ALU.add, op1=ALU.subtract).then_inc(stage_lo_ready, 1)
            for t in range(NT + 1):
                if t < NT:
                    dve.wait_ge(v_done, t + 1)
                    if t >= 2:
                        dve.wait_ge(v_lo_ready, t - 1)
                    dve.tensor_tensor(v_full[:, t % 2, :], banks[:, t % 4, 0:C], bv[:], ALU.add).then_inc(v_ready, 1)
                if t >= 1:
                    dve.wait_ge(v_hi_ready, t)
                    hi, lo = v_parts(t - 1)
                    dve.tensor_tensor(lo, v_full[:, (t - 1) % 2, :].rearrange("p (h d) -> p h d", d=SD), hi.bitcast(F32),
                                      ALU.subtract).then_inc(v_lo_ready, 1)

        @block.scalar
        def _(act):
            act.wait_ge(var_ready, 1)
            act.activation(root[:], var_eps[:], ACT.Sqrt).then_inc(root_ready, 1)
            act.wait_ge(w_loaded, 16 * 3)
            for n in range(3):
                act.activation(flat(w_hi[:, n]), flat(w_raw[:, n]), ACT.Copy,
                               scale=SD ** -0.5 if n == 0 else 1.0).then_inc(w_hi_ready, 1)
            act.wait_ge(var_ready, 2)
            act.activation(root[:], var_eps[:], ACT.Sqrt).then_inc(root_ready, 1)
            act.wait_ge(small_loaded, 16 * 6)
            for n in range(TB * CH):
                tb, h = n // CH, n % CH
                act.wait_ge(turned, n + 1)
                act.activation(z_hi[:, h, 512 * tb:512 * (tb + 1)], banks[:, n % 4, :], ACT.Identity,
                               bias=beta[:, h:h + 1], scale=gamma[:, h:h + 1]).then_inc(z_hi_ready, 1)
            act.wait_ge(z_ready, 1)
            for n, (w, oh, tb) in enumerate(QK_UNITS):
                act.wait_ge(projected, n + 1)
                if n >= 2 * TB and tb == 0:
                    act.wait_ge(stack_stored[w], 16 * 2)
                act.activation(stage_hi[:, w, 512 * tb:512 * (tb + 1)], banks[:, 4 + n % 4, :], ACT.Identity,
                               bias=bqk_scaled[:, w, oh:oh + 1]).then_inc(stage_hi_ready, 1)
            for t in range(NT):
                act.wait_ge(v_ready, t + 1)
                act.copy(v_parts(t)[0], v_full[:, t % 2, :].rearrange("p (h d) -> p h d", d=SD)).then_inc(v_hi_ready, 1)

        @block.tensor
        def _(pe):
            pe.wait_ge(small_loaded, 16 * 6)
            for n in range(TB * CH):
                tb, h = n // CH, n % CH
                pe.wait_ge(z_ready, 4 * tb + 4)
                if n >= 4:
                    pe.wait_ge(z_lo_ready, n - 3)
                for t in range(4):
                    last = pe.transpose(banks[:, n % 4, P * t:P * (t + 1)], y[:, 4 * tb + t, P * h:P * (h + 1)], ident[:])
                last.then_inc(turned, 1)
            pe.wait_ge(z_lo_ready, TB * CH)
            pe.wait_ge(w_lo_ready, 3)
            for n, (w, oh, tb) in enumerate(QK_UNITS):
                if n >= 4:
                    pe.wait_ge(stage_lo_ready, n - 3)
                passes = [(ws, zs, h) for h in range(CH) for ws, zs in ((w_hi, z_hi), (w_hi, z_lo), (w_lo, z_hi))]
                for i, (ws, zs, h) in enumerate(passes):
                    last = pe.matmul(banks[:, 4 + n % 4, :], ws[:, w, h, P * oh:P * (oh + 1)],
                                     zs[:, h, 512 * tb:512 * (tb + 1)], start=i == 0, stop=i == len(passes) - 1)
                last.then_inc(projected, 1)
            for t in range(NT):
                if t >= 4:
                    pe.wait_ge(v_ready, t - 3)
                passes = [(ws, zs, h) for h in range(CH) for ws, zs in ((w_hi, z_hi), (w_lo, z_hi), (w_hi, z_lo))]
                for i, (ws, zs, h) in enumerate(passes):
                    last = pe.matmul(banks[:, t % 4, 0:C], zs[:, h, P * t:P * (t + 1)], ws[:, 2, h, :],
                                     start=i == 0, stop=i == len(passes) - 1)
                last.then_inc(v_done, 1)


UNITS = [[(3, 0)], [(0, 0), (2, P)], [(1, 0)]]


def self_attention(nc, a, ident, v_split, attn_t, exp_sums, q_split, k_split, ctx_split, ctx_sum):
    with ExitStack() as ctx:
        def sb(name, shape, dt=F32):
            return ctx.enter_context(nc.sbuf_tensor(name, shape, dt))

        def sem(name):
            return ctx.enter_context(nc.semaphore(name))

        def psum(name, shape):
            return ctx.enter_context(nc.psum_tensor(name, shape, F32))

        q_st = [sb(f"q_st{h}", [STACK, T], F32R) for h in range(2)]
        k_st = [sb(f"k_st{h}", [STACK, T], F32R) for h in range(2)]
        v_st = [sb(f"v_st{h}", [P, NT, SLOT_ROWS], F32R) for h in range(2)]
        rel_st = [sb(f"rel_st{h}", [BIAS_S, 3, BIAS_S]) for h in range(2)]
        interp = sb("interp", [BIAS_S, N])
        interp3 = sb("interp3", [REL_STACK, N])
        key_st = sb("key_st", [REL_STACK, N], F32R)
        key_hi = sb("key_hi", [REL_STACK, N], F32R)
        rows_hi = sb("rows_hi", [REL_STACK, N], F32R)
        rows_st = [sb(f"rows_st{h}", [REL_STACK, N], F32R) for h in range(2)]
        mask_raw, mask = sb("mask_raw", [P, P]), sb("mask", [P, P], F32R)
        ident_r = sb("ident_r", [P, P], F32R)
        probs = sb("probs", [P, 4, 512])
        pt_hi, pt_lo = sb("spt_hi", [P, 3, 512], F32R), sb("spt_lo", [P, 3, 512], F32R)
        ctx_in = sb("ctx_in", [P, 2, BLK])
        ctx_acc = sb("ctx_acc", [P, 2, BLK])
        ctx_out = sb("ctx_out", [P, 3, BLK], F32R)
        tail_hi = sb("tail_hi", [P, BLK], F32R)
        neg_max = sb("neg_max", [P, 3, QI])
        s_ps = psum("s_ps", [P, 3, 512])
        t_ps = psum("t_ps", [P, 2, 512])
        o_ps = psum("o_ps", [P, 2, 512])
        r_ps = psum("r_ps", [P, 512])

        const_loaded, const_hi, const_ready = sem("const_loaded"), sem("const_hi"), sem("const_ready")
        head_loaded = [sem(f"head_loaded{h}") for h in range(2)]
        v_loaded = [sem(f"v_loaded{h}") for h in range(2)]
        rel_done, rows_hi_ready, rows_ready = sem("rel_done"), sem("rows_hi_ready"), sem("rows_ready")
        scored, maxed, exped = sem("scored"), sem("maxed"), sem("exped")
        turned, pt_rounded, pt_ready = sem("turned"), sem("pt_rounded"), sem("pt_ready")
        item_done, item_free = sem("item_done"), sem("item_free")
        ctx_loaded, ctx_ready, ctx_stored, pool_self = sem("ctx_loaded"), sem("ctx_ready"), sem("ctx_stored"), sem("pool_self")
        block = ctx.enter_context(nc.Block())

        ITEMS = 2 * B
        PER = ITEMS * len(UNITS)
        HALF = PER // 2
        LOADS = 16 * 9
        PASSES = SH // 2

        def unit(n):
            return n // HALF % 2, n // len(UNITS) % B, UNITS[n % len(UNITS)]

        def passes(eng, prologue, body):
            prologue()
            with eng.Fori(0, PASSES - 1) as it:
                body(it, False)
            body(PASSES - 1, True)

        @block.sync
        def _(sp):
            sp.dma_start(interp[:], a["interp"]).then_inc(const_loaded, 16)
            for j in range(3):
                sp.dma_start(interp3[BIAS_S * j:BIAS_S * (j + 1), :], a["interp"]).then_inc(const_loaded, 16)
            sp.dma_start(mask_raw[:], a["causal"]).then_inc(const_loaded, 16)

            def load(slot, head, channel):
                for stack, split, parts in ((q_st, q_split, (0, 0, 1)), (k_st, k_split, (0, 1, 0))):
                    for j, part in enumerate(parts):
                        sp.dma_start(stack[slot][SD * j:SD * (j + 1), :].bitcast(F32),
                                     split[part, bass.ds(channel, SD), :]).then_inc(head_loaded[slot], 16)
                for j in range(3):
                    sp.dma_start(rel_st[slot][:, j, :], a["rel_bias"][bass.ds(head, 1)].rearrange("o i j -> (o i) j")).then_inc(head_loaded[slot], 16)

            def load_v(slot, col):
                sp.dma_start(v_st[slot][:].bitcast(F32), v_split[:, :, bass.ds(col, SLOT_ROWS)].bitcast(F32)).then_inc(v_loaded[slot], 16)

            for slot in range(2):
                load(slot, slot, SD * slot)
                load_v(slot, SLOT_ROWS * slot)
            with sp.Fori(0, PASSES - 1) as it:
                for slot in range(2):
                    head, channel, col = [sp.snap(it * (2 * w) + (2 + slot) * w) for w in (1, SD, SLOT_ROWS)]
                    scored_all, weighed_all = sp.snap(it * PER + HALF * (slot + 1)), sp.snap(it * ITEMS + B * (slot + 1))
                    sp.wait_ge(scored, scored_all)
                    load(slot, head, channel)
                    sp.wait_ge(item_done, weighed_all)
                    load_v(slot, col)

        @block.gpsimd
        def _(pool):
            chain = Chain(pool, pool_self)
            for b in range(NB):
                cols = slice(BLK * b, BLK * (b + 1))
                if b >= 1:
                    pool.wait_ge(ctx_ready, b)
                pool.dma_start(ctx_in[:, 0, :], a["ctxT"][0:P, cols]).then_inc(ctx_loaded, 16)
                for d in range(2):
                    pool.dma_start(ctx_in[TAIL * d:TAIL * (d + 1), 1, :], a["ctxT"][P:CD, cols]).then_inc(ctx_loaded, 16)
                if b >= 1:
                    pool.wait_ge(ctx_stored, 16 * b)
                pool.wait_ge(ctx_loaded, 48 * (b + 1))
                chain(pool.tensor_copy(ctx_out[:, 0, :], ctx_in[:, 0, :]))
                chain.wait()
                chain(pool.tensor_copy(ctx_out[0:TAIL, 2, :], ctx_in[0:TAIL, 1, :]))
                chain.wait()
                chain(pool.tensor_copy(tail_hi[TAIL:, :], ctx_in[TAIL:, 1, :]))
                chain.wait()
                if b == 0:
                    chain(pool.tensor_copy(ctx_acc[:], ctx_in[:]))
                else:
                    chain(pool.tensor_tensor(ctx_acc[:], ctx_acc[:], ctx_in[:], ALU.add))
                chain.wait()
                chain(pool.tensor_tensor(ctx_out[:, 1, :], ctx_in[:, 0, :], ctx_out[:, 0, :].bitcast(F32), ALU.subtract))
                chain.wait()
                pool.tensor_tensor(ctx_out[TAIL:, 2, :], ctx_in[TAIL:, 1, :], tail_hi[TAIL:, :].bitcast(F32),
                                   ALU.subtract).then_inc(ctx_ready, 1)
                pool.wait_ge(ctx_ready, b + 1)
                pool.dma_start(ctx_split[b], ctx_out[:].bitcast(F32)).then_inc(ctx_stored, 16)
            pool.wait_ge(ctx_stored, 16 * NB)

        @block.tensor
        def _(pe):
            def relative_rows(it, slot):
                pe.wait_ge(head_loaded[slot % 2], it * LOADS + (slot // 2 + 1) * LOADS)
                pe.matmul(r_ps[0:REL_STACK, :], rel_st[slot % 2][:].rearrange("i j c -> i (j c)"), interp[:],
                          start=True, stop=True).then_inc(rel_done, 1)

            def scores(it, n):
                slot, b, tiles = unit(n)
                if n % HALF == 0:
                    pe.wait_ge(rows_ready, it * 2 + (n // HALF + 1))
                if n >= 3:
                    pe.wait_ge(exped, it * PER + (n - 2))
                for i, c0 in tiles:
                    w = P * (i + 1)
                    q0 = N * b + P * i
                    pe.matmul(s_ps[:, n % 3, c0:c0 + w], rows_st[slot][:, P * i:P * (i + 1)], key_st[:, 0:w],
                              start=True, stop=False)
                    pe.matmul(s_ps[:, n % 3, c0:c0 + w], q_st[slot][:, q0:q0 + P], k_st[slot][:, N * b:N * b + w],
                              start=False, stop=False)
                    last = pe.matmul(s_ps[:, n % 3, c0 + w - P:c0 + w], ident_r[:], mask[:], start=False, stop=True)
                last.then_inc(scored, 1)

            def turn(it, n):
                pe.wait_ge(exped, it * PER + (n + 1))
                if n >= 2:
                    pe.wait_ge(pt_ready, it * PER + (n - 1))
                for i, c0 in unit(n)[2]:
                    for j in range(i + 1):
                        cols = slice(c0 + P * j, c0 + P * (j + 1))
                        last = pe.transpose(t_ps[:, n % 2, cols], probs[:, n % 4, cols], ident[:])
                last.then_inc(turned, 1)

            def weigh(it, n):
                slot, b, tiles = unit(n)
                item = n // len(UNITS)
                if n % HALF == 0:
                    pe.wait_ge(v_loaded[slot], it * 16 + 16)
                if n % len(UNITS) == 0:
                    pe.wait_ge(item_free, it * ITEMS + (item + 1))
                pe.wait_ge(pt_ready, it * PER + (n + 1))
                for i, c0 in tiles:
                    for j in range(i + 1):
                        queries, cols = slice(P * i, P * (i + 1)), slice(c0 + P * j, c0 + P * (j + 1))
                        for pt in (pt_hi, pt_lo):
                            last = pe.matmul(o_ps[0:SLOT_ROWS, item % 2, queries], v_st[slot][:, QI * b + j, :],
                                             pt[:, n % 3, cols], start=pt is pt_hi and j == 0, stop=pt is pt_lo and j == i)
                if n % len(UNITS) == len(UNITS) - 1:
                    last.then_inc(item_done, 1)

            def prologue():
                pe.wait_ge(const_ready, 1)
                relative_rows(0, 0)
                for n in range(3):
                    scores(0, n)
                for n in range(2):
                    scores(0, n + 3)
                    turn(0, n)

            def body(it, last):
                for n in range(PER):
                    if n == 3:
                        relative_rows(it, 1)
                    if n == HALF + 3 and not last:
                        relative_rows(it, 2)
                    if n + 5 < PER or not last:
                        scores(it, n + 5)
                    if n + 2 < PER or not last:
                        turn(it, n + 2)
                    weigh(it, n)

            passes(pe, prologue, body)

        @block.scalar
        def _(act):
            def relative_rows(it, slot):
                act.wait_ge(rel_done, it * 2 + (slot + 1))
                act.copy(rows_st[slot % 2][0:2 * BIAS_S, :], r_ps[0:2 * BIAS_S, :])
                act.copy(rows_hi[2 * BIAS_S:, :], r_ps[2 * BIAS_S:REL_STACK, :]).then_inc(rows_hi_ready, 1)

            def exponents(it, n):
                slot, b, tiles = unit(n)
                act.wait_ge(maxed, it * PER + (n + 1))
                if n >= 4:
                    act.wait_ge(turned, it * PER + (n - 3))
                for i, c0 in tiles:
                    w = P * (i + 1)
                    total = exp_sums[:, bass.ds(it * 2 * NT + (n // HALF * NT + QI * b + i), 1)]
                    last = act.activation(probs[:, n % 4, c0:c0 + w], s_ps[:, n % 3, c0:c0 + w], ACT.Exp,
                                          bias=neg_max[:, n % 3, i:i + 1], accum_out=total)
                last.then_inc(exped, 1)

            def round_turned(it, n):
                w = sum(P * (i + 1) for i, _ in unit(n)[2])
                act.wait_ge(turned, it * PER + (n + 1))
                act.copy(pt_hi[:, n % 3, 0:w], t_ps[:, n % 2, 0:w]).then_inc(pt_rounded, 1)

            def prologue():
                act.wait_ge(const_loaded, 16 * 5)
                act.copy(key_hi[:], interp3[:])
                act.copy(key_st[0:BIAS_S, :], interp3[0:BIAS_S, :])
                act.copy(key_st[2 * BIAS_S:, :], interp3[2 * BIAS_S:, :])
                act.copy(mask[:], mask_raw[:])
                act.copy(ident_r[:], ident[:]).then_inc(const_hi, 1)
                relative_rows(0, 0)
                for n in range(3):
                    exponents(0, n)
                for n in range(2):
                    round_turned(0, n)
                    exponents(0, n + 3)

            def body(it, last):
                for n in range(PER):
                    if n == 3:
                        relative_rows(it, 1)
                    if n == HALF + 3 and not last:
                        relative_rows(it, 2)
                    if n + 2 < PER or not last:
                        round_turned(it, n + 2)
                    if n + 5 < PER or not last:
                        exponents(it, n + 5)

            passes(act, prologue, body)

        @block.vector
        def _(dve):
            def relative_rows(it, slot):
                dve.wait_ge(rows_hi_ready, it * 2 + (slot + 1))
                dve.tensor_tensor(rows_st[slot % 2][2 * BIAS_S:, :], r_ps[2 * BIAS_S:REL_STACK, :],
                                  rows_hi[2 * BIAS_S:, :].bitcast(F32), ALU.subtract).then_inc(rows_ready, 1)

            def maxima(it, n):
                dve.wait_ge(scored, it * PER + (n + 1))
                for i, c0 in unit(n)[2]:
                    last = dve.tensor_reduce(neg_max[:, n % 3, i:i + 1], s_ps[:, n % 3, c0:c0 + P * (i + 1)],
                                             AX.X, ALU.max, negate=True)
                last.then_inc(maxed, 1)

            def rest_of_turned(it, n):
                w = sum(P * (i + 1) for i, _ in unit(n)[2])
                dve.wait_ge(pt_rounded, it * PER + (n + 1))
                dve.tensor_tensor(pt_lo[:, n % 3, 0:w], t_ps[:, n % 2, 0:w], pt_hi[:, n % 3, 0:w].bitcast(F32),
                                  ALU.subtract).then_inc(pt_ready, 1)

            def store_item(it, item):
                slot, b = item // B, item % B
                dve.wait_ge(item_done, it * ITEMS + (item + 1))
                dve.tensor_copy(attn_t[SLOT_ROWS * slot:SLOT_ROWS * (slot + 1), bass.ds(it * T + N * b, N)],
                                o_ps[0:SLOT_ROWS, item % 2, :]).then_inc(item_free, 1)

            def prologue():
                dve.wait_ge(const_hi, 1)
                dve.tensor_tensor(key_st[BIAS_S:2 * BIAS_S, 0:N // 2], interp3[BIAS_S:2 * BIAS_S, 0:N // 2],
                                  key_hi[BIAS_S:2 * BIAS_S, 0:N // 2].bitcast(F32), ALU.subtract).then_inc(item_free, 2)
                dve.tensor_tensor(key_st[BIAS_S:2 * BIAS_S, N // 2:], interp3[BIAS_S:2 * BIAS_S, N // 2:],
                                  key_hi[BIAS_S:2 * BIAS_S, N // 2:].bitcast(F32), ALU.subtract).then_inc(const_ready, 1)
                relative_rows(0, 0)
                for n in range(3):
                    maxima(0, n)
                for n in range(2):
                    maxima(0, n + 3)
                    rest_of_turned(0, n)

            def body(it, last):
                for n in range(PER):
                    if n == 3:
                        relative_rows(it, 1)
                    if n == HALF + 3 and not last:
                        relative_rows(it, 2)
                    if n + 5 < PER or not last:
                        maxima(it, n + 5)
                    if n + 2 < PER or not last:
                        rest_of_turned(it, n + 2)
                    if n % len(UNITS) == len(UNITS) - 1:
                        store_item(it, n // len(UNITS))

            passes(dve, prologue, body)
            dve.wait_ge(ctx_ready, NB)
            dve.tensor_reduce(ctx_sum[:, 0:1], ctx_acc[:, 0, :], AX.X, ALU.add)
            dve.tensor_reduce(ctx_sum[0:TAIL, 1:2], ctx_acc[0:TAIL, 1, :], AX.X, ALU.add)
            dve.wait_ge(item_free, PASSES * ITEMS + 2)


def self_output(nc, a, x, ident, attn_t, exp_sums):
    with ExitStack() as ctx:
        def sb(name, shape, dt=F32):
            return ctx.enter_context(nc.sbuf_tensor(name, shape, dt))

        def sem(name):
            return ctx.enter_context(nc.semaphore(name))

        w_raw = sb("wo_raw", [P, CH, C])
        w_hi, w_lo = sb("wo_hi", [P, CH, C], F32R), sb("wo_lo", [P, CH, C], F32R)
        bo = sb("bo", [P, C])
        inv_sums = sb("inv_sums", [P, SH, NT])
        total, attn = sb("total", [P, 2, C]), sb("attn", [P, 2, C])
        o_hi, o_lo = sb("so_hi", [P, 2, CH, P], F32R), sb("so_lo", [P, 2, CH, P], F32R)
        a_ps = ctx.enter_context(nc.psum_tensor("so_a", [P, 2, 512], F32))
        t_ps = ctx.enter_context(nc.psum_tensor("so_t", [P, 2, 512], F32))
        y_ps = ctx.enter_context(nc.psum_tensor("so_y", [P, 2, 512], F32))
        loaded, w_hi_ready, w_ready = sem("so_loaded"), sem("so_w_hi"), sem("so_w")
        summed = sem("so_summed")
        token_major, inverted, divided = sem("so_token_major"), sem("so_inverted"), sem("so_divided")
        turned, hi_ready, lo_ready = sem("so_turned"), sem("so_hi_ready"), sem("so_lo_ready")
        projected, biased, added = sem("so_projected"), sem("so_biased"), sem("so_added")
        block = ctx.enter_context(nc.Block())
        PAIR = 2 * SLOT_ROWS

        @block.sync
        def _(sp):
            sp.dma_start(w_raw[:], a["WoT"].rearrange("(h p) o -> p h o", p=P)).then_inc(loaded, 16)
            sp.dma_start(bo[:], a["bo"].rearrange("(a c) -> a c", a=1).to_broadcast([P, C])).then_inc(loaded, 16)

        @block.gpsimd
        def _(pool):
            pool.wait_ge(loaded, 32)
            for t in range(NT):
                pool.tensor_tensor(x[:, t, :], x[:, t, :], bo[:], ALU.add).then_inc(biased, 1)

        @block.scalar
        def _(act):
            act.wait_ge(loaded, 32)
            act.copy(flat(w_hi[:]), flat(w_raw[:])).then_inc(w_hi_ready, 1)
            for t in range(NT):
                act.wait_ge(turned, t + 1)
                if t >= 2:
                    act.wait_ge(projected, t - 1)
                act.copy(flat(o_hi[:, t % 2]), t_ps[:, t % 2, 0:C]).then_inc(hi_ready, 1)

        @block.vector
        def _(dve):
            dve.reciprocal(inv_sums[:].rearrange("p h t -> p (h t)"), exp_sums[:]).then_inc(inverted, 1)

            def divide(t):
                dve.wait_ge(token_major, t + 1)
                if t >= 2:
                    dve.wait_ge(turned, t - 1)
                parts = a_ps[:, t % 2, :].rearrange("p (h v d) -> p h d v", v=2, d=SD)
                halves = total[:, t % 2, :].rearrange("p (h d) -> p h d", d=SD)
                dve.tensor_reduce(halves, parts, AX.X, ALU.add).then_inc(summed, 1)
                dve.wait_ge(summed, t + 1)
                dve.tensor_tensor(attn[:, t % 2, :].rearrange("p (h d) -> p h d", d=SD), halves,
                                  inv_sums[:, :, t:t + 1].to_broadcast([P, SH, SD]), ALU.mult).then_inc(divided, 1)

            dve.wait_ge(inverted, 1)
            divide(0)
            dve.wait_ge(w_hi_ready, 1)
            dve.tensor_tensor(flat(w_lo[:]), flat(w_raw[:]), flat(w_hi[:]).bitcast(F32), ALU.subtract).then_inc(w_ready, 1)
            divide(1)
            for t in range(NT + 1):
                if t < NT:
                    dve.wait_ge(hi_ready, t + 1)
                    if t >= 2:
                        dve.wait_ge(projected, t - 1)
                    dve.tensor_tensor(flat(o_lo[:, t % 2]), t_ps[:, t % 2, 0:C], flat(o_hi[:, t % 2]).bitcast(F32),
                                      ALU.subtract).then_inc(lo_ready, 1)
                if t + 2 < NT:
                    divide(t + 2)
                if t >= 1:
                    dve.wait_ge(projected, t)
                    dve.wait_ge(biased, t)
                    dve.tensor_tensor(x[:, t - 1, :], x[:, t - 1, :], y_ps[:, (t - 1) % 2, 0:C], ALU.add).then_inc(added, 1)

        @block.tensor
        def _(pe):
            def to_token_major(t):
                if t >= 2:
                    pe.wait_ge(divided, t - 1)
                for pair in range(SH // 2):
                    last = pe.transpose(a_ps[:, t % 2, PAIR * pair:PAIR * (pair + 1)],
                                        attn_t[:, T * pair + P * t:T * pair + P * (t + 1)], ident[0:PAIR, 0:PAIR])
                last.then_inc(token_major, 1)

            def turn(t):
                pe.wait_ge(divided, t + 1)
                if t >= 2:
                    pe.wait_ge(lo_ready, t - 1)
                for h in range(CH):
                    last = pe.transpose(t_ps[:, t % 2, P * h:P * (h + 1)], attn[:, t % 2, P * h:P * (h + 1)], ident[:])
                last.then_inc(turned, 1)

            to_token_major(0)
            to_token_major(1)
            turn(0)
            pe.wait_ge(w_ready, 1)
            for t in range(NT):
                if t + 2 < NT:
                    to_token_major(t + 2)
                if t + 1 < NT:
                    turn(t + 1)
                pe.wait_ge(lo_ready, t + 1)
                if t >= 2:
                    pe.wait_ge(added, t - 1)
                passes = [(os, ws, h) for h in range(CH) for os, ws in ((o_hi, w_hi), (o_hi, w_lo), (o_lo, w_hi))]
                for i, (os, ws, h) in enumerate(passes):
                    last = pe.matmul(y_ps[:, t % 2, 0:C], os[:, t % 2, h, :], ws[:, h, :], start=i == 0,
                                     stop=i == len(passes) - 1)
                last.then_inc(projected, 1)


def cross_prepare(nc, a, x, ident, x2_split, ctx_sum, k_shift):
    with ExitStack() as ctx:
        def sb(name, shape, dt=F32):
            return ctx.enter_context(nc.sbuf_tensor(name, shape, dt))

        def sem(name):
            return ctx.enter_context(nc.semaphore(name))

        y = sb("y2", [P, NT, C])
        parts, mv = sb("parts2", [P, NT, 6]), sb("mv2b", [P, NT, 2])
        var_eps, root = sb("var_eps2", [P, NT]), sb("root2", [P, NT])
        rstd, tmp = sb("rstd2", [P, NT]), sb("tmp2", [P, NT])
        bout = sb("bout", [P, C])
        wk_main, wk_tail = sb("wk_main", [P, XH * XD]), sb("wk_tail", [TAIL, XH * XD])
        xq_out = sb("xq_out", [P, 2, 2, CH, GQ], F32R)
        banks = ctx.enter_context(nc.psum_tensor("banks2", [P, 4, 512], F32))
        mean_ps = ctx.enter_context(nc.psum_tensor("mean_ps", [P, 512], F32))

        small_loaded = sem("small_loaded2")
        var_ready, root_ready, y_ready = sem("var_ready2"), sem("root_ready2"), sem("y_ready")
        dve_self = sem("dve_self2")
        xq_stored = [sem(f"xq_stored{s}") for s in range(2)]
        means_done = sem("means_done")
        turned, xq_hi, xq_lo = sem("turned2"), sem("xq_hi"), sem("xq_lo")
        block = ctx.enter_context(nc.Block())

        @block.sync
        def _(sp):
            sp.dma_start(wk_main[:], a["XWk"][0:P, :]).then_inc(small_loaded, 16)
            sp.dma_start(wk_tail[:], a["XWk"][P:CD, :]).then_inc(small_loaded, 16)
            sp.dma_start(bout[:], a["Xbout"].rearrange("(a c) -> a c", a=1).to_broadcast([P, C])).then_inc(small_loaded, 16)
            for g in range(G):
                sp.wait_ge(xq_hi, g + 1)
                sp.wait_ge(xq_lo, g + 1)
                sp.dma_start(x2_split[g], xq_out[:, g % 2].bitcast(F32)).then_inc(xq_stored[g % 2], 16)
            for s in range(2):
                sp.wait_ge(xq_stored[s], 16 * G // 2)

        @block.gpsimd
        def _(pool):
            pool.wait_ge(small_loaded, 48)
            for t in range(NT):
                pool.wait_ge(y_ready, t + 1)
                pool.tensor_tensor(x[:, t, :], x[:, t, :], bout[:], ALU.add)

        @block.vector
        def _(dve):
            chain = Chain(dve, dve_self)
            row_moments(dve, chain, x, parts, mv)
            inverse_root_seed(dve, chain, mv, var_eps, var_ready)
            dve.wait_ge(root_ready, 1)
            inverse_root(dve, chain, var_eps, root, rstd, tmp)
            for t in range(NT):
                dve.tensor_scalar(y[:, t, :], x[:, t, :], mv[:, t, 0:1], rstd[:, t:t + 1],
                                  ALU.subtract, ALU.mult).then_inc(y_ready, 1)
            for g in range(G):
                dve.wait_ge(xq_hi, g + 1)
                if g >= 2:
                    dve.wait_ge(xq_stored[g % 2], 16 * (g // 2))
                dve.tensor_tensor(flat(xq_out[:, g % 2, 1]), banks[:, g % 4, :], flat(xq_out[:, g % 2, 0]).bitcast(F32),
                                  ALU.subtract).then_inc(xq_lo, 1)
            dve.wait_ge(means_done, 1)
            dve.tensor_scalar(k_shift[:], mean_ps[:, 0:XH], -1.0 / (3.0 * KEYS), None, ALU.mult)

        @block.scalar
        def _(act):
            act.wait_ge(var_ready, 1)
            act.activation(root[:], var_eps[:], ACT.Sqrt).then_inc(root_ready, 1)
            for g in range(G):
                act.wait_ge(turned, g + 1)
                if g >= 2:
                    act.wait_ge(xq_stored[g % 2], 16 * (g // 2))
                act.copy(flat(xq_out[:, g % 2, 0]), banks[:, g % 4, :]).then_inc(xq_hi, 1)

        @block.tensor
        def _(pe):
            pe.wait_ge(small_loaded, 48)
            for h in range(XH):
                pe.matmul(mean_ps[:, h:h + 1], wk_main[:, XD * h:XD * (h + 1)], ctx_sum[:, 0:1], start=True, stop=False)
                last = pe.matmul(mean_ps[:, h:h + 1], wk_tail[:, XD * h:XD * (h + 1)], ctx_sum[0:TAIL, 1:2],
                                 start=False, stop=True)
            last.then_inc(means_done, 1)
            for g in range(G):
                pe.wait_ge(y_ready, 2 * g + 2)
                if g >= 4:
                    pe.wait_ge(xq_lo, g - 3)
                for h in range(CH):
                    for t in range(2):
                        last = pe.transpose(banks[:, g % 4, GQ * h + P * t:GQ * h + P * (t + 1)],
                                            y[:, 2 * g + t, P * h:P * (h + 1)], ident[:])
                last.then_inc(turned, 1)


PIECES = KEYS // (2 * P)
IS_CHUNK = ("A", "A+", "out", "Q+", "K+", "V+", "V")


def with_pieces(extra, ahead=()):
    items = list(ahead)
    for c in range(PIECES):
        items.append(("T", c))
        if c >= 2:
            items.append(("W", c - 2))
        items += extra.get(c, [])
    return items + [("W", PIECES - 2), ("W", PIECES - 1)]


def exponents(t, first):
    return {first + i: [("E", t, i)] for i in range(4)}


def merged(*parts):
    out = {}
    for part in parts:
        for c, items in part.items():
            out[c] = out.get(c, []) + items
    return out


STEP_0 = [("M", 0), ("A", 1, 1), ("E", 0, 0), ("V", 1), ("E", 0, 1), ("A", 1, 2), ("E", 0, 2), ("A", 1, 3), ("E", 0, 3),
          ("M", 1), ("Q+",), ("V", 0), ("E", 1, 0), ("A+", 0, 0), ("E", 1, 1), ("A+", 0, 1), ("E", 1, 2),
          ("A+", 0, 2), ("E", 1, 3)]
SCORES = {0: [("A", 0, 3)], 1: [("M", 0), ("I",)], 2: [("A", 1, 0)], 4: [("A", 1, 1)], 6: [("A", 1, 2)],
          8: [("A", 1, 3)], 9: [("M", 1)]}
EXPS = merged(exponents(0, 3), exponents(1, 10))
AHEAD = {7: [("Q+",)], 12: [("A+", 0, 0)], 14: [("A+", 0, 1)], 15: [("A+", 0, 2)]}
OUT = {10: [("out",)]}
STEP_1 = with_pieces(merged(SCORES, EXPS, AHEAD, {5: [("wkv",)], 9: [("wo",)]}))
LAST_1 = with_pieces(merged(SCORES, EXPS, AHEAD, {9: [("wo",)]}))
STEP = with_pieces(merged(SCORES, EXPS, AHEAD, OUT), [("O",)])
STEP_7 = with_pieces(merged(SCORES, EXPS, OUT, {9: [("wq",)], 11: [("K+", 0)], 13: [("K+", 1)], 15: [("Q+",)]}), [("O",)])
STEP_8 = with_pieces({0: [("K+", 2)], 1: [("I",)], 2: [("K+", 3)], 4: [("out",)], 6: [("A", 0, 0)],
                      8: [("A", 0, 1)], 10: [("A", 0, 2)], 12: [("A", 0, 3)]}, [("O",)])
AFTER = [("V+", 3), ("O",), ("V+", 2), ("A+", 1, 0), ("out",)]
LAST_7 = with_pieces(merged(SCORES, EXPS, OUT), [("O",)])
LAST_8 = with_pieces({1: [("I",)], 4: [("out",)]}, [("O",)])
LAST_AFTER = [("O",), ("out",)]
BEFORE = [("wkv",), ("wq",), ("K+", 0), ("K+", 1), ("K+", 2), ("Q+",), ("K+", 3), ("A+", 0, 0), ("A+", 0, 1), ("A+", 0, 2),
          ("A+", 0, 3), ("V+", 3), ("V+", 2), ("A+", 1, 0)]


def chunks_in(items):
    return sum(item[0] in IS_CHUNK for item in items)


FIRST = chunks_in(BEFORE)
LOOPED = (G - 4) // 2
STEP_AT = [0, chunks_in(STEP_0)]
for _g in range(2, G):
    STEP_AT.append(STEP_AT[-1] + chunks_in(STEP_1 if _g == 2 else STEP))
STEP_AT.append(STEP_AT[-1] + chunks_in(STEP_7))
AFTER_AT = STEP_AT[G] + chunks_in(STEP_8)
PER_HEAD = AFTER_AT + chunks_in(AFTER)
LAST_AT = [STEP_AT[G - 1], STEP_AT[G - 1] + chunks_in(LAST_7)]
LAST_AT.append(LAST_AT[1] + chunks_in(LAST_8))
ALL_CHUNKS = FIRST + (XH - 1) * PER_HEAD + LAST_AT[2] + chunks_in(LAST_AFTER)
assert PER_HEAD % 2 == 0 and chunks_in(STEP) % 2 == 0


def chunk_of(items, item):
    return chunks_in(items[:items.index(item)])


def run_heads(eng, run):
    run(BEFORE, -1, -1, -1, 1, 0, 0)

    def head(h, last):
        def step(items, g, at):
            run(items, h, g, h * G + g, g % 2, h * PER_HEAD + (FIRST + at), (FIRST + at) % 2)

        step(STEP_0, 0, STEP_AT[0])
        step(LAST_1 if last else STEP_1, 1, STEP_AT[1])
        with eng.Fori(0, LOOPED) as p:
            for u in range(2):
                run(STEP, h, p * 2 + (2 + u), h * G + p * 2 + (2 + u), u,
                    h * PER_HEAD + p * (STEP_AT[4] - STEP_AT[2]) + (FIRST + STEP_AT[2 + u]), (FIRST + STEP_AT[2 + u]) % 2)
        for g in range(2 + 2 * LOOPED, G - 1):
            step(STEP, g, STEP_AT[g])
        if last:
            for n, items in enumerate((LAST_7, LAST_8, LAST_AFTER)):
                step(items, G - 1 + n, LAST_AT[n])
        else:
            step(STEP_7, G - 1, STEP_AT[G - 1])
            step(STEP_8, G, STEP_AT[G])
            step(AFTER, G + 1, AFTER_AT)

    with eng.Fori(0, XH - 1) as h:
        head(h, False)
    head(XH - 1, True)


def cross_attention(nc, a, x, ident, x2_split, ctx_split, k_shift):
    with ExitStack() as ctx:
        def sb(name, shape, dt=F32):
            return ctx.enter_context(nc.sbuf_tensor(name, shape, dt))

        def sem(name):
            return ctx.enter_context(nc.semaphore(name))

        k_hi, k_lo = sb("k_hi", [P, KEYS], F32R), sb("k_lo", [P, KEYS], F32R)
        v_hi, v_lo = sb("v_hi", [P, KEYS], F32R), sb("v_lo", [P, KEYS], F32R)
        probs = sb("xprobs", [P, 2, 2, KEYS])
        blocks = sb("blocks", [P, 4, 3, BLK], F32R)
        pt_hi, pt_lo = sb("pt_hi", [P, 3, 2 * GQ], F32R), sb("pt_lo", [P, 3, 2 * GQ], F32R)
        xq = sb("xq", [P, 2, CH, GQ], F32R)
        q_hi, q_lo = sb("q_hi", [P, 2, GQ], F32R), sb("q_lo", [P, 2, GQ], F32R)
        o_hi, o_lo = sb("o_hi", [P, GQ], F32R), sb("o_lo", [P, GQ], F32R)
        wq_raw, wq_hi, wq_lo = sb("wq_raw", [P, CH * XD]), sb("wq_hi", [P, CH * XD], F32R), sb("wq_lo", [P, CH * XD], F32R)
        kv_raw, kv_hi, kv_lo = sb("kv_raw", [P, 4 * XD]), sb("kv_hi", [P, 4 * XD], F32R), sb("kv_lo", [P, 4 * XD], F32R)
        wo_raw, wo_hi, wo_lo = sb("wo_raw2", [P, C]), sb("wo_hi2", [P, C], F32R), sb("wo_lo2", [P, C], F32R)
        shift = sb("shift", [P, 1])
        chunk_max, neg_max = sb("chunk_max", [P, 2, 4]), sb("xneg_max", [P, 2, 2])
        chunk_sum, denom, inv = sb("chunk_sum", [P, 2, 2, 4]), sb("denom", [P, 2]), sb("xinv", [P, 2, 2])
        s_ps = ctx.enter_context(nc.psum_tensor("xs_ps", [P, 2, CHUNK], F32))
        t_ps = ctx.enter_context(nc.psum_tensor("xt_ps", [P, 3, 2 * GQ], F32))
        o_ps = ctx.enter_context(nc.psum_tensor("xo_ps", [P, 512], F32))

        kv_loaded, wq_loaded, wo_loaded = sem("kv_loaded"), sem("wq_loaded"), sem("wo_loaded")
        kv_w_hi, wq_w_hi, wo_w_hi = sem("kv_w_hi"), sem("wq_w_hi"), sem("wo_w_hi")
        kv_w, wq_w, wo_w = sem("kv_w"), sem("wq_w"), sem("wo_w")
        blocks_loaded = [sem(f"blocks_loaded{s}") for s in range(2)]
        xq_loaded = sem("xq_loaded")
        filled, freed = sem("filled"), sem("freed")
        kv_rounded = sem("kv_rounded")
        q_rounded, q_ready = sem("q_rounded"), sem("q_ready")
        maxed, exped, summed, inv_ready = sem("xmaxed"), sem("xexped"), sem("summed"), sem("xinv_ready")
        turned, t_rounded, t_ready = sem("xturned"), sem("t_rounded"), sem("t_ready")
        weighed = sem("xweighed")
        o_done, o_rounded, o_ready = sem("o_done"), sem("o_rounded"), sem("o_ready")
        shifted = sem("shifted")
        block = ctx.enter_context(nc.Block())

        KV_RANK = {("K+", 0): 0, ("K+", 1): 1, ("K+", 2): 2, ("K+", 3): 3, ("V+", 3): 4, ("V+", 2): 5, ("V", 1): 6, ("V", 0): 7}

        def kv_count(item, h):
            return (h if item[0] == "V" else h + 1) * 8 + (KV_RANK[item] + 1)

        @block.sync
        def _(sp):
            def load_weights(which, col):
                if which == "kv":
                    for n, name in enumerate(("XWk", "XWv")):
                        w = a[name][:, bass.ds(col, XD)]
                        sp.dma_start(kv_raw[:, 2 * XD * n:2 * XD * n + XD], w[0:P, :]).then_inc(kv_loaded, 16)
                        for d in range(2):
                            sp.dma_start(kv_raw[TAIL * d:TAIL * (d + 1), 2 * XD * n + XD:2 * XD * (n + 1)],
                                         w[P:CD, :]).then_inc(kv_loaded, 16)
                elif which == "q":
                    for k in range(CH):
                        sp.dma_start(wq_raw[:, XD * k:XD * (k + 1)],
                                     a["XWq"][P * k:P * (k + 1), bass.ds(col, XD)]).then_inc(wq_loaded, 16)
                else:
                    sp.dma_start(wo_raw[:], a["XWout"][bass.ds(col, XD), :]).then_inc(wo_loaded, 16)

            def load_blocks(pair):
                for b in (2 * pair, 2 * pair + 1):
                    sp.dma_start(blocks[:, b % 4].bitcast(F32), ctx_split[b]).then_inc(blocks_loaded[pair % 2], 16)

            def load_queries(group):
                sp.dma_start(xq[:].bitcast(F32), x2_split[bass.ds(group, 1)].rearrange("o p s k q -> (o p) s k q")).then_inc(xq_loaded, 16)

            load_weights("kv", 0)
            load_blocks(0)
            load_blocks(1)
            load_weights("q", 0)
            load_queries(0)
            sp.wait_ge(filled, 1)
            load_blocks(2)
            sp.wait_ge(filled, 2)
            load_blocks(3)
            sp.wait_ge(q_ready, 1)
            load_queries(1)
            for pair in (3, 2):
                sp.wait_ge(filled, chunk_of(BEFORE, ("V+", pair)) + 1)
                load_blocks(pair - 2)

            def head(h, last):
                def value(v):
                    return v if last else sp.snap(v)

                start = value(h * PER_HEAD + FIRST)
                wo_col = value(h * XD)
                q_base = value(h * G)
                if not last:
                    next_col = sp.snap(h * XD + XD)
                sp.wait_ge(filled, start)
                if not last:
                    load_weights("kv", next_col)
                    load_weights("q", next_col)
                load_weights("out", wo_col)
                with sp.Fori(1, G - 1) as g:
                    projected, group = sp.snap(q_base + g + 1), sp.snap(g + 1)
                    sp.wait_ge(q_ready, projected)
                    load_queries(group)
                if not last:
                    projected = [sp.snap(q_base + G + n) for n in range(2)]
                    used = [sp.snap(h * PER_HEAD + (FIRST + at + chunk_of(items, item) + 1))
                            for items, item, at in ((STEP_7, ("K+", 0), STEP_AT[G - 1]), (STEP_7, ("K+", 1), STEP_AT[G - 1]),
                                                    (AFTER, ("V+", 3), AFTER_AT), (AFTER, ("V+", 2), AFTER_AT))]
                    sp.wait_ge(q_ready, projected[0])
                    load_queries(0)
                    for n, pair in enumerate((2, 3)):
                        sp.wait_ge(filled, used[n])
                        load_blocks(pair)
                    sp.wait_ge(q_ready, projected[1])
                    load_queries(1)
                    for n, pair in enumerate((1, 0)):
                        sp.wait_ge(filled, used[2 + n])
                        load_blocks(pair)

            with sp.Fori(0, XH - 1) as h:
                head(h, False)
            head(XH - 1, True)

        @block.tensor
        def _(pe):
            def project_kv(item, h, buf):
                kind, i = item[0][0], item[1]
                if kind == "K":
                    pe.wait_ge(blocks_loaded[i % 2], (h + 1) * 64 + 32 * (i // 2 + 1))
                elif i < 2:
                    pe.wait_ge(blocks_loaded[i % 2], h * 64 + 96)
                n0 = 0 if kind == "K" else 2 * XD
                main, tail = slice(n0, n0 + XD), slice(n0 + XD, n0 + 2 * XD)
                for b in (2 * i, 2 * i + 1):
                    passes = [(kv_hi[:, main], 0, P), (kv_lo[:, main], 0, P), (kv_hi[:, main], 1, P),
                              (kv_hi[:, tail], 2, P), (kv_lo[0:TAIL, tail], 2, TAIL)]
                    o0 = BLK * (b % 2)
                    tiles = [(o0, BLK, 0)] if kind == "K" else [(o0 + P * t, P, P * t) for t in range(BLK // P)]
                    for c0, w, k0 in tiles:
                        for n, (weights, part, rows) in enumerate(passes):
                            keys = blocks[0:rows, b % 4, part, k0:k0 + w]
                            last = pe.matmul(s_ps[:, buf, c0:c0 + w], *((weights, keys) if kind == "K" else (keys, weights)),
                                             start=n == 0, stop=n == len(passes) - 1)
                return last

            def project_q(buf):
                passes = [(w, part, k) for k in range(CH) for w, part in ((wq_hi, 0), (wq_hi, 1), (wq_lo, 0))]
                for n, (w, part, k) in enumerate(passes):
                    last = pe.matmul(s_ps[:, buf, 0:GQ], w[:, XD * k:XD * (k + 1)], xq[:, part, k, :],
                                     start=n == 0, stop=n == len(passes) - 1)
                return last

            def scores(t, i, par, buf):
                for m, (q, k) in enumerate(((q_hi, k_hi), (q_hi, k_lo), (q_lo, k_hi))):
                    for b in range(2):
                        k0 = CHUNK * i + BLK * b
                        last = pe.matmul(s_ps[:, buf, BLK * b:BLK * (b + 1)], q[:, par, P * t:P * (t + 1)], k[:, k0:k0 + BLK],
                                         start=m == 0, stop=m == 2)
                return last

            def project_out(buf):
                for t in range(2):
                    for m, (o, w) in enumerate(((o_hi, wo_hi), (o_hi, wo_lo), (o_lo, wo_hi))):
                        last = pe.matmul(s_ps[:, buf, C * t:C * (t + 1)], o[:, P * t:P * (t + 1)], w[:], start=m == 0, stop=m == 2)
                return last

            def run(items, h, g, s, par, chunk, chunk_par):
                n = 0
                for item in items:
                    kind = item[0]
                    if kind in IS_CHUNK:
                        if items is not BEFORE or n >= 2:
                            pe.wait_ge(freed, chunk + (n - 1))
                        buf = (chunk_par + n) % 2
                        if kind == "A":
                            if item[1:] == (0, 0):
                                pe.wait_ge(q_ready, s + 1)
                            last = scores(item[1], item[2], par, buf)
                        elif kind == "A+":
                            if item[1:] == (0, 0):
                                pe.wait_ge(q_ready, s + 2)
                            last = scores(item[1], item[2], 1 - par, buf)
                        elif kind == "Q+":
                            if items is BEFORE or items is STEP_7:
                                pe.wait_ge(wq_w, h + 2)
                            pe.wait_ge(xq_loaded, s * 16 + 32)
                            last = project_q(buf)
                        elif kind == "out":
                            if items is STEP:
                                pe.wait_ge(wo_w, h + 1)
                            pe.wait_ge(o_ready, s - 1)
                            last = project_out(buf)
                        else:
                            if item == ("K+", 0):
                                pe.wait_ge(kv_w, h + 2)
                            last = project_kv(item, h, buf)
                        last.then_inc(filled, 1)
                        n += 1
                    elif kind == "T":
                        c = item[1]
                        if c == 0:
                            pe.wait_ge(exped, s * 2)
                        if c >= 3:
                            pe.wait_ge(t_ready, s * PIECES + (c - 2 - PIECES))
                        for j in range(2):
                            for t in range(2):
                                last = pe.transpose(t_ps[:, c % 3, GQ * j + P * t:GQ * j + P * (t + 1)],
                                                    probs[:, 1 - par, t, P * (2 * c + j):P * (2 * c + j + 1)], ident[:])
                        last.then_inc(turned, 1)
                    elif kind == "W":
                        c = item[1]
                        if c == 0 and items is not STEP_1 and items is not LAST_1:
                            pe.wait_ge(o_ready, s - 1)
                        pe.wait_ge(t_ready, s * PIECES + (c + 1 - PIECES))
                        for j in range(2):
                            vs = slice(P * (2 * c + j), P * (2 * c + j + 1))
                            for m, (v, pt) in enumerate(((v_hi, pt_hi), (v_hi, pt_lo), (v_lo, pt_hi))):
                                last = pe.matmul(o_ps[:, 0:GQ], v[:, vs], pt[:, c % 3, GQ * j:GQ * (j + 1)],
                                                 start=c == 0 and j == 0 and m == 0,
                                                 stop=c == PIECES - 1 and j == 1 and m == 2)
                        last.then_inc(o_done if c == PIECES - 1 else weighed, 1)

            run_heads(pe, run)

        @block.scalar
        def _(act):
            def run(items, h, g, s, par, chunk, chunk_par):
                n = 0
                for item in items:
                    kind = item[0]
                    buf = (chunk_par + n) % 2
                    if kind == "T":
                        c = item[1]
                        act.wait_ge(turned, s * PIECES + (c + 1 - PIECES))
                        if c >= 3:
                            act.wait_ge(weighed, s * (PIECES - 1) + (c - 2 - (PIECES - 1)))
                        act.copy(pt_hi[:, c % 3, :], t_ps[:, c % 3, :]).then_inc(t_rounded, 1)
                    elif kind == "E":
                        t, i = item[1:]
                        if i == 0:
                            act.wait_ge(maxed, s * 2 + (t + 1))
                        cols = slice(CHUNK * i, CHUNK * (i + 1))
                        ins = act.activation(probs[:, par, t, cols], probs[:, par, t, cols], ACT.Exp,
                                             bias=neg_max[:, par, t:t + 1], accum_out=chunk_sum[:, par, t, i:i + 1])
                        if i == 3:
                            ins.then_inc(exped, 1)
                    elif kind == "O":
                        act.wait_ge(o_done, s - 1)
                        act.copy(o_hi[:], o_ps[:, 0:GQ]).then_inc(o_rounded, 1)
                    elif kind == "Q+":
                        act.wait_ge(filled, chunk + (n + 1))
                        act.copy(q_hi[:, 1 - par, :], s_ps[:, buf, 0:GQ]).then_inc(q_rounded, 1)
                    elif kind in ("K+", "V+", "V"):
                        cols = slice(CHUNK * item[1], CHUNK * (item[1] + 1))
                        if item == ("K+", 0):
                            act.wait_ge(shifted, h + 2)
                        act.wait_ge(filled, chunk + (n + 1))
                        if kind == "K+":
                            act.activation(k_hi[:, cols], s_ps[:, buf, :], ACT.Identity,
                                           bias=shift[:, 0:1]).then_inc(kv_rounded, 1)
                        else:
                            act.copy(v_hi[:, cols], s_ps[:, buf, :]).then_inc(kv_rounded, 1)
                    elif kind == "wkv":
                        act.wait_ge(kv_loaded, (h + 2) * 96)
                        act.copy(kv_hi[:], kv_raw[:]).then_inc(kv_w_hi, 1)
                    elif kind == "wq":
                        act.wait_ge(wq_loaded, (h + 2) * 32)
                        act.copy(wq_hi[:], wq_raw[:]).then_inc(wq_w_hi, 1)
                    elif kind == "wo":
                        act.wait_ge(wo_loaded, (h + 1) * 16)
                        act.copy(wo_hi[:], wo_raw[:]).then_inc(wo_w_hi, 1)
                    n += kind in IS_CHUNK

            run_heads(act, run)

        @block.vector
        def _(dve):
            def run(items, h, g, s, par, chunk, chunk_par):
                n = 0
                for item in items:
                    kind = item[0]
                    buf = (chunk_par + n) % 2
                    if kind in ("A", "A+"):
                        t, i = item[1:]
                        dve.wait_ge(filled, chunk + (n + 1))
                        dve.tensor_scalar(probs[:, par if kind == "A" else 1 - par, t, CHUNK * i:CHUNK * (i + 1)],
                                          s_ps[:, buf, :], LOGIT, None, ALU.mult, ALU.max,
                                          accum_out=chunk_max[:, t, i:i + 1]).then_inc(freed, 1)
                    elif kind == "M":
                        t = item[1]
                        dve.wait_ge(freed, chunk + n)
                        dve.tensor_reduce(neg_max[:, par, t:t + 1], chunk_max[:, t, :], AX.X, ALU.max,
                                          negate=True).then_inc(maxed, 1)
                    elif kind == "T":
                        c = item[1]
                        dve.wait_ge(t_rounded, s * PIECES + (c + 1 - PIECES))
                        dve.tensor_tensor(pt_lo[:, c % 3, :], t_ps[:, c % 3, :], pt_hi[:, c % 3, :].bitcast(F32),
                                          ALU.subtract).then_inc(t_ready, 1)
                    elif kind == "I":
                        dve.wait_ge(exped, s * 2)
                        dve.tensor_reduce(denom[:], chunk_sum[:, 1 - par, :, :], AX.X, ALU.add).then_inc(summed, 1)
                        dve.wait_ge(summed, s)
                        dve.reciprocal(inv[:, 1 - par, :], denom[:]).then_inc(inv_ready, 1)
                    elif kind == "O":
                        dve.wait_ge(o_rounded, s - 1)
                        dve.tensor_tensor(o_lo[:], o_ps[:, 0:GQ], o_hi[:].bitcast(F32), ALU.subtract).then_inc(o_ready, 1)
                    elif kind == "out":
                        dve.wait_ge(filled, chunk + (n + 1))
                        dve.wait_ge(inv_ready, s - 1)
                        first = g * 2 - 4
                        for t in range(2):
                            tile = x[:, bass.ds(first + t, 1), :].rearrange("p o c -> p (o c)")
                            last = dve.scalar_tensor_tensor(out=tile, in0=s_ps[:, buf, C * t:C * (t + 1)],
                                                            scalar=inv[:, par, t:t + 1], in1=tile, op0=ALU.mult, op1=ALU.add)
                        last.then_inc(freed, 1)
                    elif kind == "Q+":
                        dve.wait_ge(q_rounded, s + 2)
                        for t, done in enumerate((q_ready, freed)):
                            half = slice(P * t, P * (t + 1))
                            dve.tensor_tensor(q_lo[:, 1 - par, half], s_ps[:, buf, half], q_hi[:, 1 - par, half].bitcast(F32),
                                              ALU.subtract).then_inc(done, 1)
                    elif kind in ("K+", "V+", "V"):
                        cols = slice(CHUNK * item[1], CHUNK * (item[1] + 1))
                        if item == ("K+", 0):
                            dve.wait_ge(shifted, h + 2)
                        dve.wait_ge(kv_rounded, kv_count(item, h))
                        if kind == "K+":
                            dve.scalar_tensor_tensor(out=k_lo[:, cols], in0=s_ps[:, buf, :], scalar=shift[:, 0:1],
                                                     in1=k_hi[:, cols].bitcast(F32), op0=ALU.add,
                                                     op1=ALU.subtract).then_inc(freed, 1)
                        else:
                            dve.tensor_tensor(v_lo[:, cols], s_ps[:, buf, :], v_hi[:, cols].bitcast(F32),
                                              ALU.subtract).then_inc(freed, 1)
                    elif kind == "wkv":
                        dve.wait_ge(kv_w_hi, h + 2)
                        dve.tensor_tensor(kv_lo[:], kv_raw[:], kv_hi[:].bitcast(F32), ALU.subtract).then_inc(kv_w, 1)
                        if items is BEFORE:
                            dve.tensor_copy(shift[:], k_shift[:, 0:1]).then_inc(shifted, 1)
                    elif kind == "wq":
                        dve.wait_ge(wq_w_hi, h + 2)
                        dve.tensor_tensor(wq_lo[:], wq_raw[:], wq_hi[:].bitcast(F32), ALU.subtract).then_inc(wq_w, 1)
                        if items is not BEFORE:
                            dve.tensor_copy(shift[:], k_shift[:, bass.ds(h + 1, 1)]).then_inc(shifted, 1)
                    elif kind == "wo":
                        dve.wait_ge(wo_w_hi, h + 1)
                        dve.tensor_tensor(wo_lo[:], wo_raw[:], wo_hi[:].bitcast(F32), ALU.subtract).then_inc(wo_w, 1)
                    n += kind in IS_CHUNK

            run_heads(dve, run)
            dve.wait_ge(freed, ALL_CHUNKS)


def channel_mix(nc, a, x, ident):
    with ExitStack() as ctx:
        def sb(name, shape, dt=F32):
            return ctx.enter_context(nc.sbuf_tensor(name, shape, dt))

        def sem(name):
            return ctx.enter_context(nc.semaphore(name))

        y = sb("y3", [P, NT, C])
        parts, mv = sb("parts3", [P, NT, 6]), sb("mv3", [P, NT, 2])
        var_eps, root = sb("var_eps3", [P, NT]), sb("root3", [P, NT])
        rstd, tmp = sb("rstd3", [P, NT]), sb("tmp3", [P, NT])
        w_raw = sb("fw_raw", [P, 3, CH, C])
        w_hi, w_lo = sb("fw_hi", [P, 3, CH, C], F32R), sb("fw_lo", [P, 3, CH, C], F32R)
        mu, nu = sb("mu", [P, 2, CH]), sb("nu", [P, 2, CH])
        yt = sb("yt", [P, CH, B, N + 1])
        part = sb("mix_part", [P, 2, N])
        full = sb("mix_full", [P, 4, N])
        mix_hi, mix_lo = sb("mix_hi", [P, 2, CH, T], F32R), sb("mix_lo", [P, 2, CH, T], F32R)
        relu, square = sb("relu", [P, 2, N]), sb("square", [P, 2, N])
        act_hi, act_lo = sb("act_hi", [P, CH, T], F32R), sb("act_lo", [P, CH, T], F32R)
        gate, gated = sb("gate", [P, 2, C]), sb("gated", [P, 2, C])
        banks = ctx.enter_context(nc.psum_tensor("banks3", [P, 8, 512], F32))

        loaded = sem("loaded3")
        var_ready, root_ready, y_ready = sem("var_ready3"), sem("root_ready3"), sem("y_ready3")
        dve_self, padded, nu_ready = sem("dve_self3"), sem("padded"), sem("nu_ready")
        w_hi_ready, w_ready = sem("fw_hi_ready"), sem("fw_ready")
        turned, yt_ready = sem("turned3"), sem("yt_ready")
        mixed, mix_rounded, mix_ready = sem("mixed"), sem("mix_rounded"), sem("mix_ready")
        k_done, relu_done, squared, act_rounded, act_ready = (sem("k_done"), sem("relu_done"), sem("squared"),
                                                              sem("act_rounded"), sem("act_ready"))
        rv_done, gate_ready, gated_ready, added = sem("rv_done"), sem("gate_ready"), sem("gated_ready"), sem("added3")
        block = ctx.enter_context(nc.Block())
        PIECES = [(b, h) for b in range(B) for h in range(CH)]

        @block.sync
        def _(sp):
            for n, name in enumerate(("W_rT", "W_kT", "W_vT")):
                sp.dma_start(w_raw[:, n, :, :], a[name].rearrange("(h p) o -> p h o", p=P)).then_inc(loaded, 16)
            with nc.allow_non_contiguous_dma(reason="a few per-channel vectors"):
                for n, name in enumerate(("mu_r", "mu_k")):
                    sp.dma_start(mu[:, n, :], a[name].rearrange("(h p) -> p h", p=P)).then_inc(loaded, 16)

        @block.gpsimd
        def _(pool):
            pool.memset(yt[:, :, :, 0:1], 0.0).then_inc(padded, 1)

        @block.vector
        def _(dve):
            chain = Chain(dve, dve_self)
            row_moments(dve, chain, x, parts, mv)
            inverse_root_seed(dve, chain, mv, var_eps, var_ready)
            dve.wait_ge(loaded, 80)
            dve.tensor_scalar(nu[:], mu[:], -1.0, 1.0, ALU.mult, ALU.add).then_inc(nu_ready, 1)
            for n in range(3):
                dve.wait_ge(w_hi_ready, n + 1)
                dve.tensor_tensor(flat(w_lo[:, n]), flat(w_raw[:, n]), flat(w_hi[:, n]).bitcast(F32),
                                  ALU.subtract).then_inc(w_ready, 1)
            dve.wait_ge(root_ready, 1)
            inverse_root(dve, chain, var_eps, root, rstd, tmp)
            for t in range(NT):
                dve.tensor_scalar(y[:, t, :], x[:, t, :], mv[:, t, 0:1], rstd[:, t:t + 1],
                                  ALU.subtract, ALU.mult).then_inc(y_ready, 1)
            dve.wait_ge(nu_ready, 1)
            dve.wait_ge(padded, 1)

            def mix_lo_of(n):
                b, h, m = n // 4, n // 2 % 2, n % 2
                dve.wait_ge(mix_rounded, n + 1)
                cols = slice(N * b, N * (b + 1))
                dve.tensor_tensor(mix_lo[:, m, h, cols], full[:, n % 4, :], mix_hi[:, m, h, cols].bitcast(F32),
                                  ALU.subtract).then_inc(mix_ready, 1)

            pieces = 2 * len(PIECES)
            for n in range(pieces + 2):
                if n < pieces:
                    (b, h), m = PIECES[n // 2], n % 2
                    dve.wait_ge(yt_ready, n // 2 + 1)
                    chain(dve.tensor_scalar(part[:, m, :], yt[:, h, b, 1:N + 1], mu[:, m, h:h + 1], None, ALU.mult))
                    chain.wait()
                    if n >= 4:
                        dve.wait_ge(mix_ready, n - 3)
                    dve.scalar_tensor_tensor(out=full[:, n % 4, :], in0=yt[:, h, b, 0:N], scalar=nu[:, m, h:h + 1],
                                             in1=part[:, m, :], op0=ALU.mult, op1=ALU.add).then_inc(mixed, 1)
                if n >= 2:
                    mix_lo_of(n - 2)
            for n in range(len(PIECES)):
                b, h = PIECES[n]
                cols = slice(N * b, N * (b + 1))
                dve.wait_ge(relu_done, n + 1)
                dve.tensor_tensor(square[:, n % 2, :], relu[:, n % 2, :], relu[:, n % 2, :], ALU.mult).then_inc(squared, 1)
                dve.wait_ge(act_rounded, n + 1)
                dve.tensor_tensor(act_lo[:, h, cols], square[:, n % 2, :], act_hi[:, h, cols].bitcast(F32),
                                  ALU.subtract).then_inc(act_ready, 1)
            for t in range(NT):
                dve.wait_ge(gate_ready, t + 1)
                if t >= 2:
                    dve.wait_ge(added, t - 1)
                dve.tensor_tensor(gated[:, t % 2, :], gate[:, t % 2, :], banks[:, t % 4, C:2 * C],
                                  ALU.mult).then_inc(gated_ready, 1)
                dve.wait_ge(gated_ready, t + 1)
                dve.tensor_tensor(x[:, t, :], x[:, t, :], gated[:, t % 2, :], ALU.add).then_inc(added, 1)

        @block.scalar
        def _(act):
            act.wait_ge(var_ready, 1)
            act.activation(root[:], var_eps[:], ACT.Sqrt).then_inc(root_ready, 1)
            act.wait_ge(loaded, 80)
            for n in range(3):
                act.copy(flat(w_hi[:, n]), flat(w_raw[:, n])).then_inc(w_hi_ready, 1)
            for n in range(len(PIECES) + 1):
                if n < len(PIECES):
                    b, h = PIECES[n]
                    act.wait_ge(turned, n + 1)
                    act.copy(yt[:, h, b, 1:N + 1], banks[:, n % 4, :]).then_inc(yt_ready, 1)
                if n >= 1:
                    b, h = PIECES[n - 1]
                    for m in range(2):
                        act.wait_ge(mixed, 2 * n - 1 + m)
                        act.copy(mix_hi[:, m, h, N * b:N * (b + 1)], full[:, (2 * n - 2 + m) % 4, :]).then_inc(mix_rounded, 1)
            for n in range(len(PIECES)):
                b, h = PIECES[n]
                act.wait_ge(k_done, n + 1)
                if n >= 2:
                    act.wait_ge(squared, n - 1)
                act.activation(relu[:, n % 2, :], banks[:, 4 + n % 4, :], ACT.Relu).then_inc(relu_done, 1)
                act.wait_ge(squared, n + 1)
                act.copy(act_hi[:, h, N * b:N * (b + 1)], square[:, n % 2, :]).then_inc(act_rounded, 1)
            for t in range(NT):
                act.wait_ge(rv_done, t + 1)
                if t >= 2:
                    act.wait_ge(gated_ready, t - 1)
                act.activation(gate[:, t % 2, :], banks[:, t % 4, 0:C], ACT.Sigmoid).then_inc(gate_ready, 1)

        @block.tensor
        def _(pe):
            for n, (b, h) in enumerate(PIECES):
                pe.wait_ge(y_ready, QI * (b + 1))
                if n >= 4:
                    pe.wait_ge(yt_ready, n - 3)
                for t in range(QI):
                    last = pe.transpose(banks[:, n % 4, P * t:P * (t + 1)], y[:, QI * b + t, P * h:P * (h + 1)], ident[:])
                last.then_inc(turned, 1)
            pe.wait_ge(w_ready, 3)
            for n, (b, oh) in enumerate(PIECES):
                pe.wait_ge(mix_ready, 4 * (b + 1))
                if n >= 4:
                    pe.wait_ge(relu_done, n - 3)
                passes = [(ws, zs, h) for h in range(CH) for ws, zs in ((w_hi, mix_hi), (w_hi, mix_lo), (w_lo, mix_hi))]
                for i, (ws, zs, h) in enumerate(passes):
                    last = pe.matmul(banks[:, 4 + n % 4, :], ws[:, 1, h, P * oh:P * (oh + 1)],
                                     zs[:, 1, h, N * b:N * (b + 1)], start=i == 0, stop=i == len(passes) - 1)
                last.then_inc(k_done, 1)
            for t in range(NT):
                pe.wait_ge(act_ready, CH * (t // QI + 1))
                if t >= 4:
                    pe.wait_ge(added, t - 3)
                rows = slice(P * t, P * (t + 1))
                for c0, w, hi, lo in ((0, 0, mix_hi[:, 0], mix_lo[:, 0]), (C, 2, act_hi, act_lo)):
                    passes = [(zs, ws, h) for h in range(CH) for zs, ws in ((hi, w_hi), (hi, w_lo), (lo, w_hi))]
                    for i, (zs, ws, h) in enumerate(passes):
                        last = pe.matmul(banks[:, t % 4, c0:c0 + C], zs[:, h, rows], ws[:, w, h, :],
                                         start=i == 0, stop=i == len(passes) - 1)
                last.then_inc(rv_done, 1)


def interpolation():
    pos = np.arange(N, dtype=np.float32) * np.float32((BIAS_S - 1) / (N - 1))
    i0 = np.floor(pos).astype(np.int32)
    i1 = np.minimum(i0 + 1, BIAS_S - 1)
    frac = pos - i0.astype(np.float32)
    m = np.zeros((N, BIAS_S), np.float32)
    np.add.at(m, (np.arange(N), i0), np.float32(1.0) - frac)
    np.add.at(m, (np.arange(N), i1), frac)
    m[-1] = 0.0
    return np.ascontiguousarray(m.T)


def kernel(**inputs):
    import concourse.bacc as bacc
    from concourse.bass_utils import run_bass_kernel_spmd

    def arr(name):
        return np.asarray(inputs[name])

    arrays = {
        "x": arr("x").reshape(T, C),
        "ctxT": arr("ctx_768").reshape(KEYS, CD).T,
        "WqT": arr("L0_attn_Wq").T, "WkT": arr("L0_attn_Wk").T, "WvT": arr("L0_attn_Wv").T, "WoT": arr("L0_attn_Wo").T,
        "bq": arr("L0_attn_bq"), "bk": arr("L0_attn_bk"), "bv": arr("L0_attn_bv"), "bo": arr("L0_attn_bo"),
        "gamma": arr("L0_attn_gamma"), "beta": arr("L0_attn_beta"), "rel_bias": arr("L0_attn_rel_bias"),
        "XWq": arr("L0_xattn_Wq"), "XWk": arr("L0_xattn_Wk"), "XWv": arr("L0_xattn_Wv"),
        "XWout": arr("L0_xattn_Wout"), "Xbout": arr("L0_xattn_bout"),
        "W_rT": arr("L0_ffn_W_r").T, "W_kT": arr("L0_ffn_W_k").T, "W_vT": arr("L0_ffn_W_v").T,
        "mu_r": arr("L0_ffn_mu_r"), "mu_k": arr("L0_ffn_mu_k"),
        "identity": np.eye(P, dtype=np.float32),
        "causal": np.triu(np.full((P, P), MASKED, np.float32), 1),
        "interp": interpolation(),
    }
    nc = bacc.Bacc("TRN2", target_bir_lowering=False, num_devices=1)
    feed, aps = {}, {}
    for name, value in arrays.items():
        value = np.ascontiguousarray(value)
        feed[f"in_{name}"] = value
        aps[name] = nc.dram_tensor(f"in_{name}", value.shape, mybir.dt.from_np(value.dtype), kind="ExternalInput").ap()
    out = nc.dram_tensor("out_x", (T, C), F32, kind="ExternalOutput").ap()
    decoder_layer(nc, aps, out)
    result = run_bass_kernel_spmd(nc, [feed], core_ids=[0])
    return result.results[0]["out_x"].reshape(B, N, C)
```

```python
from contextlib import ExitStack

import numpy as np

import concourse.bass as bass
from concourse import mybir

ALU = mybir.AluOpType
ACT = mybir.ActivationFunctionType
AX = mybir.AxisListType
F32 = mybir.dt.float32
F32R = mybir.dt.float32r

P = 128
B, N, C = 4, 512, 256
T = B * N
NT = T // P
CH = C // P
EPS = 1e-5

SH, SD = 16, 16
BIAS_S = 32
QI = N // P
STACK = 3 * SD
REL_STACK = 3 * BIAS_S
SLOT_ROWS = 2 * SD
MASKED = -1e30

XH, XD = 8, 128
CD, M = 192, 1024
KEYS = B * M
TAIL = CD - P
LOGIT = 1.5 * XD ** -0.5
G = 8
GQ = T // G
BLK = 512
NB = KEYS // BLK
CHUNK = 1024


def flat(ap):
    return ap.rearrange("p a b -> p (a b)")


def decoder_layer(nc, a, out):
    with ExitStack() as ctx:
        x = ctx.enter_context(nc.sbuf_tensor("x", [P, NT, C], F32))
        ident = ctx.enter_context(nc.sbuf_tensor("ident", [P, P], F32))
        ctx_sum = ctx.enter_context(nc.sbuf_tensor("ctx_sum", [P, 2], F32))
        q_split = nc.dram_tensor("q_split", (2, C, T), F32).ap()
        k_split = nc.dram_tensor("k_split", (2, C, T), F32).ap()
        x2_split = nc.dram_tensor("x2_split", (G, P, 2, CH, GQ), F32).ap()
        ctx_split = nc.dram_tensor("ctx_split", (NB, P, 3, BLK), F32).ap()
        with ExitStack() as keep:
            v_split = keep.enter_context(nc.sbuf_tensor("v_split", [P, NT, SH * SLOT_ROWS], F32R))
            self_projections(nc, a, x, ident, v_split, q_split, k_split)
            attn_t = keep.enter_context(nc.sbuf_tensor("attn_t", [2 * SLOT_ROWS, SH // 2 * T], F32))
            exp_sums = keep.enter_context(nc.sbuf_tensor("exp_sums", [P, SH * NT], F32))
            self_attention(nc, a, ident, v_split, attn_t, exp_sums, q_split, k_split, ctx_split, ctx_sum)
            self_output(nc, a, x, ident, attn_t, exp_sums)
        k_shift = ctx.enter_context(nc.sbuf_tensor("k_shift", [P, XH], F32))
        with ExitStack() as keep:
            streams = CrossStreams(nc, keep, a, ctx_split)
            cross_prepare(nc, a, x, ident, x2_split, ctx_sum, k_shift, streams)
            cross_attention(nc, a, x, ident, x2_split, k_shift, streams)
        channel_mix(nc, a, x, ident, out)


class Chain:

    def __init__(self, eng, sem):
        self.eng, self.sem, self.n = eng, sem, 0

    def __call__(self, ins):
        self.n += 1
        ins.then_inc(self.sem, 1)

    def wait(self):
        self.eng.wait_ge(self.sem, self.n)


def row_moments(dve, chain, src, parts, mv):
    for t in range(NT):
        chain(dve.bn_stats(parts[:, t, :], src[:, t, :]))
    chain.wait()
    for t in range(NT):
        chain(dve.bn_aggr(mv[:, t, :], parts[:, t, :]))
    chain.wait()


def inverse_root_seed(dve, chain, mv, var_eps, var_ready):
    dve.tensor_scalar(var_eps[:], mv[:, :, 1], EPS, None, ALU.add).then_inc(var_ready, 1)


def inverse_root(dve, chain, var_eps, root, rstd, tmp):
    chain(dve.reciprocal(rstd, root))
    chain.wait()
    chain(dve.tensor_tensor(tmp[:], rstd, rstd, ALU.mult))
    chain.wait()
    chain(dve.tensor_tensor(tmp[:], tmp[:], var_eps, ALU.mult))
    chain.wait()
    chain(dve.tensor_scalar(tmp[:], tmp[:], -0.5, 1.5, ALU.mult, ALU.add))
    chain.wait()
    chain(dve.tensor_tensor(rstd, rstd, tmp[:], ALU.mult))
    chain.wait()


def self_projections(nc, a, x, ident, v_split, q_split, k_split):
    with ExitStack() as ctx:
        def sb(name, shape, dt=F32):
            return ctx.enter_context(nc.sbuf_tensor(name, shape, dt))

        def sem(name):
            return ctx.enter_context(nc.semaphore(name))

        y = sb("y", [P, NT, C])
        z_full = sb("z_full", [P, 2, 512])
        z_hi = sb("z_hi", [P, CH, T], F32R)
        z_lo = sb("z_lo", [P, CH, T], F32R)
        w_raw = sb("w_raw", [P, 3, CH, C])
        w_hi = sb("w_hi", [P, 3, CH, C], F32R)
        w_lo = sb("w_lo", [P, 3, CH, C], F32R)
        v_full = sb("v_full", [P, 2, C])
        stage_hi = sb("stage_hi", [P, 2, T], F32R)
        stage_lo = sb("stage_lo", [P, 2, T], F32R)
        gamma, beta = sb("gamma", [P, CH]), sb("beta", [P, CH])
        bqk = sb("bqk", [P, 2, CH])
        bqk_scaled = sb("bqk_scaled", [P, 2, CH])
        bv = sb("bv", [P, C])
        parts, mv = sb("parts", [P, NT, 6]), sb("mv", [P, NT, 2])
        var_eps, root = sb("var_eps", [P, 2, NT]), sb("root", [P, 2, NT])
        factor, rstd, tmp = sb("factor", [P, 2, NT]), sb("rstd", [P, NT]), sb("tmp", [P, NT])
        banks = ctx.enter_context(nc.psum_tensor("banks", [P, 8, 512], F32))

        x_loaded = [sem(f"x_loaded{n}") for n in range(NT // 4)]
        w_loaded, small_loaded = sem("w_loaded"), sem("small_loaded")
        var_ready, root_ready, z_ready = sem("var_ready"), sem("root_ready"), sem("z_ready")
        dve_self, biases_ready = sem("dve_self"), sem("biases_ready")
        w_hi_ready, w_lo_ready = sem("w_hi_ready"), sem("w_lo_ready")
        turned, z_hi_ready, z_lo_ready = sem("turned"), sem("z_hi_ready"), sem("z_lo_ready")
        projected, stage_hi_ready, stage_lo_ready = sem("projected"), sem("stage_hi_ready"), sem("stage_lo_ready")
        stack_stored = [sem("q_stack_stored"), sem("k_stack_stored")]
        v_done, v_ready, v_hi_ready, v_lo_ready = sem("v_done"), sem("v_ready"), sem("v_hi_ready"), sem("v_lo_ready")
        block = ctx.enter_context(nc.Block())

        TB = T // 512
        QK_UNITS = [(w, oh, tb) for oh in range(CH) for w in range(2) for tb in range(TB)]

        def v_parts(t):
            heads = v_split[:, t, :].rearrange("p (h r) -> p h r", r=SLOT_ROWS)
            return heads[:, :, 0:SD], heads[:, :, SD:]

        @block.sync
        def _(sp):
            xs = a["x"].rearrange("(t p) c -> p t c", p=P)
            for t in range(0, NT, 4):
                sp.dma_start(x[:, t:t + 4, :], xs[:, t:t + 4, :]).then_inc(x_loaded[t // 4], 16)
            for n, name in enumerate(("WqT", "WkT", "WvT")):
                sp.dma_start(w_raw[:, n, :, :], a[name].rearrange("(h p) o -> p h o", p=P)).then_inc(w_loaded, 16)
            with nc.allow_non_contiguous_dma(reason="a few per-channel vectors"):
                sp.dma_start(gamma[:], a["gamma"].rearrange("(h p) -> p h", p=P)).then_inc(small_loaded, 16)
                sp.dma_start(beta[:], a["beta"].rearrange("(h p) -> p h", p=P)).then_inc(small_loaded, 16)
                sp.dma_start(bqk[:, 0, :], a["bq"].rearrange("(h p) -> p h", p=P)).then_inc(small_loaded, 16)
                sp.dma_start(bqk[:, 1, :], a["bk"].rearrange("(h p) -> p h", p=P)).then_inc(small_loaded, 16)
            sp.dma_start(bv[:], a["bv"].rearrange("(a c) -> a c", a=1).to_broadcast([P, C])).then_inc(small_loaded, 16)
            sp.dma_start(ident[:], a["identity"]).then_inc(small_loaded, 16)
            n = 0
            for oh in range(CH):
                rows = slice(P * oh, P * (oh + 1))
                for w, dest in enumerate((q_split, k_split)):
                    n += TB
                    sp.wait_ge(stage_hi_ready, n)
                    sp.dma_start(dest[0, rows], stage_hi[:, w, :].bitcast(F32)).then_inc(stack_stored[w], 16)
                    sp.wait_ge(stage_lo_ready, n)
                    sp.dma_start(dest[1, rows], stage_lo[:, w, :].bitcast(F32)).then_inc(stack_stored[w], 16)
            for w in range(2):
                sp.wait_ge(stack_stored[w], 16 * 2 * CH)

        @block.vector
        def _(dve):
            chain = Chain(dve, dve_self)
            for t in range(NT):
                if t % 4 == 0:
                    dve.wait_ge(x_loaded[t // 4], 16)
                chain(dve.bn_stats(parts[:, t, :], x[:, t, :]))
            chain.wait()
            for t in range(NT):
                chain(dve.bn_aggr(mv[:, t, :], parts[:, t, :]))
            chain.wait()
            dve.tensor_scalar(var_eps[:, 0, :], mv[:, :, 1], EPS, None, ALU.add).then_inc(var_ready, 1)
            dve.wait_ge(root_ready, 1)
            inverse_root(dve, chain, var_eps[:, 0, :], root[:, 0, :], factor[:, 0, :], tmp)
            chain(dve.tensor_tensor(tmp[:], factor[:, 0, :], factor[:, 0, :], ALU.mult))
            chain.wait()
            chain(dve.tensor_tensor(tmp[:], tmp[:], mv[:, :, 1], ALU.mult))
            chain.wait()
            dve.tensor_scalar(var_eps[:, 1, :], tmp[:], EPS, None, ALU.add).then_inc(var_ready, 1)
            dve.wait_ge(root_ready, 2)
            inverse_root(dve, chain, var_eps[:, 1, :], root[:, 1, :], factor[:, 1, :], tmp)
            chain(dve.tensor_tensor(rstd[:], factor[:, 0, :], factor[:, 1, :], ALU.mult))
            chain.wait()

            def normalise(tb):
                for t in range(4 * tb, 4 * tb + 4):
                    dve.tensor_scalar(y[:, t, :], x[:, t, :], mv[:, t, 0:1], rstd[:, t:t + 1],
                                      ALU.subtract, ALU.mult).then_inc(z_ready, 1)

            normalise(0)
            dve.wait_ge(small_loaded, 16 * 6)
            dve.tensor_scalar(bqk_scaled[:, 0, :], bqk[:, 0, :], SD ** -0.5, None, ALU.mult)
            dve.tensor_copy(bqk_scaled[:, 1, :], bqk[:, 1, :]).then_inc(biases_ready, 1)
            normalise(1)
            for n in range(TB * CH):
                tb, h = n // CH, n % CH
                if h == 0 and 1 <= tb < TB - 1:
                    normalise(tb + 1)
                dve.wait_ge(turned, n + 1)
                dve.wait_ge(z_hi_ready, n + 1)
                if n >= 2:
                    dve.wait_ge(z_lo_ready, n - 1)
                chain(dve.tensor_scalar(z_full[:, n % 2, :], banks[:, n % 4, :], gamma[:, h:h + 1], beta[:, h:h + 1],
                                        ALU.mult, ALU.add))
                chain.wait()
                dve.tensor_tensor(z_lo[:, h, 512 * tb:512 * (tb + 1)], z_full[:, n % 2, :],
                                  z_hi[:, h, 512 * tb:512 * (tb + 1)].bitcast(F32), ALU.subtract).then_inc(z_lo_ready, 1)
                if n < 3:
                    dve.wait_ge(w_hi_ready, n + 1)
                    dve.scalar_tensor_tensor(out=flat(w_lo[:, n]), in0=flat(w_raw[:, n]), scalar=SD ** -0.5 if n == 0 else 1.0,
                                             in1=flat(w_hi[:, n]).bitcast(F32), op0=ALU.mult,
                                             op1=ALU.subtract).then_inc(w_lo_ready, 1)
            for n, (w, oh, tb) in enumerate(QK_UNITS):
                dve.wait_ge(stage_hi_ready, n + 1)
                if n >= 2 * TB and tb == 0:
                    dve.wait_ge(stack_stored[w], 16 * 2)
                dve.scalar_tensor_tensor(out=stage_lo[:, w, 512 * tb:512 * (tb + 1)], in0=banks[:, 4 + n % 4, :],
                                         scalar=bqk_scaled[:, w, oh:oh + 1],
                                         in1=stage_hi[:, w, 512 * tb:512 * (tb + 1)].bitcast(F32),
                                         op0=ALU.add, op1=ALU.subtract).then_inc(stage_lo_ready, 1)
            for t in range(NT + 1):
                if t < NT:
                    dve.wait_ge(v_done, t + 1)
                    if t >= 2:
                        dve.wait_ge(v_lo_ready, t - 1)
                    dve.tensor_tensor(v_full[:, t % 2, :], banks[:, t % 4, 0:C], bv[:], ALU.add).then_inc(v_ready, 1)
                if t >= 1:
                    dve.wait_ge(v_hi_ready, t)
                    hi, lo = v_parts(t - 1)
                    dve.tensor_tensor(lo, v_full[:, (t - 1) % 2, :].rearrange("p (h d) -> p h d", d=SD), hi.bitcast(F32),
                                      ALU.subtract).then_inc(v_lo_ready, 1)

        @block.scalar
        def _(act):
            act.wait_ge(var_ready, 1)
            act.activation(root[:, 0, :], var_eps[:, 0, :], ACT.Sqrt).then_inc(root_ready, 1)
            act.wait_ge(var_ready, 2)
            act.activation(root[:, 1, :], var_eps[:, 1, :], ACT.Sqrt).then_inc(root_ready, 1)
            act.wait_ge(w_loaded, 16 * 3)
            for n in range(3):
                act.activation(flat(w_hi[:, n]), flat(w_raw[:, n]), ACT.Copy,
                               scale=SD ** -0.5 if n == 0 else 1.0).then_inc(w_hi_ready, 1)
            act.wait_ge(small_loaded, 16 * 6)
            for n in range(TB * CH):
                tb, h = n // CH, n % CH
                act.wait_ge(turned, n + 1)
                act.activation(z_hi[:, h, 512 * tb:512 * (tb + 1)], banks[:, n % 4, :], ACT.Identity,
                               bias=beta[:, h:h + 1], scale=gamma[:, h:h + 1]).then_inc(z_hi_ready, 1)
            act.wait_ge(biases_ready, 1)
            for n, (w, oh, tb) in enumerate(QK_UNITS):
                act.wait_ge(projected, n + 1)
                if n >= 2 * TB and tb == 0:
                    act.wait_ge(stack_stored[w], 16 * 2)
                act.activation(stage_hi[:, w, 512 * tb:512 * (tb + 1)], banks[:, 4 + n % 4, :], ACT.Identity,
                               bias=bqk_scaled[:, w, oh:oh + 1]).then_inc(stage_hi_ready, 1)
            for t in range(NT):
                act.wait_ge(v_ready, t + 1)
                act.copy(v_parts(t)[0], v_full[:, t % 2, :].rearrange("p (h d) -> p h d", d=SD)).then_inc(v_hi_ready, 1)

        @block.tensor
        def _(pe):
            pe.wait_ge(small_loaded, 16 * 6)
            for n in range(TB * CH):
                tb, h = n // CH, n % CH
                pe.wait_ge(z_ready, 4 * tb + 4)
                if n >= 4:
                    pe.wait_ge(z_lo_ready, n - 3)
                for t in range(4):
                    last = pe.transpose(banks[:, n % 4, P * t:P * (t + 1)], y[:, 4 * tb + t, P * h:P * (h + 1)], ident[:])
                last.then_inc(turned, 1)
            pe.wait_ge(w_lo_ready, 3)
            for n, (w, oh, tb) in enumerate(QK_UNITS):
                if n < TB:
                    pe.wait_ge(z_lo_ready, CH * (tb + 1))
                if n >= 4:
                    pe.wait_ge(stage_lo_ready, n - 3)
                passes = [(ws, zs, h) for h in range(CH) for ws, zs in ((w_hi, z_hi), (w_hi, z_lo), (w_lo, z_hi))]
                for i, (ws, zs, h) in enumerate(passes):
                    last = pe.matmul(banks[:, 4 + n % 4, :], ws[:, w, h, P * oh:P * (oh + 1)],
                                     zs[:, h, 512 * tb:512 * (tb + 1)], start=i == 0, stop=i == len(passes) - 1)
                last.then_inc(projected, 1)
            for t in range(NT):
                if t >= 4:
                    pe.wait_ge(v_ready, t - 3)
                passes = [(ws, zs, h) for h in range(CH) for ws, zs in ((w_hi, z_hi), (w_lo, z_hi), (w_hi, z_lo))]
                for i, (ws, zs, h) in enumerate(passes):
                    last = pe.matmul(banks[:, t % 4, 0:C], zs[:, h, P * t:P * (t + 1)], ws[:, 2, h, :],
                                     start=i == 0, stop=i == len(passes) - 1)
                last.then_inc(v_done, 1)


UNITS = [[(3, 0)], [(0, 0), (2, P)], [(1, 0)]]


def self_attention(nc, a, ident, v_split, attn_t, exp_sums, q_split, k_split, ctx_split, ctx_sum):
    with ExitStack() as ctx:
        def sb(name, shape, dt=F32):
            return ctx.enter_context(nc.sbuf_tensor(name, shape, dt))

        def sem(name):
            return ctx.enter_context(nc.semaphore(name))

        def psum(name, shape):
            return ctx.enter_context(nc.psum_tensor(name, shape, F32))

        q_st = [sb(f"q_st{h}", [STACK, T], F32R) for h in range(2)]
        k_st = [sb(f"k_st{h}", [STACK, T], F32R) for h in range(2)]
        v_st = [sb(f"v_st{h}", [P, NT, SLOT_ROWS], F32R) for h in range(2)]
        rel_st = [sb(f"rel_st{h}", [BIAS_S, 3, BIAS_S]) for h in range(2)]
        interp = sb("interp", [BIAS_S, N])
        interp3 = sb("interp3", [REL_STACK, N])
        key_st = sb("key_st", [REL_STACK, N], F32R)
        key_hi = sb("key_hi", [REL_STACK, N], F32R)
        rows_hi = sb("rows_hi", [REL_STACK, N], F32R)
        rows_st = [sb(f"rows_st{h}", [REL_STACK, N], F32R) for h in range(2)]
        mask_raw, mask = sb("mask_raw", [P, P]), sb("mask", [P, P], F32R)
        ident_r = sb("ident_r", [P, P], F32R)
        probs = sb("probs", [P, 4, 512])
        pt_hi, pt_lo = sb("spt_hi", [P, 3, 512], F32R), sb("spt_lo", [P, 3, 512], F32R)
        ctx_in = sb("ctx_in", [P, 2, BLK])
        ctx_acc = sb("ctx_acc", [P, 2, BLK])
        ctx_out = sb("ctx_out", [P, 3, BLK], F32R)
        tail_hi = sb("tail_hi", [P, BLK], F32R)
        neg_max = sb("neg_max", [P, 3, QI])
        s_ps = psum("s_ps", [P, 3, 512])
        t_ps = psum("t_ps", [P, 2, 512])
        o_ps = psum("o_ps", [P, 2, 512])
        r_ps = psum("r_ps", [P, 512])

        const_loaded, const_hi, const_ready = sem("const_loaded"), sem("const_hi"), sem("const_ready")
        head_loaded = [sem(f"head_loaded{h}") for h in range(2)]
        v_loaded = [sem(f"v_loaded{h}") for h in range(2)]
        rel_done, rows_hi_ready, rows_ready = sem("rel_done"), sem("rows_hi_ready"), sem("rows_ready")
        scored, maxed, exped = sem("scored"), sem("maxed"), sem("exped")
        turned, pt_rounded, pt_ready = sem("turned"), sem("pt_rounded"), sem("pt_ready")
        item_done, item_free = sem("item_done"), sem("item_free")
        ctx_loaded, ctx_ready, ctx_stored, pool_self = sem("ctx_loaded"), sem("ctx_ready"), sem("ctx_stored"), sem("pool_self")
        block = ctx.enter_context(nc.Block())

        ITEMS = 2 * B
        PER = ITEMS * len(UNITS)
        HALF = PER // 2
        LOADS = 16 * 7
        PASSES = SH // 2

        def unit(n):
            return n // HALF % 2, n // len(UNITS) % B, UNITS[n % len(UNITS)]

        def passes(eng, prologue, body):
            prologue()
            with eng.Fori(0, PASSES - 1) as it:
                body(it, False)
            body(PASSES - 1, True)

        @block.sync
        def _(sp):
            def load(slot, head, channel):
                for stack, split, parts in ((q_st, q_split, (0, 0, 1)), (k_st, k_split, (0, 1, 0))):
                    for j, part in enumerate(parts):
                        sp.dma_start(stack[slot][SD * j:SD * (j + 1), :].bitcast(F32),
                                     split[part, bass.ds(channel, SD), :]).then_inc(head_loaded[slot], 16)
                rel = a["rel_bias"][bass.ds(head, 1)].rearrange("o i (r j) -> (o i) r j", r=1)
                sp.dma_start(rel_st[slot][:], rel.to_broadcast([BIAS_S, 3, BIAS_S])).then_inc(head_loaded[slot], 16)

            def load_v(slot, col):
                sp.dma_start(v_st[slot][:].bitcast(F32), v_split[:, :, bass.ds(col, SLOT_ROWS)].bitcast(F32)).then_inc(v_loaded[slot], 16)

            for slot in range(2):
                load(slot, slot, SD * slot)
                load_v(slot, SLOT_ROWS * slot)
            with sp.Fori(0, PASSES - 1) as it:
                for slot in range(2):
                    head, channel, col = [sp.snap(it * (2 * w) + (2 + slot) * w) for w in (1, SD, SLOT_ROWS)]
                    scored_all, weighed_all = sp.snap(it * PER + HALF * (slot + 1)), sp.snap(it * ITEMS + B * (slot + 1))
                    sp.wait_ge(scored, scored_all)
                    load(slot, head, channel)
                    sp.wait_ge(item_done, weighed_all)
                    load_v(slot, col)

        @block.gpsimd
        def _(pool):
            chain = Chain(pool, pool_self)
            for b in range(NB):
                cols = slice(BLK * b, BLK * (b + 1))
                if b >= 1:
                    pool.wait_ge(ctx_ready, b)
                pool.dma_start(ctx_in[:, 0, :], a["ctxT"][0:P, cols]).then_inc(ctx_loaded, 16)
                for d in range(2):
                    pool.dma_start(ctx_in[TAIL * d:TAIL * (d + 1), 1, :], a["ctxT"][P:CD, cols]).then_inc(ctx_loaded, 16)
                if b >= 1:
                    pool.wait_ge(ctx_stored, 16 * b)
                pool.wait_ge(ctx_loaded, 48 * (b + 1))
                chain(pool.tensor_copy(ctx_out[:, 0, :], ctx_in[:, 0, :]))
                chain.wait()
                chain(pool.tensor_copy(ctx_out[0:TAIL, 2, :], ctx_in[0:TAIL, 1, :]))
                chain.wait()
                chain(pool.tensor_copy(tail_hi[TAIL:, :], ctx_in[TAIL:, 1, :]))
                chain.wait()
                if b == 0:
                    chain(pool.tensor_copy(ctx_acc[:], ctx_in[:]))
                else:
                    chain(pool.tensor_tensor(ctx_acc[:], ctx_acc[:], ctx_in[:], ALU.add))
                chain.wait()
                chain(pool.tensor_tensor(ctx_out[:, 1, :], ctx_in[:, 0, :], ctx_out[:, 0, :].bitcast(F32), ALU.subtract))
                chain.wait()
                pool.tensor_tensor(ctx_out[TAIL:, 2, :], ctx_in[TAIL:, 1, :], tail_hi[TAIL:, :].bitcast(F32),
                                   ALU.subtract).then_inc(ctx_ready, 1)
                pool.wait_ge(ctx_ready, b + 1)
                pool.dma_start(ctx_split[b], ctx_out[:].bitcast(F32)).then_inc(ctx_stored, 16)
            pool.wait_ge(ctx_stored, 16 * NB)

        @block.tensor
        def _(pe):
            def relative_rows(it, slot):
                pe.wait_ge(head_loaded[slot % 2], it * LOADS + (slot // 2 + 1) * LOADS)
                pe.matmul(r_ps[0:REL_STACK, :], rel_st[slot % 2][:].rearrange("i j c -> i (j c)"), interp[:],
                          start=True, stop=True).then_inc(rel_done, 1)

            def scores(it, n):
                slot, b, tiles = unit(n)
                if n % HALF == 0:
                    pe.wait_ge(rows_ready, it * 2 + (n // HALF + 1))
                if n >= 3:
                    pe.wait_ge(exped, it * PER + (n - 2))
                for i, c0 in tiles:
                    w = P * (i + 1)
                    q0 = N * b + P * i
                    pe.matmul(s_ps[:, n % 3, c0:c0 + w], rows_st[slot][:, P * i:P * (i + 1)], key_st[:, 0:w],
                              start=True, stop=False)
                    pe.matmul(s_ps[:, n % 3, c0:c0 + w], q_st[slot][:, q0:q0 + P], k_st[slot][:, N * b:N * b + w],
                              start=False, stop=False)
                    last = pe.matmul(s_ps[:, n % 3, c0 + w - P:c0 + w], ident_r[:], mask[:], start=False, stop=True)
                last.then_inc(scored, 1)

            def turn(it, n):
                pe.wait_ge(exped, it * PER + (n + 1))
                if n >= 2:
                    pe.wait_ge(pt_ready, it * PER + (n - 1))
                for i, c0 in unit(n)[2]:
                    for j in range(i + 1):
                        cols = slice(c0 + P * j, c0 + P * (j + 1))
                        last = pe.transpose(t_ps[:, n % 2, cols], probs[:, n % 4, cols], ident[:])
                last.then_inc(turned, 1)

            def weigh(it, n):
                slot, b, tiles = unit(n)
                item = n // len(UNITS)
                if n % HALF == 0:
                    pe.wait_ge(v_loaded[slot], it * 16 + 16)
                if n % len(UNITS) == 0:
                    pe.wait_ge(item_free, it * ITEMS + (item + 1))
                pe.wait_ge(pt_ready, it * PER + (n + 1))
                for i, c0 in tiles:
                    for j in range(i + 1):
                        queries, cols = slice(P * i, P * (i + 1)), slice(c0 + P * j, c0 + P * (j + 1))
                        for pt in (pt_hi, pt_lo):
                            last = pe.matmul(o_ps[0:SLOT_ROWS, item % 2, queries], v_st[slot][:, QI * b + j, :],
                                             pt[:, n % 3, cols], start=pt is pt_hi and j == 0, stop=pt is pt_lo and j == i)
                if n % len(UNITS) == len(UNITS) - 1:
                    last.then_inc(item_done, 1)

            def prologue():
                pe.wait_ge(const_ready, 1)
                relative_rows(0, 0)
                for n in range(3):
                    scores(0, n)
                for n in range(2):
                    scores(0, n + 3)
                    turn(0, n)

            def body(it, last):
                for n in range(PER):
                    if n == 3:
                        relative_rows(it, 1)
                    if n == HALF + 3 and not last:
                        relative_rows(it, 2)
                    if n + 5 < PER or not last:
                        scores(it, n + 5)
                    if n + 2 < PER or not last:
                        turn(it, n + 2)
                    weigh(it, n)

            passes(pe, prologue, body)

        @block.scalar
        def _(act):
            def relative_rows(it, slot):
                act.wait_ge(rel_done, it * 2 + (slot + 1))
                act.copy(rows_st[slot % 2][0:2 * BIAS_S, :], r_ps[0:2 * BIAS_S, :])
                act.copy(rows_hi[2 * BIAS_S:, :], r_ps[2 * BIAS_S:REL_STACK, :]).then_inc(rows_hi_ready, 1)

            def exponents(it, n):
                slot, b, tiles = unit(n)
                act.wait_ge(maxed, it * PER + (n + 1))
                if n >= 4:
                    act.wait_ge(turned, it * PER + (n - 3))
                for i, c0 in tiles:
                    w = P * (i + 1)
                    total = exp_sums[:, bass.ds(it * 2 * NT + (n // HALF * NT + QI * b + i), 1)]
                    last = act.activation(probs[:, n % 4, c0:c0 + w], s_ps[:, n % 3, c0:c0 + w], ACT.Exp,
                                          bias=neg_max[:, n % 3, i:i + 1], accum_out=total)
                last.then_inc(exped, 1)

            def round_turned(it, n):
                w = sum(P * (i + 1) for i, _ in unit(n)[2])
                act.wait_ge(turned, it * PER + (n + 1))
                act.copy(pt_hi[:, n % 3, 0:w], t_ps[:, n % 2, 0:w]).then_inc(pt_rounded, 1)

            def prologue():
                act.dma_start(interp3[:], a["interp3"]).then_inc(const_loaded, 16)
                act.dma_start(interp[:], a["interp"]).then_inc(const_loaded, 16)
                act.dma_start(mask_raw[:], a["causal"]).then_inc(const_loaded, 16)
                act.wait_ge(const_loaded, 16 * 3)
                act.copy(key_hi[:], interp3[:])
                act.copy(key_st[0:BIAS_S, :], interp3[0:BIAS_S, :])
                act.copy(key_st[2 * BIAS_S:, :], interp3[2 * BIAS_S:, :])
                act.copy(mask[:], mask_raw[:])
                act.copy(ident_r[:], ident[:]).then_inc(const_hi, 1)
                relative_rows(0, 0)
                for n in range(3):
                    exponents(0, n)
                for n in range(2):
                    round_turned(0, n)
                    exponents(0, n + 3)

            def body(it, last):
                for n in range(PER):
                    if n == 3:
                        relative_rows(it, 1)
                    if n == HALF + 3 and not last:
                        relative_rows(it, 2)
                    if n + 2 < PER or not last:
                        round_turned(it, n + 2)
                    if n + 5 < PER or not last:
                        exponents(it, n + 5)

            passes(act, prologue, body)

        @block.vector
        def _(dve):
            def relative_rows(it, slot):
                dve.wait_ge(rows_hi_ready, it * 2 + (slot + 1))
                dve.tensor_tensor(rows_st[slot % 2][2 * BIAS_S:, :], r_ps[2 * BIAS_S:REL_STACK, :],
                                  rows_hi[2 * BIAS_S:, :].bitcast(F32), ALU.subtract).then_inc(rows_ready, 1)

            def maxima(it, n):
                dve.wait_ge(scored, it * PER + (n + 1))
                for i, c0 in unit(n)[2]:
                    last = dve.tensor_reduce(neg_max[:, n % 3, i:i + 1], s_ps[:, n % 3, c0:c0 + P * (i + 1)],
                                             AX.X, ALU.max, negate=True)
                last.then_inc(maxed, 1)

            def rest_of_turned(it, n):
                w = sum(P * (i + 1) for i, _ in unit(n)[2])
                dve.wait_ge(pt_rounded, it * PER + (n + 1))
                dve.tensor_tensor(pt_lo[:, n % 3, 0:w], t_ps[:, n % 2, 0:w], pt_hi[:, n % 3, 0:w].bitcast(F32),
                                  ALU.subtract).then_inc(pt_ready, 1)

            def store_item(it, item):
                slot, b = item // B, item % B
                dve.wait_ge(item_done, it * ITEMS + (item + 1))
                dve.tensor_copy(attn_t[SLOT_ROWS * slot:SLOT_ROWS * (slot + 1), bass.ds(it * T + N * b, N)],
                                o_ps[0:SLOT_ROWS, item % 2, :]).then_inc(item_free, 1)

            def prologue():
                dve.wait_ge(const_hi, 1)
                dve.tensor_tensor(key_st[BIAS_S:2 * BIAS_S, 0:N // 2], interp3[BIAS_S:2 * BIAS_S, 0:N // 2],
                                  key_hi[BIAS_S:2 * BIAS_S, 0:N // 2].bitcast(F32), ALU.subtract).then_inc(item_free, 2)
                dve.tensor_tensor(key_st[BIAS_S:2 * BIAS_S, N // 2:], interp3[BIAS_S:2 * BIAS_S, N // 2:],
                                  key_hi[BIAS_S:2 * BIAS_S, N // 2:].bitcast(F32), ALU.subtract).then_inc(const_ready, 1)
                relative_rows(0, 0)
                for n in range(3):
                    maxima(0, n)
                for n in range(2):
                    maxima(0, n + 3)
                    rest_of_turned(0, n)

            def body(it, last):
                for n in range(PER):
                    if n == 3:
                        relative_rows(it, 1)
                    if n == HALF + 3 and not last:
                        relative_rows(it, 2)
                    if n + 5 < PER or not last:
                        maxima(it, n + 5)
                    if n + 2 < PER or not last:
                        rest_of_turned(it, n + 2)
                    if n % len(UNITS) == len(UNITS) - 1:
                        store_item(it, n // len(UNITS))

            passes(dve, prologue, body)
            dve.wait_ge(ctx_ready, NB)
            dve.tensor_reduce(ctx_sum[:, 0:1], ctx_acc[:, 0, :], AX.X, ALU.add)
            dve.tensor_reduce(ctx_sum[0:TAIL, 1:2], ctx_acc[0:TAIL, 1, :], AX.X, ALU.add)


def self_output(nc, a, x, ident, attn_t, exp_sums):
    with ExitStack() as ctx:
        def sb(name, shape, dt=F32):
            return ctx.enter_context(nc.sbuf_tensor(name, shape, dt))

        def sem(name):
            return ctx.enter_context(nc.semaphore(name))

        w_raw = sb("wo_raw", [P, CH, C])
        w_hi, w_lo = sb("wo_hi", [P, CH, C], F32R), sb("wo_lo", [P, CH, C], F32R)
        bo = sb("bo", [P, C])
        inv_sums = sb("inv_sums", [P, SH, NT])
        total, attn = sb("total", [P, 2, C]), sb("attn", [P, 2, C])
        o_hi, o_lo = sb("so_hi", [P, 2, CH, P], F32R), sb("so_lo", [P, 2, CH, P], F32R)
        a_ps = ctx.enter_context(nc.psum_tensor("so_a", [P, 2, 512], F32))
        t_ps = ctx.enter_context(nc.psum_tensor("so_t", [P, 2, 512], F32))
        y_ps = ctx.enter_context(nc.psum_tensor("so_y", [P, 2, 512], F32))
        loaded, w_hi_ready, w_ready = sem("so_loaded"), sem("so_w_hi"), sem("so_w")
        summed = sem("so_summed")
        token_major, inverted, divided = sem("so_token_major"), sem("so_inverted"), sem("so_divided")
        turned, hi_ready, lo_ready = sem("so_turned"), sem("so_hi_ready"), sem("so_lo_ready")
        projected, biased, added = sem("so_projected"), sem("so_biased"), sem("so_added")
        block = ctx.enter_context(nc.Block())
        PAIR = 2 * SLOT_ROWS

        @block.sync
        def _(sp):
            sp.dma_start(w_raw[:], a["WoT"].rearrange("(h p) o -> p h o", p=P)).then_inc(loaded, 16)
            sp.dma_start(bo[:], a["bo"].rearrange("(a c) -> a c", a=1).to_broadcast([P, C])).then_inc(loaded, 16)

        @block.gpsimd
        def _(pool):
            pool.wait_ge(loaded, 32)
            for t in range(NT):
                pool.tensor_tensor(x[:, t, :], x[:, t, :], bo[:], ALU.add).then_inc(biased, 1)

        @block.scalar
        def _(act):
            act.wait_ge(loaded, 32)
            act.copy(flat(w_hi[:]), flat(w_raw[:])).then_inc(w_hi_ready, 1)
            for t in range(NT):
                act.wait_ge(turned, t + 1)
                if t >= 2:
                    act.wait_ge(projected, t - 1)
                act.copy(flat(o_hi[:, t % 2]), t_ps[:, t % 2, 0:C]).then_inc(hi_ready, 1)

        @block.vector
        def _(dve):
            dve.reciprocal(inv_sums[:].rearrange("p h t -> p (h t)"), exp_sums[:]).then_inc(inverted, 1)

            def divide(t):
                dve.wait_ge(token_major, t + 1)
                if t >= 2:
                    dve.wait_ge(turned, t - 1)
                parts = a_ps[:, t % 2, :].rearrange("p (h v d) -> p h d v", v=2, d=SD)
                halves = total[:, t % 2, :].rearrange("p (h d) -> p h d", d=SD)
                dve.tensor_reduce(halves, parts, AX.X, ALU.add).then_inc(summed, 1)
                dve.wait_ge(summed, t + 1)
                dve.tensor_tensor(attn[:, t % 2, :].rearrange("p (h d) -> p h d", d=SD), halves,
                                  inv_sums[:, :, t:t + 1].to_broadcast([P, SH, SD]), ALU.mult).then_inc(divided, 1)

            dve.wait_ge(inverted, 1)
            divide(0)
            dve.wait_ge(w_hi_ready, 1)
            dve.tensor_tensor(flat(w_lo[:]), flat(w_raw[:]), flat(w_hi[:]).bitcast(F32), ALU.subtract).then_inc(w_ready, 1)
            divide(1)
            for t in range(NT + 1):
                if t < NT:
                    dve.wait_ge(hi_ready, t + 1)
                    if t >= 2:
                        dve.wait_ge(projected, t - 1)
                    dve.tensor_tensor(flat(o_lo[:, t % 2]), t_ps[:, t % 2, 0:C], flat(o_hi[:, t % 2]).bitcast(F32),
                                      ALU.subtract).then_inc(lo_ready, 1)
                if t + 2 < NT:
                    divide(t + 2)
                if t >= 1:
                    dve.wait_ge(projected, t)
                    dve.wait_ge(biased, t)
                    dve.tensor_tensor(x[:, t - 1, :], x[:, t - 1, :], y_ps[:, (t - 1) % 2, 0:C], ALU.add).then_inc(added, 1)

        @block.tensor
        def _(pe):
            def to_token_major(t):
                if t >= 2:
                    pe.wait_ge(divided, t - 1)
                for pair in range(SH // 2):
                    last = pe.transpose(a_ps[:, t % 2, PAIR * pair:PAIR * (pair + 1)],
                                        attn_t[:, T * pair + P * t:T * pair + P * (t + 1)], ident[0:PAIR, 0:PAIR])
                last.then_inc(token_major, 1)

            def turn(t):
                pe.wait_ge(divided, t + 1)
                if t >= 2:
                    pe.wait_ge(lo_ready, t - 1)
                for h in range(CH):
                    last = pe.transpose(t_ps[:, t % 2, P * h:P * (h + 1)], attn[:, t % 2, P * h:P * (h + 1)], ident[:])
                last.then_inc(turned, 1)

            to_token_major(0)
            to_token_major(1)
            turn(0)
            pe.wait_ge(w_ready, 1)
            for t in range(NT):
                if t + 2 < NT:
                    to_token_major(t + 2)
                if t + 1 < NT:
                    turn(t + 1)
                pe.wait_ge(lo_ready, t + 1)
                if t >= 2:
                    pe.wait_ge(added, t - 1)
                passes = [(os, ws, h) for h in range(CH) for os, ws in ((o_hi, w_hi), (o_hi, w_lo), (o_lo, w_hi))]
                for i, (os, ws, h) in enumerate(passes):
                    last = pe.matmul(y_ps[:, t % 2, 0:C], os[:, t % 2, h, :], ws[:, h, :], start=i == 0,
                                     stop=i == len(passes) - 1)
                last.then_inc(projected, 1)


class CrossStreams:

    def __init__(self, nc, ctx, a, ctx_split):
        def sb(name, shape, dt=F32):
            return ctx.enter_context(nc.sbuf_tensor(name, shape, dt))

        def sem(name):
            return ctx.enter_context(nc.semaphore(name))

        self.a, self.ctx_split = a, ctx_split
        self.blocks = sb("blocks", [P, 4, 3, BLK], F32R)
        self.wq_raw = sb("wq_raw", [P, CH * XD])
        self.kv_raw = sb("kv_raw", [P, 4 * XD])
        self.kv_loaded, self.wq_loaded = sem("kv_loaded"), sem("wq_loaded")
        self.blocks_loaded = [sem(f"blocks_loaded{s}") for s in range(2)]

    def load_kv(self, sp, col):
        for n, name in enumerate(("XWk", "XWv")):
            w = self.a[name][:, bass.ds(col, XD)]
            sp.dma_start(self.kv_raw[:, 2 * XD * n:2 * XD * n + XD], w[0:P, :]).then_inc(self.kv_loaded, 16)
            for d in range(2):
                sp.dma_start(self.kv_raw[TAIL * d:TAIL * (d + 1), 2 * XD * n + XD:2 * XD * (n + 1)],
                             w[P:CD, :]).then_inc(self.kv_loaded, 16)

    def load_wq(self, sp, col):
        for k in range(CH):
            sp.dma_start(self.wq_raw[:, XD * k:XD * (k + 1)],
                         self.a["XWq"][P * k:P * (k + 1), bass.ds(col, XD)]).then_inc(self.wq_loaded, 16)

    def load_blocks(self, sp, pair):
        for b in (2 * pair, 2 * pair + 1):
            sp.dma_start(self.blocks[:, b % 4].bitcast(F32), self.ctx_split[b]).then_inc(self.blocks_loaded[pair % 2], 16)


def cross_prepare(nc, a, x, ident, x2_split, ctx_sum, k_shift, streams):
    with ExitStack() as ctx:
        def sb(name, shape, dt=F32):
            return ctx.enter_context(nc.sbuf_tensor(name, shape, dt))

        def sem(name):
            return ctx.enter_context(nc.semaphore(name))

        y = sb("y2", [P, NT, C])
        parts, mv = sb("parts2", [P, NT, 6]), sb("mv2b", [P, NT, 2])
        var_eps, root = sb("var_eps2", [P, NT]), sb("root2", [P, NT])
        rstd, tmp = sb("rstd2", [P, NT]), sb("tmp2", [P, NT])
        bout = sb("bout", [P, C])
        wk_main, wk_tail = sb("wk_main", [P, XH * XD]), sb("wk_tail", [TAIL, XH * XD])
        xq_out = sb("xq_out", [P, G, 2, CH, GQ], F32R)
        banks = ctx.enter_context(nc.psum_tensor("banks2", [P, 4, 512], F32))
        mean_ps = ctx.enter_context(nc.psum_tensor("mean_ps", [P, 512], F32))

        small_loaded = sem("small_loaded2")
        var_ready, root_ready, y_ready = sem("var_ready2"), sem("root_ready2"), sem("y_ready")
        dve_self = sem("dve_self2")
        xq_stored = sem("xq_stored")
        means_done = sem("means_done")
        turned, xq_hi, xq_lo = sem("turned2"), sem("xq_hi"), sem("xq_lo")
        block = ctx.enter_context(nc.Block())

        @block.sync
        def _(sp):
            sp.dma_start(wk_main[:], a["XWk"][0:P, :]).then_inc(small_loaded, 16)
            sp.dma_start(wk_tail[:], a["XWk"][P:CD, :]).then_inc(small_loaded, 16)
            sp.dma_start(bout[:], a["Xbout"].rearrange("(a c) -> a c", a=1).to_broadcast([P, C])).then_inc(small_loaded, 16)
            streams.load_kv(sp, 0)
            streams.load_wq(sp, 0)
            for pair in range(2):
                streams.load_blocks(sp, pair)
            for g in range(G):
                sp.wait_ge(xq_hi, g + 1)
                sp.wait_ge(xq_lo, g + 1)
                sp.dma_start(x2_split[g], xq_out[:, g].bitcast(F32)).then_inc(xq_stored, 16)
            sp.wait_ge(xq_stored, 16 * G)

        @block.gpsimd
        def _(pool):
            pool.wait_ge(small_loaded, 48)
            for t in range(NT):
                pool.wait_ge(y_ready, t + 1)
                pool.tensor_tensor(x[:, t, :], x[:, t, :], bout[:], ALU.add)

        @block.vector
        def _(dve):
            chain = Chain(dve, dve_self)
            row_moments(dve, chain, x, parts, mv)
            inverse_root_seed(dve, chain, mv, var_eps, var_ready)
            dve.wait_ge(root_ready, 1)
            inverse_root(dve, chain, var_eps[:], root[:], rstd[:], tmp)
            for t in range(NT):
                dve.tensor_scalar(y[:, t, :], x[:, t, :], mv[:, t, 0:1], rstd[:, t:t + 1],
                                  ALU.subtract, ALU.mult).then_inc(y_ready, 1)
            for g in range(G):
                dve.wait_ge(xq_hi, g + 1)
                dve.tensor_tensor(flat(xq_out[:, g, 1]), banks[:, g % 4, :], flat(xq_out[:, g, 0]).bitcast(F32),
                                  ALU.subtract).then_inc(xq_lo, 1)
            dve.wait_ge(means_done, 1)
            dve.tensor_scalar(k_shift[:], mean_ps[:, 0:XH], -1.0 / (3.0 * KEYS), None, ALU.mult)

        @block.scalar
        def _(act):
            act.wait_ge(var_ready, 1)
            act.activation(root[:], var_eps[:], ACT.Sqrt).then_inc(root_ready, 1)
            for g in range(G):
                act.wait_ge(turned, g + 1)
                act.copy(flat(xq_out[:, g, 0]), banks[:, g % 4, :]).then_inc(xq_hi, 1)

        @block.tensor
        def _(pe):
            pe.wait_ge(small_loaded, 48)
            for h in range(XH):
                pe.matmul(mean_ps[:, h:h + 1], wk_main[:, XD * h:XD * (h + 1)], ctx_sum[:, 0:1], start=True, stop=False)
                last = pe.matmul(mean_ps[:, h:h + 1], wk_tail[:, XD * h:XD * (h + 1)], ctx_sum[0:TAIL, 1:2],
                                 start=False, stop=True)
            last.then_inc(means_done, 1)
            for g in range(G):
                pe.wait_ge(y_ready, 2 * g + 2)
                if g >= 4:
                    pe.wait_ge(xq_lo, g - 3)
                for h in range(CH):
                    for t in range(2):
                        last = pe.transpose(banks[:, g % 4, GQ * h + P * t:GQ * h + P * (t + 1)],
                                            y[:, 2 * g + t, P * h:P * (h + 1)], ident[:])
                last.then_inc(turned, 1)


PIECES = KEYS // (2 * P)
IS_CHUNK = ("A", "A+", "out", "Q+", "K+", "V+", "V")


def with_pieces(extra, ahead=()):
    items = list(ahead)
    for c in range(PIECES):
        items.append(("T", c))
        if c >= 2:
            items.append(("W", c - 2))
        items += extra.get(c, [])
    return items + [("W", PIECES - 2), ("W", PIECES - 1)]


def exponents(t, first):
    return {first + i: [("E", t, i)] for i in range(4)}


def merged(*parts):
    out = {}
    for part in parts:
        for c, items in part.items():
            out[c] = out.get(c, []) + items
    return out


STEP_0 = [("M", 0), ("A", 1, 1), ("E", 0, 0), ("E", 0, 1), ("V", 1), ("A", 1, 2), ("E", 0, 2), ("V", 0), ("A", 1, 3),
          ("E", 0, 3), ("M", 1), ("V", 3), ("E", 1, 0), ("Q+",), ("E", 1, 1), ("V", 2), ("A+", 0, 0), ("E", 1, 2),
          ("A+", 0, 1), ("E", 1, 3), ("A+", 0, 2)]
SCORES = {0: [("A", 0, 3)], 1: [("M", 0), ("I",)], 2: [("A", 1, 0)], 4: [("A", 1, 1)], 6: [("A", 1, 2)],
          8: [("A", 1, 3)], 9: [("M", 1)]}
EXPS = merged(exponents(0, 3), exponents(1, 10))
AHEAD = {7: [("Q+",)], 12: [("A+", 0, 0)], 14: [("A+", 0, 1)], 15: [("A+", 0, 2)]}
OUT = {10: [("out",)]}
STEP_1 = with_pieces(merged(SCORES, EXPS, AHEAD, {5: [("wkv",)], 9: [("wo",)]}))
LAST_1 = with_pieces(merged(SCORES, EXPS, AHEAD, {9: [("wo",)]}))
STEP = with_pieces(merged(SCORES, EXPS, AHEAD, OUT), [("O",)])
STEP_7 = with_pieces(merged(SCORES, EXPS, OUT, {9: [("wq",)], 11: [("K+", 0)], 13: [("K+", 1)], 15: [("Q+",)]}), [("O",)])
STEP_8 = with_pieces({0: [("K+", 2)], 1: [("I",)], 2: [("K+", 3)], 4: [("out",)], 6: [("A", 0, 0)],
                      8: [("A", 0, 1)], 10: [("A", 0, 2)], 12: [("A", 0, 3)], 13: [("V+", 4)], 15: [("V+", 5)]}, [("O",)])
AFTER = [("V+", 7), ("O",), ("V+", 6), ("A+", 1, 0), ("out",)]
LAST_7 = with_pieces(merged(SCORES, EXPS, OUT), [("O",)])
LAST_8 = with_pieces({1: [("I",)], 4: [("out",)]}, [("O",)])
LAST_AFTER = [("O",), ("out",)]
BEFORE = [("wkv",), ("wq",), ("K+", 0), ("K+", 1), ("K+", 2), ("Q+",), ("K+", 3), ("A+", 0, 0), ("A+", 0, 1), ("A+", 0, 2),
          ("A+", 0, 3), ("V+", 4), ("V+", 5), ("V+", 7), ("V+", 6), ("A+", 1, 0)]


def chunks_in(items):
    return sum(item[0] in IS_CHUNK for item in items)


FIRST = chunks_in(BEFORE)
LOOPED = (G - 4) // 2
STEP_AT = [0, chunks_in(STEP_0)]
for _g in range(2, G):
    STEP_AT.append(STEP_AT[-1] + chunks_in(STEP_1 if _g == 2 else STEP))
STEP_AT.append(STEP_AT[-1] + chunks_in(STEP_7))
AFTER_AT = STEP_AT[G] + chunks_in(STEP_8)
PER_HEAD = AFTER_AT + chunks_in(AFTER)
LAST_AT = [STEP_AT[G - 1], STEP_AT[G - 1] + chunks_in(LAST_7)]
LAST_AT.append(LAST_AT[1] + chunks_in(LAST_8))
ALL_CHUNKS = FIRST + (XH - 1) * PER_HEAD + LAST_AT[2] + chunks_in(LAST_AFTER)
assert PER_HEAD % 2 == 0 and chunks_in(STEP) % 2 == 0


def chunk_of(items, item):
    return chunks_in(items[:items.index(item)])


def run_heads(eng, run):
    run(BEFORE, -1, -1, -1, 1, 0, 0)

    def head(h, last):
        def step(items, g, at):
            run(items, h, g, h * G + g, g % 2, h * PER_HEAD + (FIRST + at), (FIRST + at) % 2)

        step(STEP_0, 0, STEP_AT[0])
        step(LAST_1 if last else STEP_1, 1, STEP_AT[1])
        with eng.Fori(0, LOOPED) as p:
            for u in range(2):
                run(STEP, h, p * 2 + (2 + u), h * G + p * 2 + (2 + u), u,
                    h * PER_HEAD + p * (STEP_AT[4] - STEP_AT[2]) + (FIRST + STEP_AT[2 + u]), (FIRST + STEP_AT[2 + u]) % 2)
        for g in range(2 + 2 * LOOPED, G - 1):
            step(STEP, g, STEP_AT[g])
        if last:
            for n, items in enumerate((LAST_7, LAST_8, LAST_AFTER)):
                step(items, G - 1 + n, LAST_AT[n])
        else:
            step(STEP_7, G - 1, STEP_AT[G - 1])
            step(STEP_8, G, STEP_AT[G])
            step(AFTER, G + 1, AFTER_AT)

    with eng.Fori(0, XH - 1) as h:
        head(h, False)
    head(XH - 1, True)


def cross_attention(nc, a, x, ident, x2_split, k_shift, streams):
    with ExitStack() as ctx:
        def sb(name, shape, dt=F32):
            return ctx.enter_context(nc.sbuf_tensor(name, shape, dt))

        def sem(name):
            return ctx.enter_context(nc.semaphore(name))

        k_hi, k_lo = sb("k_hi", [P, KEYS], F32R), sb("k_lo", [P, KEYS], F32R)
        v_hi, v_lo = sb("v_hi", [P, KEYS], F32R), sb("v_lo", [P, KEYS], F32R)
        probs = sb("xprobs", [P, 2, 2, KEYS])
        blocks, wq_raw, kv_raw = streams.blocks, streams.wq_raw, streams.kv_raw
        pt_hi, pt_lo = sb("pt_hi", [P, 3, 2 * GQ], F32R), sb("pt_lo", [P, 3, 2 * GQ], F32R)
        xq = sb("xq", [P, 2, CH, GQ], F32R)
        q_hi, q_lo = sb("q_hi", [P, 2, GQ], F32R), sb("q_lo", [P, 2, GQ], F32R)
        o_hi, o_lo = sb("o_hi", [P, GQ], F32R), sb("o_lo", [P, GQ], F32R)
        wq_hi, wq_lo = sb("wq_hi", [P, CH * XD], F32R), sb("wq_lo", [P, CH * XD], F32R)
        kv_split = sb("kv_split", [P, 4, 2, XD], F32R)
        wo_raw, wo_hi, wo_lo = sb("wo_raw2", [P, C]), sb("wo_hi2", [P, C], F32R), sb("wo_lo2", [P, C], F32R)
        v_rest = sb("v_rest", [P, 2, BLK // 2])
        shift = sb("shift", [P, 1])
        chunk_max, neg_max = sb("chunk_max", [P, 2, 4]), sb("xneg_max", [P, 2, 2])
        chunk_sum, denom, inv = sb("chunk_sum", [P, 2, 2, 4]), sb("denom", [P, 2]), sb("xinv", [P, 2, 2])
        s_ps = ctx.enter_context(nc.psum_tensor("xs_ps", [P, 2, CHUNK], F32))
        t_ps = ctx.enter_context(nc.psum_tensor("xt_ps", [P, 3, 2 * GQ], F32))
        o_ps = ctx.enter_context(nc.psum_tensor("xo_ps", [P, 512], F32))

        kv_loaded, wq_loaded, wo_loaded = streams.kv_loaded, streams.wq_loaded, sem("wo_loaded")
        kv_w_hi, wq_w_hi, wo_w_hi = sem("kv_w_hi"), sem("wq_w_hi"), sem("wo_w_hi")
        kv_w, wq_w, wo_w = sem("kv_w"), sem("wq_w"), sem("wo_w")
        blocks_loaded = streams.blocks_loaded
        xq_loaded = sem("xq_loaded")
        filled, freed = sem("filled"), sem("freed")
        kv_half = sem("kv_half")
        kv_rounded = sem("kv_rounded")
        v_rest_ready = sem("v_rest_ready")
        q_rounded, q_ready = sem("q_rounded"), sem("q_ready")
        maxed, exped, summed, inv_ready = sem("xmaxed"), sem("xexped"), sem("summed"), sem("xinv_ready")
        turned, t_rounded, t_ready = sem("xturned"), sem("t_rounded"), sem("t_ready")
        weighed = sem("xweighed")
        o_done, o_rounded, o_ready = sem("o_done"), sem("o_rounded"), sem("o_ready")
        shifted = sem("shifted")
        block = ctx.enter_context(nc.Block())

        KV_ORDER = [("K+", i) for i in range(4)] + [("V+", b) for b in (4, 5, 7, 6)] + [("V", b) for b in (1, 0, 3, 2)]

        def v_half(b, half, bank):
            k0 = BLK * b + BLK // 2 * half
            return slice(k0, k0 + BLK // 2), bank.rearrange("p (t w d) -> p t w d", w=2, d=XD)

        def kv_count(item, h):
            return (h if item[0] == "V" else h + 1) * len(KV_ORDER) + (KV_ORDER.index(item) + 1)

        @block.sync
        def _(sp):
            def load_queries(group):
                sp.dma_start(xq[:].bitcast(F32), x2_split[bass.ds(group, 1)].rearrange("o p s k q -> (o p) s k q")).then_inc(xq_loaded, 16)

            load_queries(0)
            sp.wait_ge(filled, 1)
            streams.load_blocks(sp, 2)
            sp.wait_ge(filled, 2)
            streams.load_blocks(sp, 3)
            sp.wait_ge(q_ready, 1)
            load_queries(1)
            for pair, last_v in ((2, ("V+", 5)), (3, ("V+", 6))):
                sp.wait_ge(filled, chunk_of(BEFORE, last_v) + 1)
                streams.load_blocks(sp, pair - 2)

            def head(h, last):
                def value(v):
                    return v if last else sp.snap(v)

                start = value(h * PER_HEAD + FIRST)
                wo_col = value(h * XD)
                q_base = value(h * G)
                if not last:
                    next_col = sp.snap(h * XD + XD)
                sp.wait_ge(filled, start)
                if not last:
                    streams.load_kv(sp, next_col)
                    streams.load_wq(sp, next_col)
                sp.dma_start(wo_raw[:], a["XWout"][bass.ds(wo_col, XD), :]).then_inc(wo_loaded, 16)
                with sp.Fori(1, G - 1) as g:
                    projected, group = sp.snap(q_base + g + 1), sp.snap(g + 1)
                    sp.wait_ge(q_ready, projected)
                    load_queries(group)
                if not last:
                    projected = [sp.snap(q_base + G + n) for n in range(2)]
                    used = [sp.snap(h * PER_HEAD + (FIRST + at + chunk_of(items, item) + 1))
                            for items, item, at in ((STEP_7, ("K+", 0), STEP_AT[G - 1]), (STEP_7, ("K+", 1), STEP_AT[G - 1]),
                                                    (STEP_8, ("V+", 5), STEP_AT[G]), (AFTER, ("V+", 6), AFTER_AT))]
                    sp.wait_ge(q_ready, projected[0])
                    load_queries(0)
                    for n, pair in enumerate((2, 3)):
                        sp.wait_ge(filled, used[n])
                        streams.load_blocks(sp, pair)
                    sp.wait_ge(q_ready, projected[1])
                    load_queries(1)
                    for n, pair in enumerate((0, 1)):
                        sp.wait_ge(filled, used[2 + n])
                        streams.load_blocks(sp, pair)

            with sp.Fori(0, XH - 1) as h:
                head(h, False)
            head(XH - 1, True)

        @block.tensor
        def _(pe):
            def project_k(i, h, buf):
                pe.wait_ge(blocks_loaded[i % 2], (h + 1) * 64 + 32 * (i // 2 + 1))
                passes = [(kv_split[:, 0, 0, :], 0, P), (kv_split[:, 0, 1, :], 0, P), (kv_split[:, 0, 0, :], 1, P),
                          (kv_split[:, 1, 0, :], 2, P), (kv_split[0:TAIL, 1, 1, :], 2, TAIL)]
                for b in (2 * i, 2 * i + 1):
                    for n, (weights, part, rows) in enumerate(passes):
                        last = pe.matmul(s_ps[:, buf, BLK * (b % 2):BLK * (b % 2 + 1)], weights, blocks[0:rows, b % 4, part, :],
                                         start=n == 0, stop=n == len(passes) - 1)
                    if b == 2 * i:
                        last.then_inc(kv_half, 1)
                return last

            def project_v(b, h, buf):
                if b < 4:
                    pe.wait_ge(blocks_loaded[b // 2], h * 64 + 96)
                for t in range(BLK // P):
                    for part in range(3):
                        weights = kv_split[:, 3 if part == 2 else 2].rearrange("p w d -> p (w d)")
                        last = pe.matmul(s_ps[:, buf, 2 * XD * t:2 * XD * (t + 1)], blocks[:, b % 4, part, P * t:P * (t + 1)],
                                         weights, start=part == 0, stop=part == 2)
                    if t == 1:
                        last.then_inc(kv_half, 1)
                return last

            def project_q(buf):
                passes = [(w, part, k) for k in range(CH) for w, part in ((wq_hi, 0), (wq_hi, 1), (wq_lo, 0))]
                for n, (w, part, k) in enumerate(passes):
                    last = pe.matmul(s_ps[:, buf, 0:GQ], w[:, XD * k:XD * (k + 1)], xq[:, part, k, :],
                                     start=n == 0, stop=n == len(passes) - 1)
                return last

            def scores(t, i, par, buf):
                for m, (q, k) in enumerate(((q_hi, k_hi), (q_hi, k_lo), (q_lo, k_hi))):
                    for b in range(2):
                        k0 = CHUNK * i + BLK * b
                        last = pe.matmul(s_ps[:, buf, BLK * b:BLK * (b + 1)], q[:, par, P * t:P * (t + 1)], k[:, k0:k0 + BLK],
                                         start=m == 0, stop=m == 2)
                return last

            def project_out(buf):
                for t in range(2):
                    for m, (o, w) in enumerate(((o_hi, wo_hi), (o_hi, wo_lo), (o_lo, wo_hi))):
                        last = pe.matmul(s_ps[:, buf, C * t:C * (t + 1)], o[:, P * t:P * (t + 1)], w[:], start=m == 0, stop=m == 2)
                return last

            def run(items, h, g, s, par, chunk, chunk_par):
                n = 0
                for item in items:
                    kind = item[0]
                    if kind in IS_CHUNK:
                        if items is not BEFORE or n >= 2:
                            pe.wait_ge(freed, chunk + (n - 1))
                        buf = (chunk_par + n) % 2
                        if kind == "A":
                            if item[1:] == (0, 0):
                                pe.wait_ge(q_ready, s + 1)
                            last = scores(item[1], item[2], par, buf)
                        elif kind == "A+":
                            if item[1:] == (0, 0):
                                pe.wait_ge(q_ready, s + 2)
                            last = scores(item[1], item[2], 1 - par, buf)
                        elif kind == "Q+":
                            if items is BEFORE or items is STEP_7:
                                pe.wait_ge(wq_w, h + 2)
                            pe.wait_ge(xq_loaded, s * 16 + 32)
                            last = project_q(buf)
                        elif kind == "out":
                            if items is STEP:
                                pe.wait_ge(wo_w, h + 1)
                            pe.wait_ge(o_ready, s - 1)
                            last = project_out(buf)
                        else:
                            if item == ("K+", 0):
                                pe.wait_ge(kv_w, h + 2)
                            last = (project_k if kind == "K+" else project_v)(item[1], h, buf)
                        last.then_inc(filled, 1)
                        n += 1
                    elif kind == "T":
                        c = item[1]
                        if c == 0:
                            pe.wait_ge(exped, s * 2)
                        if c >= 3:
                            pe.wait_ge(t_ready, s * PIECES + (c - 2 - PIECES))
                        for j in range(2):
                            for t in range(2):
                                last = pe.transpose(t_ps[:, c % 3, GQ * j + P * t:GQ * j + P * (t + 1)],
                                                    probs[:, 1 - par, t, P * (2 * c + j):P * (2 * c + j + 1)], ident[:])
                        last.then_inc(turned, 1)
                    elif kind == "W":
                        c = item[1]
                        if c == 0 and items is not STEP_1 and items is not LAST_1:
                            pe.wait_ge(o_ready, s - 1)
                        pe.wait_ge(t_ready, s * PIECES + (c + 1 - PIECES))
                        for j in range(2):
                            vs = slice(P * (2 * c + j), P * (2 * c + j + 1))
                            for m, (v, pt) in enumerate(((v_hi, pt_hi), (v_hi, pt_lo), (v_lo, pt_hi))):
                                last = pe.matmul(o_ps[:, 0:GQ], v[:, vs], pt[:, c % 3, GQ * j:GQ * (j + 1)],
                                                 start=c == 0 and j == 0 and m == 0,
                                                 stop=c == PIECES - 1 and j == 1 and m == 2)
                        last.then_inc(o_done if c == PIECES - 1 else weighed, 1)

            run_heads(pe, run)

        @block.scalar
        def _(act):
            def run(items, h, g, s, par, chunk, chunk_par):
                n = 0
                for item in items:
                    kind = item[0]
                    buf = (chunk_par + n) % 2
                    if kind == "T":
                        c = item[1]
                        act.wait_ge(turned, s * PIECES + (c + 1 - PIECES))
                        if c >= 3:
                            act.wait_ge(weighed, s * (PIECES - 1) + (c - 2 - (PIECES - 1)))
                        act.copy(pt_hi[:, c % 3, :], t_ps[:, c % 3, :]).then_inc(t_rounded, 1)
                    elif kind == "E":
                        t, i = item[1:]
                        if i == 0:
                            act.wait_ge(maxed, s * 2 + (t + 1))
                        cols = slice(CHUNK * i, CHUNK * (i + 1))
                        ins = act.activation(probs[:, par, t, cols], probs[:, par, t, cols], ACT.Exp,
                                             bias=neg_max[:, par, t:t + 1], accum_out=chunk_sum[:, par, t, i:i + 1])
                        if i == 3:
                            ins.then_inc(exped, 1)
                    elif kind == "O":
                        act.wait_ge(o_done, s - 1)
                        act.copy(o_hi[:], o_ps[:, 0:GQ]).then_inc(o_rounded, 1)
                    elif kind == "Q+":
                        act.wait_ge(filled, chunk + (n + 1))
                        act.copy(q_hi[:, 1 - par, :], s_ps[:, buf, 0:GQ]).then_inc(q_rounded, 1)
                    elif kind in ("K+", "V+", "V"):
                        if item == ("K+", 0):
                            act.wait_ge(shifted, h + 2)
                        act.wait_ge(kv_half, kv_count(item, h))
                        for half in range(2):
                            if half:
                                act.wait_ge(filled, chunk + (n + 1))
                            bank = s_ps[:, buf, BLK * half:BLK * (half + 1)]
                            if kind == "K+":
                                cols = slice(CHUNK * item[1] + BLK * half, CHUNK * item[1] + BLK * (half + 1))
                                act.activation(k_hi[:, cols], bank, ACT.Identity, bias=shift[:, 0:1]).then_inc(kv_rounded, 1)
                            else:
                                keys, products = v_half(item[1], half, bank)
                                act.copy(v_hi[:, keys].rearrange("p (t d) -> p t d", d=XD), products[:, :, 0, :]).then_inc(kv_rounded, 1)
                    elif kind == "wkv":
                        act.wait_ge(kv_loaded, (h + 2) * 96)
                        act.copy(kv_split[:, :, 0, :], kv_raw[:].rearrange("p (n d) -> p n d", d=XD)).then_inc(kv_w_hi, 1)
                    elif kind == "wq":
                        act.wait_ge(wq_loaded, (h + 2) * 32)
                        act.copy(wq_hi[:], wq_raw[:]).then_inc(wq_w_hi, 1)
                    elif kind == "wo":
                        act.wait_ge(wo_loaded, (h + 1) * 16)
                        act.copy(wo_hi[:], wo_raw[:]).then_inc(wo_w_hi, 1)
                    n += kind in IS_CHUNK

            run_heads(act, run)

        @block.vector
        def _(dve):
            def run(items, h, g, s, par, chunk, chunk_par):
                n = 0
                for item in items:
                    kind = item[0]
                    buf = (chunk_par + n) % 2
                    if kind in ("A", "A+"):
                        t, i = item[1:]
                        dve.wait_ge(filled, chunk + (n + 1))
                        dve.tensor_scalar(probs[:, par if kind == "A" else 1 - par, t, CHUNK * i:CHUNK * (i + 1)],
                                          s_ps[:, buf, :], LOGIT, None, ALU.mult, ALU.max,
                                          accum_out=chunk_max[:, t, i:i + 1]).then_inc(freed, 1)
                    elif kind == "M":
                        t = item[1]
                        dve.wait_ge(freed, chunk + n)
                        dve.tensor_reduce(neg_max[:, par, t:t + 1], chunk_max[:, t, :], AX.X, ALU.max,
                                          negate=True).then_inc(maxed, 1)
                    elif kind == "T":
                        c = item[1]
                        dve.wait_ge(t_rounded, s * PIECES + (c + 1 - PIECES))
                        dve.tensor_tensor(pt_lo[:, c % 3, :], t_ps[:, c % 3, :], pt_hi[:, c % 3, :].bitcast(F32),
                                          ALU.subtract).then_inc(t_ready, 1)
                    elif kind == "I":
                        dve.wait_ge(exped, s * 2)
                        dve.tensor_reduce(denom[:], chunk_sum[:, 1 - par, :, :], AX.X, ALU.add).then_inc(summed, 1)
                        dve.wait_ge(summed, s)
                        dve.reciprocal(inv[:, 1 - par, :], denom[:]).then_inc(inv_ready, 1)
                    elif kind == "O":
                        dve.wait_ge(o_rounded, s - 1)
                        dve.tensor_tensor(o_lo[:], o_ps[:, 0:GQ], o_hi[:].bitcast(F32), ALU.subtract).then_inc(o_ready, 1)
                    elif kind == "out":
                        dve.wait_ge(filled, chunk + (n + 1))
                        dve.wait_ge(inv_ready, s - 1)
                        first = g * 2 - 4
                        for t in range(2):
                            tile = x[:, bass.ds(first + t, 1), :].rearrange("p o c -> p (o c)")
                            last = dve.scalar_tensor_tensor(out=tile, in0=s_ps[:, buf, C * t:C * (t + 1)],
                                                            scalar=inv[:, par, t:t + 1], in1=tile, op0=ALU.mult, op1=ALU.add)
                        last.then_inc(freed, 1)
                    elif kind == "Q+":
                        dve.wait_ge(q_rounded, s + 2)
                        for t, done in enumerate((q_ready, freed)):
                            half = slice(P * t, P * (t + 1))
                            dve.tensor_tensor(q_lo[:, 1 - par, half], s_ps[:, buf, half], q_hi[:, 1 - par, half].bitcast(F32),
                                              ALU.subtract).then_inc(done, 1)
                    elif kind in ("K+", "V+", "V"):
                        if item == ("K+", 0):
                            dve.wait_ge(shifted, h + 2)
                        for half in range(2):
                            bank = s_ps[:, buf, BLK * half:BLK * (half + 1)]
                            dve.wait_ge(kv_rounded, kv_count(item, h) * 2 + (half - 1))
                            if kind == "K+":
                                cols = slice(CHUNK * item[1] + BLK * half, CHUNK * item[1] + BLK * (half + 1))
                                last = dve.scalar_tensor_tensor(out=k_lo[:, cols], in0=bank, scalar=shift[:, 0:1],
                                                                in1=k_hi[:, cols].bitcast(F32), op0=ALU.add, op1=ALU.subtract)
                            else:
                                keys, products = v_half(item[1], half, bank)
                                rest = v_rest[:, half, :].rearrange("p (t d) -> p t d", d=XD)
                                dve.tensor_tensor(rest, products[:, :, 0, :], v_hi[:, keys].rearrange("p (t d) -> p t d", d=XD).bitcast(F32),
                                                  ALU.subtract).then_inc(v_rest_ready, 1)
                                blocks_before = KV_ORDER.index(item) - 4
                                dve.wait_ge(v_rest_ready, (h if kind == "V" else h + 1) * 16 + (2 * blocks_before + half + 1))
                                last = dve.tensor_tensor(v_lo[:, keys].rearrange("p (t d) -> p t d", d=XD), products[:, :, 1, :],
                                                         rest, ALU.add)
                        last.then_inc(freed, 1)
                    elif kind == "wkv":
                        dve.wait_ge(kv_w_hi, h + 2)
                        dve.tensor_tensor(kv_split[:, :, 1, :], kv_raw[:].rearrange("p (n d) -> p n d", d=XD),
                                          kv_split[:, :, 0, :].bitcast(F32), ALU.subtract).then_inc(kv_w, 1)
                        if items is BEFORE:
                            dve.tensor_copy(shift[:], k_shift[:, 0:1]).then_inc(shifted, 1)
                    elif kind == "wq":
                        dve.wait_ge(wq_w_hi, h + 2)
                        dve.tensor_tensor(wq_lo[:], wq_raw[:], wq_hi[:].bitcast(F32), ALU.subtract).then_inc(wq_w, 1)
                        if items is not BEFORE:
                            dve.tensor_copy(shift[:], k_shift[:, bass.ds(h + 1, 1)]).then_inc(shifted, 1)
                    elif kind == "wo":
                        dve.wait_ge(wo_w_hi, h + 1)
                        dve.tensor_tensor(wo_lo[:], wo_raw[:], wo_hi[:].bitcast(F32), ALU.subtract).then_inc(wo_w, 1)
                    n += kind in IS_CHUNK

            run_heads(dve, run)
            dve.wait_ge(freed, ALL_CHUNKS)


def channel_mix(nc, a, x, ident, out):
    with ExitStack() as ctx:
        def sb(name, shape, dt=F32):
            return ctx.enter_context(nc.sbuf_tensor(name, shape, dt))

        def sem(name):
            return ctx.enter_context(nc.semaphore(name))

        y = sb("y3", [P, NT, C])
        parts, mv = sb("parts3", [P, NT, 6]), sb("mv3", [P, NT, 2])
        var_eps, root = sb("var_eps3", [P, NT]), sb("root3", [P, NT])
        rstd, tmp = sb("rstd3", [P, NT]), sb("tmp3", [P, NT])
        w_raw = sb("fw_raw", [P, 3, CH, C])
        w_hi, w_lo = sb("fw_hi", [P, 3, CH, C], F32R), sb("fw_lo", [P, 3, CH, C], F32R)
        mu, nu = sb("mu", [P, 2, CH]), sb("nu", [P, 2, CH])
        yt = sb("yt", [P, CH, B, N + 1])
        part = sb("mix_part", [P, 2, 2, N])
        full = sb("mix_full", [P, 4, N])
        mix_hi, mix_lo = sb("mix_hi", [P, 2, CH, T], F32R), sb("mix_lo", [P, 2, CH, T], F32R)
        relu, square = sb("relu", [P, 2, N]), sb("square", [P, 2, N])
        act_hi, act_lo = sb("act_hi", [P, CH, T], F32R), sb("act_lo", [P, CH, T], F32R)
        gate, gated = sb("gate", [P, 2, C]), sb("gated", [P, 2, C])
        banks = ctx.enter_context(nc.psum_tensor("banks3", [P, 8, 512], F32))

        loaded, stored = sem("loaded3"), sem("stored3")
        var_ready, root_ready, y_ready = sem("var_ready3"), sem("root_ready3"), sem("y_ready3")
        dve_self, padded, nu_ready = sem("dve_self3"), sem("padded"), sem("nu_ready")
        w_hi_ready, w_ready = sem("fw_hi_ready"), sem("fw_ready")
        turned, yt_ready = sem("turned3"), sem("yt_ready")
        scaled = [sem("scaled_r"), sem("scaled_k")]
        mixed, mix_rounded = sem("mixed"), sem("mix_rounded")
        mix_ready = [sem("mix_r_ready"), sem("mix_k_ready")]
        k_done, relu_done, squared, act_rounded, act_ready = (sem("k_done"), sem("relu_done"), sem("squared"),
                                                              sem("act_rounded"), sem("act_ready"))
        rv_done, gate_ready, gated_ready, added = sem("rv_done"), sem("gate_ready"), sem("gated_ready"), sem("added3")
        block = ctx.enter_context(nc.Block())
        PIECES = [(b, h) for b in range(B) for h in range(CH)]

        @block.sync
        def _(sp):
            for n, name in enumerate(("W_rT", "W_kT", "W_vT")):
                sp.dma_start(w_raw[:, n, :, :], a[name].rearrange("(h p) o -> p h o", p=P)).then_inc(loaded, 16)
            with nc.allow_non_contiguous_dma(reason="a few per-channel vectors"):
                for n, name in enumerate(("mu_r", "mu_k")):
                    sp.dma_start(mu[:, n, :], a[name].rearrange("(h p) -> p h", p=P)).then_inc(loaded, 16)
            stores = out.rearrange("(t p) c -> p t c", p=P)
            for t in range(0, NT, 2):
                sp.wait_ge(added, t + 2)
                sp.dma_start(stores[:, t:t + 2, :], x[:, t:t + 2, :]).then_inc(stored, 16)
            sp.wait_ge(stored, 16 * NT // 2)

        @block.gpsimd
        def _(pool):
            pool.memset(yt[:, :, :, 0:1], 0.0).then_inc(padded, 1)
            pool.wait_ge(loaded, 80)
            for n in range(len(PIECES) + 1):
                if n < len(PIECES):
                    b, h = PIECES[n]
                    pool.wait_ge(yt_ready, n + 1)
                    if n >= 2:
                        pool.wait_ge(mixed, 2 * (n - 1))
                        pool.wait_ge(mix_ready[0], n - 1)
                    pool.tensor_scalar(part[:, n % 2, 0, :], yt[:, h, b, 1:N + 1], mu[:, 0, h:h + 1], None,
                                       ALU.mult).then_inc(scaled[0], 1)
                if n >= 1:
                    b, h = PIECES[n - 1]
                    cols = slice(N * b, N * (b + 1))
                    if n < len(PIECES):
                        pool.wait_ge(scaled[0], n + 1)
                    pool.wait_ge(mix_rounded, 2 * n)
                    pool.tensor_tensor(mix_lo[:, 0, h, cols], full[:, (2 * n - 2) % 4, :], mix_hi[:, 0, h, cols].bitcast(F32),
                                       ALU.subtract).then_inc(mix_ready[0], 1)

        @block.vector
        def _(dve):
            chain = Chain(dve, dve_self)
            row_moments(dve, chain, x, parts, mv)
            inverse_root_seed(dve, chain, mv, var_eps, var_ready)
            dve.wait_ge(loaded, 80)
            dve.tensor_scalar(nu[:], mu[:], -1.0, 1.0, ALU.mult, ALU.add).then_inc(nu_ready, 1)
            for n in range(3):
                dve.wait_ge(w_hi_ready, n + 1)
                dve.tensor_tensor(flat(w_lo[:, n]), flat(w_raw[:, n]), flat(w_hi[:, n]).bitcast(F32),
                                  ALU.subtract).then_inc(w_ready, 1)
            dve.wait_ge(root_ready, 1)
            inverse_root(dve, chain, var_eps[:], root[:], rstd[:], tmp)
            for t in range(NT):
                dve.tensor_scalar(y[:, t, :], x[:, t, :], mv[:, t, 0:1], rstd[:, t:t + 1],
                                  ALU.subtract, ALU.mult).then_inc(y_ready, 1)
            dve.wait_ge(nu_ready, 1)
            dve.wait_ge(padded, 1)

            for n in range(len(PIECES) + 1):
                if n < len(PIECES):
                    b, h = PIECES[n]
                    dve.wait_ge(yt_ready, n + 1)
                    if n >= 2:
                        dve.wait_ge(mix_ready[0], n - 1)
                        dve.wait_ge(mix_ready[1], n - 1)
                    for m in (1, 0):
                        dve.wait_ge(scaled[m], n + 1)
                        dve.scalar_tensor_tensor(out=full[:, (2 * n + m) % 4, :], in0=yt[:, h, b, 0:N], scalar=nu[:, m, h:h + 1],
                                                 in1=part[:, n % 2, m, :], op0=ALU.mult, op1=ALU.add).then_inc(mixed, 1)
                if n >= 1:
                    b, h = PIECES[n - 1]
                    cols = slice(N * b, N * (b + 1))
                    dve.wait_ge(mix_rounded, 2 * n - 1)
                    dve.tensor_tensor(mix_lo[:, 1, h, cols], full[:, (2 * n - 1) % 4, :], mix_hi[:, 1, h, cols].bitcast(F32),
                                      ALU.subtract).then_inc(mix_ready[1], 1)
            for n in range(len(PIECES)):
                b, h = PIECES[n]
                cols = slice(N * b, N * (b + 1))
                dve.wait_ge(relu_done, n + 1)
                dve.tensor_tensor(square[:, n % 2, :], relu[:, n % 2, :], relu[:, n % 2, :], ALU.mult).then_inc(squared, 1)
                dve.wait_ge(act_rounded, n + 1)
                dve.tensor_tensor(act_lo[:, h, cols], square[:, n % 2, :], act_hi[:, h, cols].bitcast(F32),
                                  ALU.subtract).then_inc(act_ready, 1)
            for t in range(NT):
                dve.wait_ge(gate_ready, t + 1)
                if t >= 2:
                    dve.wait_ge(added, t - 1)
                dve.tensor_tensor(gated[:, t % 2, :], gate[:, t % 2, :], banks[:, t % 4, C:2 * C],
                                  ALU.mult).then_inc(gated_ready, 1)
                dve.wait_ge(gated_ready, t + 1)
                dve.tensor_tensor(x[:, t, :], x[:, t, :], gated[:, t % 2, :], ALU.add).then_inc(added, 1)

        @block.scalar
        def _(act):
            act.wait_ge(var_ready, 1)
            act.activation(root[:], var_eps[:], ACT.Sqrt).then_inc(root_ready, 1)
            act.wait_ge(loaded, 80)
            for n in range(3):
                act.copy(flat(w_hi[:, n]), flat(w_raw[:, n])).then_inc(w_hi_ready, 1)
            for n in range(len(PIECES) + 1):
                if n < len(PIECES):
                    b, h = PIECES[n]
                    act.wait_ge(turned, n + 1)
                    act.copy(yt[:, h, b, 1:N + 1], banks[:, n % 4, :]).then_inc(yt_ready, 1)
                    if n >= 2:
                        act.wait_ge(mixed, 2 * (n - 2) + 1)
                    act.activation(part[:, n % 2, 1, :], banks[:, n % 4, :], ACT.Identity,
                                   scale=mu[:, 1, h:h + 1]).then_inc(scaled[1], 1)
                if n >= 1:
                    b, h = PIECES[n - 1]
                    for k, m in enumerate((1, 0)):
                        act.wait_ge(mixed, 2 * n - 1 + k)
                        act.copy(mix_hi[:, m, h, N * b:N * (b + 1)], full[:, (2 * n - 2 + m) % 4, :]).then_inc(mix_rounded, 1)
            for n in range(len(PIECES)):
                b, h = PIECES[n]
                act.wait_ge(k_done, n + 1)
                if n >= 2:
                    act.wait_ge(squared, n - 1)
                act.activation(relu[:, n % 2, :], banks[:, 4 + n % 4, :], ACT.Relu).then_inc(relu_done, 1)
                act.wait_ge(squared, n + 1)
                act.copy(act_hi[:, h, N * b:N * (b + 1)], square[:, n % 2, :]).then_inc(act_rounded, 1)
            for t in range(NT):
                act.wait_ge(rv_done, t + 1)
                if t >= 2:
                    act.wait_ge(gated_ready, t - 1)
                act.activation(gate[:, t % 2, :], banks[:, t % 4, 0:C], ACT.Sigmoid).then_inc(gate_ready, 1)

        @block.tensor
        def _(pe):
            for n, (b, h) in enumerate(PIECES):
                pe.wait_ge(y_ready, QI * (b + 1))
                if n >= 4:
                    pe.wait_ge(scaled[1], n - 3)
                for t in range(QI):
                    last = pe.transpose(banks[:, n % 4, P * t:P * (t + 1)], y[:, QI * b + t, P * h:P * (h + 1)], ident[:])
                last.then_inc(turned, 1)
            pe.wait_ge(w_ready, 3)
            for n, (b, oh) in enumerate(PIECES):
                pe.wait_ge(mix_ready[1], CH * (b + 1))
                if n >= 4:
                    pe.wait_ge(relu_done, n - 3)
                passes = [(ws, zs, h) for h in range(CH) for ws, zs in ((w_hi, mix_hi), (w_hi, mix_lo), (w_lo, mix_hi))]
                for i, (ws, zs, h) in enumerate(passes):
                    last = pe.matmul(banks[:, 4 + n % 4, :], ws[:, 1, h, P * oh:P * (oh + 1)],
                                     zs[:, 1, h, N * b:N * (b + 1)], start=i == 0, stop=i == len(passes) - 1)
                last.then_inc(k_done, 1)
            pe.wait_ge(mix_ready[0], len(PIECES))
            for t in range(NT):
                pe.wait_ge(act_ready, CH * (t // QI + 1))
                if t >= 4:
                    pe.wait_ge(added, t - 3)
                rows = slice(P * t, P * (t + 1))
                for c0, w, hi, lo in ((0, 0, mix_hi[:, 0], mix_lo[:, 0]), (C, 2, act_hi, act_lo)):
                    passes = [(zs, ws, h) for h in range(CH) for zs, ws in ((hi, w_hi), (hi, w_lo), (lo, w_hi))]
                    for i, (zs, ws, h) in enumerate(passes):
                        last = pe.matmul(banks[:, t % 4, c0:c0 + C], zs[:, h, rows], ws[:, w, h, :],
                                         start=i == 0, stop=i == len(passes) - 1)
                last.then_inc(rv_done, 1)


def interpolation():
    pos = np.arange(N, dtype=np.float32) * np.float32((BIAS_S - 1) / (N - 1))
    i0 = np.floor(pos).astype(np.int32)
    i1 = np.minimum(i0 + 1, BIAS_S - 1)
    frac = pos - i0.astype(np.float32)
    m = np.zeros((N, BIAS_S), np.float32)
    np.add.at(m, (np.arange(N), i0), np.float32(1.0) - frac)
    np.add.at(m, (np.arange(N), i1), frac)
    m[-1] = 0.0
    return np.ascontiguousarray(m.T)


def kernel(**inputs):
    import concourse.bacc as bacc
    from concourse.bass_utils import run_bass_kernel_spmd

    def arr(name):
        return np.asarray(inputs[name])

    arrays = {
        "x": arr("x").reshape(T, C),
        "ctxT": arr("ctx_768").reshape(KEYS, CD).T,
        "WqT": arr("L0_attn_Wq").T, "WkT": arr("L0_attn_Wk").T, "WvT": arr("L0_attn_Wv").T, "WoT": arr("L0_attn_Wo").T,
        "bq": arr("L0_attn_bq"), "bk": arr("L0_attn_bk"), "bv": arr("L0_attn_bv"), "bo": arr("L0_attn_bo"),
        "gamma": arr("L0_attn_gamma"), "beta": arr("L0_attn_beta"), "rel_bias": arr("L0_attn_rel_bias"),
        "XWq": arr("L0_xattn_Wq"), "XWk": arr("L0_xattn_Wk"), "XWv": arr("L0_xattn_Wv"),
        "XWout": arr("L0_xattn_Wout"), "Xbout": arr("L0_xattn_bout"),
        "W_rT": arr("L0_ffn_W_r").T, "W_kT": arr("L0_ffn_W_k").T, "W_vT": arr("L0_ffn_W_v").T,
        "mu_r": arr("L0_ffn_mu_r"), "mu_k": arr("L0_ffn_mu_k"),
        "identity": np.eye(P, dtype=np.float32),
        "causal": np.triu(np.full((P, P), MASKED, np.float32), 1),
        "interp": interpolation(), "interp3": np.tile(interpolation(), (3, 1)),
    }
    nc = bacc.Bacc("TRN2", target_bir_lowering=False, num_devices=1)
    feed, aps = {}, {}
    for name, value in arrays.items():
        value = np.ascontiguousarray(value)
        feed[f"in_{name}"] = value
        aps[name] = nc.dram_tensor(f"in_{name}", value.shape, mybir.dt.from_np(value.dtype), kind="ExternalInput").ap()
    out = nc.dram_tensor("out_x", (T, C), F32, kind="ExternalOutput").ap()
    decoder_layer(nc, aps, out)
    result = run_bass_kernel_spmd(nc, [feed], core_ids=[0])
    return result.results[0]["out_x"].reshape(B, N, C)
```
